# Optimizing a Trainium2 kernel written in Bass

```python
import numpy as np
import jax
import jax.numpy as jnp

def _softmax(x, axis=-1):
    return jax.nn.softmax(x, axis=axis)

def _gelu(x):
    return jax.nn.gelu(x, approximate=True)

def _silu(x):
    return jax.nn.silu(x)

def _sigmoid(x):
    return jax.nn.sigmoid(x)

def _layernorm(x, axis=-1, eps=1e-05):
    m = jnp.mean(x, axis=axis, keepdims=True)
    v = jnp.var(x, axis=axis, keepdims=True)
    return (x - m) / jnp.sqrt(v + eps)

def _scatter_add(tgt, idx, src, axis=0):
    return tgt.at[idx].add(src)

def _segment_sum(src, seg, n):
    return jax.ops.segment_sum(src, seg, n)
kernel_name = 'mk_perceiver_d2_seqx_r4_d91a01'

def setup_inputs(seed: int=0):
    np.random.seed(seed)
    _w = jnp.asarray

    def _rec_inputs():
        import jax
        import jax.numpy as jnp
        _rk = jax.random.key(seed)
        x = -0.000125 + 0.9999 * jax.random.normal(jax.random.fold_in(_rk, 1), (2, 64, 256), jnp.float32)
        _lenS = 64 - jax.random.randint(jax.random.fold_in(_rk, 7), (2,), 0, max(1, 64 // 4) + 1, jnp.int32)
        _lenS2 = 1024 - jax.random.randint(jax.random.fold_in(_rk, 8), (2,), 0, max(1, 1024 // 4) + 1, jnp.int32)
        _ctx_2048P = jax.random.normal(jax.random.fold_in(_rk, 11), (2, 16, 512), jnp.float32)
        _ctx_2048c = jax.random.dirichlet(jax.random.fold_in(_rk, 511), 0.3 * jnp.ones((16,), jnp.float32), (2, 1024))
        _ctx_2048t = jnp.einsum('bsk,bkd->bsd', _ctx_2048c, _ctx_2048P)
        _ctx_2048t = _ctx_2048t * jax.lax.rsqrt(jnp.mean(jnp.square(_ctx_2048t)) + 1e-12) * 0.953939
        ctx_2048 = -1.39393e-06 + 0.999914 * (_ctx_2048t + 0.3 * jax.random.normal(jax.random.fold_in(_rk, 611), (2, 1024, 512), jnp.float32))
        return (x, ctx_2048)
    x, ctx_2048 = _rec_inputs()

    def _L0_xattn_setup():
        import jax, jax.numpy as jnp
        import numpy as np
        B, N, DIM = (8, 1024, 256)
        M, CTX = (64, 512)
        HEADS, DH = (16, 64)
        INNER = HEADS * DH
        EPS = 1e-06

        def _split_heads(t):
            b, n, _ = t.shape
            return t.reshape(b, n, HEADS, DH).transpose(0, 2, 1, 3)
        key = jax.random.key(seed)
        ks = jax.random.split(key, 6)
        x = jax.random.normal(ks[0], (B, N, DIM), dtype=jnp.float32)
        context = jax.random.normal(ks[1], (B, M, CTX), dtype=jnp.float32)
        Wq = jax.random.normal(ks[2], (DIM, INNER), dtype=jnp.float32) / np.sqrt(DIM)
        Wkv = jax.random.normal(ks[3], (CTX, 2 * INNER), dtype=jnp.float32) / np.sqrt(CTX)
        null_kv = jax.random.normal(ks[4], (2, DH), dtype=jnp.float32) / np.sqrt(2.0)
        Wout = jax.random.normal(ks[5], (INNER, DIM), dtype=jnp.float32) / np.sqrt(INNER)
        ln_scale = jnp.ones((DIM,), dtype=jnp.float32)
        ln_bias = jnp.zeros((DIM,), dtype=jnp.float32)
        return {'x': x, 'context': context, 'Wq': Wq, 'Wkv': Wkv, 'null_kv': null_kv, 'Wout': Wout, 'ln_scale': ln_scale, 'ln_bias': ln_bias}
    _L0_xattn_all = _L0_xattn_setup()
    _L0_xattn_in = {k: v for k, v in _L0_xattn_all.items() if k in ('Wq', 'Wkv', 'null_kv', 'Wout', 'ln_scale', 'ln_bias')}
    del _L0_xattn_all

    def _L0_attn_setup():
        import jax, jax.numpy as jnp
        import numpy as np
        DIM = 256
        DIM_HEAD = 64
        HEADS = DIM // DIM_HEAD
        SCALE = DIM_HEAD ** (-0.5)
        RMS_EPS = 1e-08
        LN_EPS = 1e-05

        def _layernorm(x, g, b):
            mu = jnp.mean(x, axis=-1, keepdims=True)
            var = jnp.mean(jnp.square(x - mu), axis=-1, keepdims=True)
            return (x - mu) * jax.lax.rsqrt(var + LN_EPS) * g + b

        def _rmsnorm(x, gamma):
            norm = jnp.sqrt(jnp.sum(jnp.square(x), axis=-1, keepdims=True)) * DIM_HEAD ** (-0.5)
            return x / jnp.maximum(norm, RMS_EPS) * gamma
        key = jax.random.key(seed)
        ks = jax.random.split(key, 8)
        b, n = (2, 512)
        x = jax.random.normal(ks[0], (b, n, DIM), dtype=jnp.float32)
        init = 1.0 / np.sqrt(DIM)
        Wq = jax.random.uniform(ks[1], (DIM, DIM), jnp.float32, -init, init)
        Wk = jax.random.uniform(ks[2], (DIM, DIM), jnp.float32, -init, init)
        Wv = jax.random.uniform(ks[3], (DIM, DIM), jnp.float32, -init, init)
        Wo = jax.random.uniform(ks[4], (DIM, DIM), jnp.float32, -init, init)
        bo = jax.random.uniform(ks[5], (DIM,), jnp.float32, -init, init)
        ln_g = jnp.ones((DIM,), jnp.float32)
        ln_b = jnp.zeros((DIM,), jnp.float32)
        q_gamma = jnp.ones((DIM_HEAD,), jnp.float32)
        k_gamma = jnp.ones((DIM_HEAD,), jnp.float32)
        return dict(x=x, Wq=Wq, Wk=Wk, Wv=Wv, Wo=Wo, bo=bo, ln_g=ln_g, ln_b=ln_b, q_gamma=q_gamma, k_gamma=k_gamma)
    _L0_attn_all = _L0_attn_setup()
    _L0_attn_in = {k: v for k, v in _L0_attn_all.items() if k in ('Wq', 'Wk', 'Wv', 'Wo', 'bo', 'ln_g', 'ln_b', 'q_gamma', 'k_gamma')}
    del _L0_attn_all

    def _L0_ffn_setup():
        import jax, jax.numpy as jnp
        import numpy as np
        B, S, H, F, E = (8, 512, 256, 1024, 8)
        INIT_LAMBDA = 0.2
        key = jax.random.key(seed)
        ks = jax.random.split(key, 12)
        std = 0.02
        return {'hidden_states': jax.random.normal(ks[0], (B, S, H), jnp.float32), 'gate_w1': jax.random.normal(ks[1], (H, H), jnp.float32) * 0.01, 'gate_b1': jnp.zeros((H,), jnp.float32), 'gate_w2': jax.random.normal(ks[2], (E, H), jnp.float32) * 0.01, 'gate_b2': jnp.full((E,), INIT_LAMBDA, jnp.float32), 'W1': jax.random.normal(ks[3], (F, H), jnp.float32) * std, 'b1': jax.random.normal(ks[4], (F,), jnp.float32) * std, 'W2': jax.random.normal(ks[5], (H, F), jnp.float32) * std, 'b2': jax.random.normal(ks[6], (H,), jnp.float32) * std, 'TW1': jax.random.normal(ks[7], (E, F, H), jnp.float32) * std, 'Tb1': jax.random.normal(ks[8], (E, F), jnp.float32) * std, 'TW2': jax.random.normal(ks[9], (E, H, F), jnp.float32) * std, 'Tb2': jax.random.normal(ks[10], (E, H), jnp.float32) * std}
    _L0_ffn_all = _L0_ffn_setup()
    _L0_ffn_in = {k: v for k, v in _L0_ffn_all.items() if k in ('gate_w1', 'gate_b1', 'gate_w2', 'gate_b2', 'W1', 'b1', 'W2', 'b2', 'TW1', 'Tb1', 'TW2', 'Tb2')}
    del _L0_ffn_all

    def _L1_xattn_setup():
        import jax, jax.numpy as jnp
        import numpy as np
        NUM_HEADS = 16
        key = jax.random.key(seed)
        ks = jax.random.split(key, 5)
        dim = 256
        B, N, N_c = (4, 256, 64)
        x = jax.random.normal(ks[0], (B, N, dim), dtype=jnp.float32)
        context = jax.random.normal(ks[1], (B, N_c, 2 * dim), dtype=jnp.float32)
        w_qkv = jax.random.normal(ks[2], (3 * dim, dim), dtype=jnp.float32) * 0.02
        w_proj = jax.random.normal(ks[3], (dim, dim), dtype=jnp.float32) * 0.02
        b_proj = jax.random.normal(ks[4], (dim,), dtype=jnp.float32) * 0.02
        return {'x': x, 'context': context, 'w_qkv': w_qkv, 'w_proj': w_proj, 'b_proj': b_proj}
    _L1_xattn_all = _L1_xattn_setup()
    _L1_xattn_in = {k: v for k, v in _L1_xattn_all.items() if k in ('w_qkv', 'w_proj', 'b_proj')}
    del _L1_xattn_all

    def _L1_attn_setup():
        import jax, jax.numpy as jnp
        import numpy as np
        D_MODEL = 256
        D_STATE = 128
        D_CONV = 4
        EXPAND = 2
        HEADDIM = 64
        D_INNER = D_MODEL * EXPAND
        NHEADS = D_INNER // HEADDIM
        CONV_DIM = D_INNER + 2 * D_STATE
        D_IN_PROJ = 2 * D_INNER + 2 * D_STATE + NHEADS
        POOL = 50
        SDIM = 64
        HEAD_DIM_RET = SDIM // 4
        TAU1 = 0.5
        TAU2 = 0.3
        HID = D_MODEL // 4
        B = 4
        T = 512
        EPS = 1e-05

        def _rmsnorm(x, w):
            return x * jax.lax.rsqrt(jnp.mean(x * x, axis=-1, keepdims=True) + EPS) * w

        def _mamba2(x, in_w, conv_w, conv_b, dt_bias, A_log, D_param, gnorm_w, out_w):
            Bn, Tn, _ = x.shape
            zxbcdt = x @ in_w.T
            z = zxbcdt[..., :D_INNER]
            xBC = zxbcdt[..., D_INNER:D_INNER + CONV_DIM]
            dt = zxbcdt[..., D_INNER + CONV_DIM:]
            xp = jnp.pad(jnp.transpose(xBC, (0, 2, 1)), ((0, 0), (0, 0), (D_CONV - 1, 0)))
            conv = jax.lax.conv_general_dilated(xp, conv_w[:, None, :], (1,), 'VALID', dimension_numbers=('NCH', 'OIH', 'NCH'), feature_group_count=CONV_DIM)
            xBC = jax.nn.silu(jnp.transpose(conv, (0, 2, 1)) + conv_b)
            xs = xBC[..., :D_INNER].reshape(Bn, Tn, NHEADS, HEADDIM)
            Bm = xBC[..., D_INNER:D_INNER + D_STATE]
            Cm = xBC[..., D_INNER + D_STATE:]
            dt = jax.nn.softplus(dt + dt_bias)
            A = -jnp.exp(A_log)
            dA = jnp.exp(dt * A)
            dtx = dt[..., None] * xs

            def step(h, inp):
                dA_t, dtx_t, B_t, C_t = inp
                h = h * dA_t[:, :, None, None] + dtx_t[..., None] * B_t[:, None, None, :]
                y = jnp.einsum('bhpn,bn->bhp', h, C_t)
                return (h, y)
            tm = lambda a: jnp.moveaxis(a, 1, 0)
            h0 = jnp.zeros((Bn, NHEADS, HEADDIM, D_STATE), x.dtype)
            _, ys = jax.lax.scan(step, h0, (tm(dA), tm(dtx), tm(Bm), tm(Cm)))
            y = jnp.moveaxis(ys, 0, 1) + D_param[None, None, :, None] * xs
            y = y.reshape(Bn, Tn, D_INNER)
            y = _rmsnorm(y * jax.nn.silu(z), gnorm_w)
            return y @ out_w.T

        def _update_memory(tokens, imp, summ_w, pool, prio, counts):
            Bn, Tn, Dm = tokens.shape
            S = min(Tn, POOL)
            order = jnp.argsort(-imp, axis=1)[:, :S]
            s_imp = jnp.take_along_axis(imp, order, axis=1)
            s_tok = jnp.take_along_axis(tokens, order[..., None], axis=1)
            s_sum = s_tok @ summ_w.T
            s_mask = s_imp > TAU1
            ar = jnp.arange(Bn)

            def body(carry, inp):
                pool, prio, counts = carry
                hi, si, ss = inp
                add = hi & (counts < POOL)
                idx = jnp.minimum(counts, POOL - 1)
                pool = pool.at[ar, idx].set(jnp.where(add[:, None], ss, pool[ar, idx]))
                prio = prio.at[ar, idx].set(jnp.where(add, si, prio[ar, idx]))
                counts = counts + add.astype(counts.dtype)
                repl = hi & (counts >= POOL)
                mi = jnp.argmin(prio, axis=1)
                should = repl & (si > prio[ar, mi])
                pool = pool.at[ar, mi].set(jnp.where(should[:, None], ss, pool[ar, mi]))
                prio = prio.at[ar, mi].set(jnp.where(should, si, prio[ar, mi]))
                return ((pool, prio, counts), None)
            xs = (jnp.moveaxis(s_mask, 1, 0), jnp.moveaxis(s_imp, 1, 0), jnp.moveaxis(s_sum, 1, 0))
            (pool, prio, counts), _ = jax.lax.scan(body, (pool, prio, counts), xs)
            return (pool, prio, counts)
        key = jax.random.key(seed)
        ks = jax.random.split(key, 16)

        def w(k, shape, fan_in):
            return jax.random.normal(k, shape, dtype=jnp.float32) / np.float32(np.sqrt(fan_in))
        inp = {}
        inp['x'] = jax.random.normal(ks[0], (B, T, D_MODEL), dtype=jnp.float32)
        inp['norm_w'] = jnp.ones((D_MODEL,), jnp.float32)
        inp['in_w'] = w(ks[1], (D_IN_PROJ, D_MODEL), D_MODEL)
        inp['conv_w'] = w(ks[2], (CONV_DIM, D_CONV), D_CONV)
        inp['conv_b'] = jnp.zeros((CONV_DIM,), jnp.float32)
        inp['dt_bias'] = jnp.log(jnp.expm1(jax.random.uniform(ks[3], (NHEADS,), minval=0.001, maxval=0.1))).astype(jnp.float32)
        inp['A_log'] = jnp.log(jax.random.uniform(ks[4], (NHEADS,), minval=1.0, maxval=16.0)).astype(jnp.float32)
        inp['D_param'] = jnp.ones((NHEADS,), jnp.float32)
        inp['gnorm_w'] = jnp.ones((D_INNER,), jnp.float32)
        inp['out_w'] = w(ks[5], (D_MODEL, D_INNER), D_INNER)
        inp['scorer_w1'] = w(ks[6], (HID, D_MODEL), D_MODEL)
        inp['scorer_w2'] = w(ks[7], (1, HID), HID)
        inp['summ_w'] = w(ks[8], (SDIM, D_MODEL), D_MODEL)
        inp['q_w'] = w(ks[9], (SDIM, D_MODEL), D_MODEL)
        inp['k_w'] = w(ks[10], (SDIM, SDIM), SDIM)
        inp['v_w'] = w(ks[11], (D_MODEL, SDIM), SDIM)
        inp['gate_w'] = w(ks[12], (D_MODEL, 2 * D_MODEL), 2 * D_MODEL)
        return inp
    _L1_attn_all = _L1_attn_setup()
    _L1_attn_in = {k: v for k, v in _L1_attn_all.items() if k in ('norm_w', 'in_w', 'conv_w', 'conv_b', 'dt_bias', 'A_log', 'D_param', 'gnorm_w', 'out_w', 'scorer_w1', 'scorer_w2', 'summ_w', 'q_w', 'k_w', 'v_w', 'gate_w')}
    del _L1_attn_all

    def _L1_ffn_setup():
        import jax, jax.numpy as jnp
        import numpy as np
        B, S, D, F, E = (4, 512, 256, 1024, 8)
        key = jax.random.key(seed)
        ks = jax.random.split(key, 7)
        s1 = 1.0 / np.sqrt(D)
        s2 = 1.0 / np.sqrt(F)
        x = jax.random.normal(ks[0], (B, S, D), dtype=jnp.float32)
        W1 = jax.random.uniform(ks[1], (E, D, F), jnp.float32, -s1, s1)
        b1 = jax.random.uniform(ks[2], (E, F), jnp.float32, -s1, s1)
        W2 = jax.random.uniform(ks[3], (E, F, D), jnp.float32, -s2, s2)
        b2 = jax.random.uniform(ks[4], (E, D), jnp.float32, -s2, s2)
        Wr = jax.random.uniform(ks[5], (D, E), jnp.float32, -s1, s1)
        br = jax.random.uniform(ks[6], (E,), jnp.float32, -s1, s1)
        return {'x': x, 'W1': W1, 'b1': b1, 'W2': W2, 'b2': b2, 'Wr': Wr, 'br': br}
    _L1_ffn_all = _L1_ffn_setup()
    _L1_ffn_in = {k: v for k, v in _L1_ffn_all.items() if k in ('W1', 'b1', 'W2', 'b2', 'Wr', 'br')}
    del _L1_ffn_all
    return {'x': x, 'ctx_2048': ctx_2048, 'L0_xattn_Wq': _L0_xattn_in['Wq'], 'L0_xattn_Wkv': _L0_xattn_in['Wkv'], 'L0_xattn_null_kv': _L0_xattn_in['null_kv'], 'L0_xattn_Wout': _L0_xattn_in['Wout'], 'L0_xattn_ln_scale': _L0_xattn_in['ln_scale'], 'L0_xattn_ln_bias': _L0_xattn_in['ln_bias'], 'L0_attn_Wq': _L0_attn_in['Wq'], 'L0_attn_Wk': _L0_attn_in['Wk'], 'L0_attn_Wv': _L0_attn_in['Wv'], 'L0_attn_Wo': _L0_attn_in['Wo'], 'L0_attn_bo': _L0_attn_in['bo'], 'L0_attn_ln_g': _L0_attn_in['ln_g'], 'L0_attn_ln_b': _L0_attn_in['ln_b'], 'L0_attn_q_gamma': _L0_attn_in['q_gamma'], 'L0_attn_k_gamma': _L0_attn_in['k_gamma'], 'L0_ffn_gate_w1': _L0_ffn_in['gate_w1'], 'L0_ffn_gate_b1': _L0_ffn_in['gate_b1'], 'L0_ffn_gate_w2': _L0_ffn_in['gate_w2'], 'L0_ffn_gate_b2': _L0_ffn_in['gate_b2'], 'L0_ffn_W1': _L0_ffn_in['W1'], 'L0_ffn_b1': _L0_ffn_in['b1'], 'L0_ffn_W2': _L0_ffn_in['W2'], 'L0_ffn_b2': _L0_ffn_in['b2'], 'L0_ffn_TW1': _L0_ffn_in['TW1'], 'L0_ffn_Tb1': _L0_ffn_in['Tb1'], 'L0_ffn_TW2': _L0_ffn_in['TW2'], 'L0_ffn_Tb2': _L0_ffn_in['Tb2'], 'L1_xattn_w_qkv': _L1_xattn_in['w_qkv'], 'L1_xattn_w_proj': _L1_xattn_in['w_proj'], 'L1_xattn_b_proj': _L1_xattn_in['b_proj'], 'L1_attn_norm_w': _L1_attn_in['norm_w'], 'L1_attn_in_w': _L1_attn_in['in_w'], 'L1_attn_conv_w': _L1_attn_in['conv_w'], 'L1_attn_conv_b': _L1_attn_in['conv_b'], 'L1_attn_dt_bias': _L1_attn_in['dt_bias'], 'L1_attn_A_log': _L1_attn_in['A_log'], 'L1_attn_D_param': _L1_attn_in['D_param'], 'L1_attn_gnorm_w': _L1_attn_in['gnorm_w'], 'L1_attn_out_w': _L1_attn_in['out_w'], 'L1_attn_scorer_w1': _L1_attn_in['scorer_w1'], 'L1_attn_scorer_w2': _L1_attn_in['scorer_w2'], 'L1_attn_summ_w': _L1_attn_in['summ_w'], 'L1_attn_q_w': _L1_attn_in['q_w'], 'L1_attn_k_w': _L1_attn_in['k_w'], 'L1_attn_v_w': _L1_attn_in['v_w'], 'L1_attn_gate_w': _L1_attn_in['gate_w'], 'L1_ffn_W1': _L1_ffn_in['W1'], 'L1_ffn_b1': _L1_ffn_in['b1'], 'L1_ffn_W2': _L1_ffn_in['W2'], 'L1_ffn_b2': _L1_ffn_in['b2'], 'L1_ffn_Wr': _L1_ffn_in['Wr'], 'L1_ffn_br': _L1_ffn_in['br']}

def reference(x, ctx_2048, L0_xattn_Wq, L0_xattn_Wkv, L0_xattn_null_kv, L0_xattn_Wout, L0_xattn_ln_scale, L0_xattn_ln_bias, L0_attn_Wq, L0_attn_Wk, L0_attn_Wv, L0_attn_Wo, L0_attn_bo, L0_attn_ln_g, L0_attn_ln_b, L0_attn_q_gamma, L0_attn_k_gamma, L0_ffn_gate_w1, L0_ffn_gate_b1, L0_ffn_gate_w2, L0_ffn_gate_b2, L0_ffn_W1, L0_ffn_b1, L0_ffn_W2, L0_ffn_b2, L0_ffn_TW1, L0_ffn_Tb1, L0_ffn_TW2, L0_ffn_Tb2, L1_xattn_w_qkv, L1_xattn_w_proj, L1_xattn_b_proj, L1_attn_norm_w, L1_attn_in_w, L1_attn_conv_w, L1_attn_conv_b, L1_attn_dt_bias, L1_attn_A_log, L1_attn_D_param, L1_attn_gnorm_w, L1_attn_out_w, L1_attn_scorer_w1, L1_attn_scorer_w2, L1_attn_summ_w, L1_attn_q_w, L1_attn_k_w, L1_attn_v_w, L1_attn_gate_w, L1_ffn_W1, L1_ffn_b1, L1_ffn_W2, L1_ffn_b2, L1_ffn_Wr, L1_ffn_br):
    import jax
    import jax.numpy as jnp

    def _L0_xattn_ref(x, context, Wq, Wkv, null_kv, Wout, ln_scale, ln_bias):
        import jax, jax.numpy as jnp
        import numpy as np
        B, N, DIM = (8, 1024, 256)
        M, CTX = (64, 512)
        HEADS, DH = (16, 64)
        INNER = HEADS * DH
        EPS = 1e-06

        def _split_heads(t):
            b, n, _ = t.shape
            return t.reshape(b, n, HEADS, DH).transpose(0, 2, 1, 3)
        scale = DH ** (-0.5)
        b = x.shape[0]
        q = _split_heads(jnp.einsum('bnd,df->bnf', x, Wq))
        kv = jnp.einsum('bmc,cf->bmf', context, Wkv)
        k, v = jnp.split(kv, 2, axis=-1)
        k, v = (_split_heads(k), _split_heads(v))
        nk = jnp.broadcast_to(null_kv[0], (b, HEADS, 1, DH))
        nv = jnp.broadcast_to(null_kv[1], (b, HEADS, 1, DH))
        k = jnp.concatenate((nk, k), axis=-2)
        v = jnp.concatenate((nv, v), axis=-2)
        q = q * scale
        sim = jnp.einsum('bhid,bhjd->bhij', q, k)
        attn = jax.nn.softmax(sim, axis=-1)
        out = jnp.einsum('bhij,bhjd->bhid', attn, v)
        out = out.transpose(0, 2, 1, 3).reshape(b, -1, INNER)
        out = jnp.einsum('bnf,fd->bnd', out, Wout)
        mu = jnp.mean(out, axis=-1, keepdims=True)
        var = jnp.var(out, axis=-1, keepdims=True)
        out = (out - mu) * jax.lax.rsqrt(var + EPS) * ln_scale + ln_bias
        return out

    def _L0_attn_ref(x, Wq, Wk, Wv, Wo, bo, ln_g, ln_b, q_gamma, k_gamma):
        import jax, jax.numpy as jnp
        import numpy as np
        DIM = 256
        DIM_HEAD = 64
        HEADS = DIM // DIM_HEAD
        SCALE = DIM_HEAD ** (-0.5)
        RMS_EPS = 1e-08
        LN_EPS = 1e-05

        def _layernorm(x, g, b):
            mu = jnp.mean(x, axis=-1, keepdims=True)
            var = jnp.mean(jnp.square(x - mu), axis=-1, keepdims=True)
            return (x - mu) * jax.lax.rsqrt(var + LN_EPS) * g + b

        def _rmsnorm(x, gamma):
            norm = jnp.sqrt(jnp.sum(jnp.square(x), axis=-1, keepdims=True)) * DIM_HEAD ** (-0.5)
            return x / jnp.maximum(norm, RMS_EPS) * gamma
        b, n, _ = x.shape
        xn = _layernorm(x, ln_g, ln_b)

        def split_heads(t):
            return t.reshape(b, n, HEADS, DIM_HEAD).transpose(0, 2, 1, 3)
        q = split_heads(xn @ Wq.T)
        k = split_heads(xn @ Wk.T)
        v = split_heads(xn @ Wv.T)
        q = _rmsnorm(q, q_gamma) * SCALE
        k = _rmsnorm(k, k_gamma)
        sim = jnp.einsum('bhid,bhjd->bhij', q, k)
        attn = jax.nn.softmax(sim, axis=-1)
        out = jnp.einsum('bhij,bhjd->bhid', attn, v)
        out = out.transpose(0, 2, 1, 3).reshape(b, n, DIM)
        return out @ Wo.T + bo

    def _L0_ffn_ref(hidden_states, gate_w1, gate_b1, gate_w2, gate_b2, W1, b1, W2, b2, TW1, Tb1, TW2, Tb2):
        import jax, jax.numpy as jnp
        import numpy as np
        B, S, H, F, E = (8, 512, 256, 1024, 8)
        INIT_LAMBDA = 0.2
        x = hidden_states
        h = jax.nn.relu(jnp.einsum('bsh,oh->bso', x, gate_w1) + gate_b1)
        g = jnp.einsum('bso,eo->bse', h, gate_w2) + gate_b2
        g = g.mean(axis=1)
        mW1 = W1 + jnp.einsum('be,efh->bfh', g, TW1)
        mb1 = b1 + g @ Tb1
        mW2 = W2 + jnp.einsum('be,ehf->bhf', g, TW2)
        mb2 = b2 + g @ Tb2
        u = jax.nn.gelu(jnp.einsum('bsh,bfh->bsf', x, mW1) + mb1[:, None, :])
        out = jnp.einsum('bsf,bhf->bsh', u, mW2) + mb2[:, None, :]
        return out

    def _L1_xattn_ref(x, context, w_qkv, w_proj, b_proj):
        import jax, jax.numpy as jnp
        import numpy as np
        NUM_HEADS = 16
        B, N, C = x.shape
        H = NUM_HEADS
        D = C // H
        scale = D ** (-0.5)
        qkv = (x @ w_qkv.T).reshape(B, N, 3, H, D).transpose(2, 0, 3, 1, 4)
        q, k, v = (qkv[0], qkv[1], qkv[2])
        N_c = context.shape[1]
        kv = context.reshape(B, N_c, 2, H, D).transpose(2, 0, 3, 1, 4)
        extra_k, extra_v = (kv[0], kv[1])
        k = jnp.concatenate([extra_k, k], axis=2)
        v = jnp.concatenate([extra_v, v], axis=2)
        dtype = q.dtype
        attn = jnp.einsum('bhnd,bhmd->bhnm', q * scale, k).astype(jnp.float32)
        attn = jax.nn.softmax(attn, axis=-1).astype(dtype)
        out = jnp.einsum('bhnm,bhmd->bhnd', attn, v)
        out = out.transpose(0, 2, 1, 3).reshape(B, N, C)
        return out @ w_proj.T + b_proj

    def _L1_attn_ref(x, norm_w, in_w, conv_w, conv_b, dt_bias, A_log, D_param, gnorm_w, out_w, scorer_w1, scorer_w2, summ_w, q_w, k_w, v_w, gate_w):
        import jax, jax.numpy as jnp
        import numpy as np
        D_MODEL = 256
        D_STATE = 128
        D_CONV = 4
        EXPAND = 2
        HEADDIM = 64
        D_INNER = D_MODEL * EXPAND
        NHEADS = D_INNER // HEADDIM
        CONV_DIM = D_INNER + 2 * D_STATE
        D_IN_PROJ = 2 * D_INNER + 2 * D_STATE + NHEADS
        POOL = 50
        SDIM = 64
        HEAD_DIM_RET = SDIM // 4
        TAU1 = 0.5
        TAU2 = 0.3
        HID = D_MODEL // 4
        B = 4
        T = 512
        EPS = 1e-05

        def _rmsnorm(x, w):
            return x * jax.lax.rsqrt(jnp.mean(x * x, axis=-1, keepdims=True) + EPS) * w

        def _mamba2(x, in_w, conv_w, conv_b, dt_bias, A_log, D_param, gnorm_w, out_w):
            Bn, Tn, _ = x.shape
            zxbcdt = x @ in_w.T
            z = zxbcdt[..., :D_INNER]
            xBC = zxbcdt[..., D_INNER:D_INNER + CONV_DIM]
            dt = zxbcdt[..., D_INNER + CONV_DIM:]
            xp = jnp.pad(jnp.transpose(xBC, (0, 2, 1)), ((0, 0), (0, 0), (D_CONV - 1, 0)))
            conv = jax.lax.conv_general_dilated(xp, conv_w[:, None, :], (1,), 'VALID', dimension_numbers=('NCH', 'OIH', 'NCH'), feature_group_count=CONV_DIM)
            xBC = jax.nn.silu(jnp.transpose(conv, (0, 2, 1)) + conv_b)
            xs = xBC[..., :D_INNER].reshape(Bn, Tn, NHEADS, HEADDIM)
            Bm = xBC[..., D_INNER:D_INNER + D_STATE]
            Cm = xBC[..., D_INNER + D_STATE:]
            dt = jax.nn.softplus(dt + dt_bias)
            A = -jnp.exp(A_log)
            dA = jnp.exp(dt * A)
            dtx = dt[..., None] * xs

            def step(h, inp):
                dA_t, dtx_t, B_t, C_t = inp
                h = h * dA_t[:, :, None, None] + dtx_t[..., None] * B_t[:, None, None, :]
                y = jnp.einsum('bhpn,bn->bhp', h, C_t)
                return (h, y)
            tm = lambda a: jnp.moveaxis(a, 1, 0)
            h0 = jnp.zeros((Bn, NHEADS, HEADDIM, D_STATE), x.dtype)
            _, ys = jax.lax.scan(step, h0, (tm(dA), tm(dtx), tm(Bm), tm(Cm)))
            y = jnp.moveaxis(ys, 0, 1) + D_param[None, None, :, None] * xs
            y = y.reshape(Bn, Tn, D_INNER)
            y = _rmsnorm(y * jax.nn.silu(z), gnorm_w)
            return y @ out_w.T

        def _update_memory(tokens, imp, summ_w, pool, prio, counts):
            Bn, Tn, Dm = tokens.shape
            S = min(Tn, POOL)
            order = jnp.argsort(-imp, axis=1)[:, :S]
            s_imp = jnp.take_along_axis(imp, order, axis=1)
            s_tok = jnp.take_along_axis(tokens, order[..., None], axis=1)
            s_sum = s_tok @ summ_w.T
            s_mask = s_imp > TAU1
            ar = jnp.arange(Bn)

            def body(carry, inp):
                pool, prio, counts = carry
                hi, si, ss = inp
                add = hi & (counts < POOL)
                idx = jnp.minimum(counts, POOL - 1)
                pool = pool.at[ar, idx].set(jnp.where(add[:, None], ss, pool[ar, idx]))
                prio = prio.at[ar, idx].set(jnp.where(add, si, prio[ar, idx]))
                counts = counts + add.astype(counts.dtype)
                repl = hi & (counts >= POOL)
                mi = jnp.argmin(prio, axis=1)
                should = repl & (si > prio[ar, mi])
                pool = pool.at[ar, mi].set(jnp.where(should[:, None], ss, pool[ar, mi]))
                prio = prio.at[ar, mi].set(jnp.where(should, si, prio[ar, mi]))
                return ((pool, prio, counts), None)
            xs = (jnp.moveaxis(s_mask, 1, 0), jnp.moveaxis(s_imp, 1, 0), jnp.moveaxis(s_sum, 1, 0))
            (pool, prio, counts), _ = jax.lax.scan(body, (pool, prio, counts), xs)
            return (pool, prio, counts)
        residual = x
        xn = _rmsnorm(x, norm_w)
        y = _mamba2(xn, in_w, conv_w, conv_b, dt_bias, A_log, D_param, gnorm_w, out_w)
        h = jax.nn.relu(y @ scorer_w1.T)
        scores = jax.nn.sigmoid((h @ scorer_w2.T)[..., 0])
        Bn = x.shape[0]
        pool = jnp.zeros((Bn, POOL, SDIM), x.dtype)
        prio = jnp.zeros((Bn, POOL), x.dtype)
        counts = jnp.zeros((Bn,), jnp.int32)
        pool, prio, counts = _update_memory(y, scores, summ_w, pool, prio, counts)
        mean_score = jnp.mean(scores, axis=1)
        retrieve_mask = (mean_score > TAU2) & (counts > 0)
        memory_mask = jnp.arange(POOL)[None, :] < counts[:, None]
        q = y @ q_w.T
        k = pool @ k_w.T
        v = pool @ v_w.T
        scale = np.float32(1.0 / np.sqrt(HEAD_DIM_RET))
        logits = jnp.einsum('btd,bpd->btp', q, k) * scale
        logits = jnp.where(memory_mask[:, None, :], logits, jnp.float32(-1000000000.0))
        attn = jax.nn.softmax(logits, axis=-1)
        retrieved = jnp.einsum('btp,bpd->btd', attn, v)
        gate = jax.nn.sigmoid(jnp.concatenate([y, retrieved], axis=-1) @ gate_w.T)
        y = y + gate * retrieved * retrieve_mask[:, None, None].astype(y.dtype)
        return residual + y

    def _L1_ffn_ref(x, W1, b1, W2, b2, Wr, br):
        import jax, jax.numpy as jnp
        import numpy as np
        B, S, D, F, E = (4, 512, 256, 1024, 8)
        b, s, d = x.shape
        e = Wr.shape[1]
        logits = x @ Wr + br
        idx = jnp.argmax(logits, axis=-1)
        probs = jax.nn.softmax(logits, axis=-1)
        gates = jnp.take_along_axis(probs, idx[..., None], axis=-1)[..., 0]
        xf = x.reshape(-1, d)
        idxf = idx.reshape(-1)
        gf = gates.reshape(-1)
        out = jnp.zeros_like(xf)
        for ei in range(e):
            h = jax.nn.gelu(xf @ W1[ei] + b1[ei], approximate=False)
            y = h @ W2[ei] + b2[ei]
            mask = (idxf == ei).astype(xf.dtype)
            out = out + y * (gf * mask)[:, None]
        return out.reshape(b, s, d)
    x = x + _L0_xattn_ref(_layernorm(x, axis=-1), ctx_2048, L0_xattn_Wq, L0_xattn_Wkv, L0_xattn_null_kv, L0_xattn_Wout, L0_xattn_ln_scale, L0_xattn_ln_bias)
    x = x + _L0_attn_ref(_layernorm(x, axis=-1), L0_attn_Wq, L0_attn_Wk, L0_attn_Wv, L0_attn_Wo, L0_attn_bo, L0_attn_ln_g, L0_attn_ln_b, L0_attn_q_gamma, L0_attn_k_gamma)
    x = x + _L0_ffn_ref(_layernorm(x, axis=-1), L0_ffn_gate_w1, L0_ffn_gate_b1, L0_ffn_gate_w2, L0_ffn_gate_b2, L0_ffn_W1, L0_ffn_b1, L0_ffn_W2, L0_ffn_b2, L0_ffn_TW1, L0_ffn_Tb1, L0_ffn_TW2, L0_ffn_Tb2)
    x = x + _L1_xattn_ref(_layernorm(x, axis=-1), ctx_2048, L1_xattn_w_qkv, L1_xattn_w_proj, L1_xattn_b_proj)
    x = x + _L1_attn_ref(_layernorm(x, axis=-1), L1_attn_norm_w, L1_attn_in_w, L1_attn_conv_w, L1_attn_conv_b, L1_attn_dt_bias, L1_attn_A_log, L1_attn_D_param, L1_attn_gnorm_w, L1_attn_out_w, L1_attn_scorer_w1, L1_attn_scorer_w2, L1_attn_summ_w, L1_attn_q_w, L1_attn_k_w, L1_attn_v_w, L1_attn_gate_w)
    x = x + _L1_ffn_ref(_layernorm(x, axis=-1), L1_ffn_W1, L1_ffn_b1, L1_ffn_W2, L1_ffn_b2, L1_ffn_Wr, L1_ffn_br)
    return x

_drawn_inputs = setup_inputs


def setup_inputs(seed=0):
    import zlib

    import numpy as np

    out = dict(_drawn_inputs(seed))
    spreads = {'L0_xattn_ln_scale': (1.0, 0.2),
     'L0_xattn_ln_bias': (0.0, 0.1),
     'L0_attn_ln_g': (1.0, 0.2),
     'L0_attn_ln_b': (0.0, 0.29),
     'L0_attn_q_gamma': (1.0, 0.6),
     'L0_attn_k_gamma': (1.0, 0.6),
     'L0_ffn_gate_b1': (0.0, 0.8),
     'L0_ffn_gate_b2': (0.20000000298023224, 0.6),
     'L1_attn_norm_w': (1.0, 0.2),
     'L1_attn_conv_b': (0.0, 0.1),
     'L1_attn_D_param': (1.0, 0.2),
     'L1_attn_gnorm_w': (1.0, 0.2)}
    factors = {'L0_xattn_null_kv': 8.0,
     'L0_ffn_gate_w1': 8.0,
     'L0_ffn_gate_w2': 8.0,
     'L0_ffn_b1': 8.0,
     'L0_ffn_b2': 3.567,
     'L0_ffn_Tb1': 8.0,
     'L0_ffn_Tb2': 5.801,
     'L1_xattn_w_qkv': 4.465,
     'L1_xattn_b_proj': 3.297,
     'L1_ffn_W1': 3.141,
     'L1_ffn_b1': 8.0,
     'L1_ffn_W2': 2.982,
     'L1_ffn_b2': 8.0,
     'L1_ffn_Wr': 3.27,
     'L1_ffn_br': 8.0}
    for name, (base, spread) in spreads.items():
        noise = np.random.default_rng([zlib.crc32(name.encode()), seed]).standard_normal(out[name].shape)
        drawn = base * np.exp(spread * noise) if base else spread * noise
        out[name] = jnp.asarray(drawn.astype(out[name].dtype))
    for name, factor in factors.items():
        out[name] = (out[name] * factor).astype(out[name].dtype)
    return out
```

```python
from contextlib import ExitStack

import concourse.bass as bass
import numpy as np
from concourse import mybir

ALU = mybir.AluOpType
ACT = mybir.ActivationFunctionType
F32 = mybir.dt.float32
AX_X = mybir.AxisListType.X

P = 128
B, NQ, DIM = 2, 64, 256
TOK = B * NQ
NCTX, CTX = 1024, 512
KT = DIM // P
CT = CTX // P
KEYT = NCTX // P
H0, DH0 = 16, 64
INNER = H0 * DH0
PAIRS = H0 // 2
HA = 4
F, E = 1024, 8
FT = F // P
H1, DH1 = 16, 16
DIN, DST, NH, HD = 512, 128, 8, 64
CONV, TAPS = DIN + 2 * DST, 4
CHT = CONV // P
PAD = NQ + TAPS - 1
POOL, SD, RETDIM = 50, 64, 16
UNIT = 2048

UNITS = (["wq", "wk0", "wk1", "wv0", "wv1", "wout", "att", "f1b"] + [f"f1e{e}" for e in range(E)]
         + ["f2b"] + [f"f2e{e}" for e in range(E)] + ["xat", "mb1", "mb2", "mb3"]
         + [f"m1e{e}" for e in range(E)] + [f"m2e{e}" for e in range(E)])
RELEASE = {u: n + 1 for n, u in enumerate(UNITS)}
NR, NA, NC = 4, 5, 8

CONST = {}
COLS = {}
VECS = {}


def _lay(table, items):
    at = 0
    for name, n in items:
        table[name] = (at, at + n)
        at += n
    return at


NCONST = _lay(CONST, [("ident", P), ("ones", P), ("same", P), ("causal", P), ("tie", P), ("neg", P),
                      ("hmask", 8), ("neghalf", 1), ("dec", E)])
NCOLS = _lay(COLS, [("gate_b1", KT), ("conv_w", CHT * TAPS), ("conv_b", CHT), ("nk", 1), ("gw2", KT * E),
                    ("wr", KT * E)])
NVECS = _lay(VECS, [("ln_scale", DIM), ("ln_bias", DIM), ("ln_g", DIM), ("ln_b", DIM), ("bo", DIM),
                    ("qk_gamma", 2 * DH0), ("gate_b2", E), ("nv", DH0), ("b_proj", DIM), ("norm_w", DIM),
                    ("gnorm_w", DIN), ("dt_bias", NH), ("A_log", NH), ("D_param", NH), ("sw2", SD), ("br", E)])
BIAS1, BIAS2 = (0, F), (F, F + DIM)
NROWS = F + DIM
N_RSQRT, RSQRT_QK = 11, 4
TURN0 = 10


def plan_places():
    last, plan = {}, []

    def put(unit, place, after=None):
        need = RELEASE[last[place]] if place in last else 0
        if after:
            need = max(need, RELEASE[after])
        last[place] = unit
        plan.append((unit, place, need))

    for unit, place in zip(UNITS[:7], (0, 1, 2, 3, 0, 1, 2)):
        put(unit, place)
    arena = list(range(NR, NR + NA))
    cycle = arena + [3, 0, 1, 2]
    first = UNITS.index("f1b")
    for n in range(9):
        put(UNITS[first + n], cycle[n], after="wout")
    for n in range(10):
        put(UNITS[first + 9 + n], cycle[n % 9])
    late = UNITS[UNITS.index("mb1"):]
    order = cycle[1:] + list(range(NR + NA, NR + NA + NC)) + [cycle[0], cycle[4], cycle[5]]
    for unit, place in zip(late, order):
        put(unit, place, after="xat" if place >= NR + NA else None)
    return plan


PLAN = plan_places()
PLACE = {unit: place for unit, place, _ in PLAN}
LANDED = {unit: 16 * sum(1 for _, q, _ in PLAN[:n + 1] if q == place) for n, (unit, place, _) in enumerate(PLAN)}


def bc(ap, axis, n):
    shape = list(ap.shape)
    shape.insert(axis, n)
    return ap.unsqueeze(axis).to_broadcast(shape)


def cut(base, at, *free):
    n = 1
    for f in free:
        n *= f
    ap = base[:, at:at + n]
    if len(free) == 1:
        return ap
    axes = "abcd"[:len(free)]
    return ap.rearrange(f"p ({' '.join(axes)}) -> p {' '.join(axes)}", **dict(zip(axes, free)))


ONCE = {
    "tensor_made": [
        "null_ps", "out0_ps", "qkT_ps", "simA_ps", "ptA_ps", "pvA_ps", "outA_ps", "gh_ps", "g_ps",
        "qk1_ps", "v1_ps", "o1tok_ps", "out1_ps", "xbc_ps", "dt_ps", "z_ps", "decay_ps", "G_ps",
        "xs_ps", "ym_ps", "ygT_ps", "y_tok_ps", "sc_ps", "pq_ps", "km_ps", "vm_ps", "lg_ps",
        "scT_ps", "rank_ps", "pmT_ps", "ret_ps", "retT_ps", "gate_ps", "route_ps", "maskT_ps"],
    "scalar_made": [
        "qT_sbA", "sq_ready", "qkT_sb", "simA_exp", "ptA_sb", "gT_sb", "expA", "xbc_sbA", "dte",
        "conv_tanh", "z_tanh", "dtl", "ex_ready", "gm_ready", "ygT_sb", "pq_sb", "sct", "km_sb",
        "vm_sb", "pm_exp", "pmT_sb", "retT_sb", "gate_tanh", "rz", "maskT_sb"],
    "vector_made": [
        "qT_sbV", "qk_ready", "simA_max", "probsA", "hm_ready", "k1_sb", "o1_ready", "xbc_sbV",
        "dtn_ready", "conv_done", "dtA_ready", "xs_act", "M_ready", "yg_ready", "scz", "scb_ready",
        "cmp_ready", "lmax", "pm_ready", "ret_sb", "mask_ready", "dm_ready", "rneg", "result"],
}


def perceiver_kernel(nc, x_in, ctx_in, ctxT_in, units_in, const_in, cols_in, vecs_in, rows_in, gate_in, out):
    with ExitStack() as stack:
        def sb(name, *free):
            return stack.enter_context(nc.sbuf_tensor(name, [P, *free], F32))

        names = {}

        def ev(name):
            if name not in names:
                names[name] = stack.enter_context(nc.semaphore(name))
            return names[name]

        ticked = {kind: [] for kind in ONCE}

        def made(name):
            kind = next(k for k, results in ONCE.items() if name in results)
            return ev(kind), ONCE[kind].index(name) + 1

        def tick(name):
            kind = next(k for k, results in ONCE.items() if name in results)
            ticked[kind].append(name)
            assert ticked[kind] == ONCE[kind][:len(ticked[kind])], "ONCE is not in the program's order"
            return ev(kind), 1

        ctxmem = sb("ctxmem", NC * UNIT)
        ctxT = cut(ctxmem, 0, B, CT, NCTX)
        ctxN = cut(ctxmem, B * CT * NCTX, B, KEYT, CTX)
        arena = sb("arena", 8 * UNIT)
        fixed = sb("fixed", NR * UNIT)
        pbuf = sb("pbuf", 4 * 1152)
        work = sb("work", PAIRS * TOK)
        const = sb("const", NCONST)
        cols = sb("cols", NCOLS)
        vecs = sb("vecs", NVECS)
        bias_rows = sb("bias_rows", NROWS)
        x = sb("x", DIM)
        hn = sb("hn", DIM)
        xn = sb("xn", DIM)
        xT = sb("xT", KT, TOK)
        vsb = sb("vsb", DIM)
        small = sb("small", 320)

        def c_(name):
            return const[:, CONST[name][0]:CONST[name][1]]

        def p_(name):
            return cols[:, COLS[name][0]:COLS[name][1]]

        def v_(name):
            return vecs[:, VECS[name][0]:VECS[name][1]]

        def unit(name):
            n = PLACE[name]
            if n < NR:
                return fixed[:, n * UNIT:(n + 1) * UNIT]
            if n < NR + NA:
                return arena[:, (n - NR) * UNIT:(n - NR + 1) * UNIT]
            n -= NR + NA
            return ctxmem[:, n * UNIT:(n + 1) * UNIT]

        ident = c_("ident")
        cw = p_("conv_w").rearrange("p (t k) -> p t k", t=CHT)
        W = [stack.enter_context(nc.psum_tensor(f"W{n}", [P, 1024], F32)) for n in range(4)]

        def bank(n):
            return W[n // 2][:, 512 * (n % 2):512 * (n % 2) + 512]

        st6, mv = cut(small, 0, 6), cut(small, 6, 2)
        ve, rstd = cut(small, 8, 1), cut(small, 9, 1)
        mx = cut(small, 10, 1)
        stat = cut(small, 16, B, PAIRS, 2)
        null_s = cut(small, 48, B * PAIRS)
        negm = cut(small, 64, B * PAIRS)
        tokstat = cut(small, 80, 2, 4, 2)
        rinv0, w_null = cut(small, 96, 2, 4), cut(small, 104, 2, 4)
        ssq, rqk = cut(small, 112, 8), cut(small, 120, 8)
        smax, ssum, srec = cut(small, 128, 4), cut(small, 132, 4), cut(small, 136, 4)
        hmean = cut(small, 140, KT, B)
        gmix = cut(small, 144, B, E)
        gtok = cut(small, 160, E + 1)
        selfmax = cut(small, 176, B * PAIRS)
        z1 = cut(small, 192, B * PAIRS, 2)
        z1s, rinv1 = cut(small, 224, B * PAIRS), cut(small, 240, B * PAIRS)
        dta, dtm, dtn, dte = (cut(small, 256 + 8 * n, NH) for n in range(4))
        dt, expA, dtA, dtAn = (cut(small, 128 + 8 * n, NH) for n in range(4))
        dneg = cut(small, 160, NH)
        scz, sct, score, msum, mtrue, cnt, rm = (cut(small, 288 + n, 1) for n in range(7))
        ms, lmax, zsum, zrec = (cut(small, 296 + n, 1) for n in range(4))
        rl, req, mask = (cut(small, 176 + 8 * n, E) for n in range(3))
        rmax, rsel, rneg, rz, gate = (cut(small, 304 + n, 1) for n in range(5))

        qp = cut(arena, 0, CT, B, H0, NQ)
        pt = cut(arena, CT * B * H0 * NQ, KEYT, 512)
        op = cut(arena, CT * B * H0 * NQ + KEYT * 512, CT, 8, TOK)
        probs0 = cut(pbuf, 0, 3, NCTX)
        heads0, tmp0 = cut(pbuf, 3072, 512), cut(pbuf, 3584, 512)
        gatew = cut(pbuf, 4096, KT, DIM)
        qT = cut(work, 0, PAIRS, TOK)
        oT0 = qT
        scr = arena[:, NA * UNIT:]
        QK, QKT, PA = cut(scr, 0, 512), cut(scr, 512, 4, TOK), cut(scr, 1024, HA, TOK)
        SA, PTA, SQ = cut(scr, 1536, HA, NQ), cut(scr, 1792, HA, TOK), cut(scr, 2304, 512)
        XE = cut(scr, 0, E, KT, TOK)
        U, UT = cut(scr, 2048, F), cut(scr, 3072, FT, TOK)
        HG, HM, GT = cut(scr, 4096, KT, TOK), cut(scr, 4352, KT, B * E), cut(scr, 4400, TOK)
        DM, MASKT, ACC = cut(scr, 4096, E * TOK), cut(scr, 5120, TOK), cut(scr, 5248, DIM)
        QZ = cut(scr, 0, 2, B, 8, NQ)
        PT1 = [cut(scr, 2048 + 1152 * n, 9, TOK) for n in range(2)]
        SELF, O1, K1 = cut(scr, 4352, B, PAIRS, NQ), cut(scr, 5376, B, PAIRS, 2, DH1), cut(scr, 5888, 2, TOK)
        probs1 = cut(pbuf, 0, 4, 1152)
        Q1 = cut(work, 0, 2, TOK)
        XP, C1 = cut(scr, 0, CHT, B, PAD), cut(scr, 832, CHT, TOK)
        XC, TH = cut(scr, 1600, CHT, TOK), cut(scr, 2368, CHT * TOK)
        ZS, ZT, XS = cut(scr, 3136, DIN), cut(scr, 3648, DIN), cut(scr, 4160, DIN)
        DTX, Y2, GM = cut(scr, 4672, DIN), cut(scr, 5184, DIN), cut(scr, 5696, TOK)
        DX = cut(scr, 0, DIN)
        EX, MT = cut(pbuf, 0, NH, TOK), cut(pbuf, 1024, NH, TOK)
        YG, YGT = cut(pbuf, 2048, DIN), cut(pbuf, 2560, 4, TOK)
        PQ, KM, VM = cut(pbuf, 3072, 2, TOK), cut(pbuf, 3328, TOK), cut(pbuf, 3456, DIM)
        SCB, SCT, CMP, CMP2, KEEP, KEEPS = (cut(pbuf, 3712 + P * n, P) for n in range(6))
        LG, PEN, PM, PMT = (cut(work, P * n, P) for n in range(4))
        RET, RETT = cut(work, 512, DIM), cut(work, 768, KT, TOK)
        GTH, G1 = cut(scr, 832, DIM), cut(scr, 1088, DIM)

        GROUPS = [(0, 0), (0, 1), (1, 0), (1, 1)]
        ROWT = 16

        def row(r):
            half, b = GROUPS[r // 4]
            return half, b, 4 * half + r % 4

        uses67 = []
        for g in range(4):
            uses67 += [("op_sb", 4 * g + c) for c in range(CT)]
            if g % 2:
                uses67 += [("st_sb", g // 2), ("hd_sb", g // 2)]

        def bank67(kind, n):
            return bank(6 + uses67.index((kind, n)) % 2)

        block = stack.enter_context(nc.Block())

        @block.sync
        def _(sync):
            sync.dma_start(x[:, :], x_in).then_inc(ev("x_in"), 16)
            sync.dma_start(const[:, :], const_in).then_inc(ev("const_in"), 16)

            def load(n):
                name, place, used = PLAN[n]
                if used:
                    sync.wait_ge(ev("units_used"), used)
                sync.dma_start(unit(name), units_in[UNITS.index(name)]).then_inc(ev(f"place{place}"), 16)

            for n in range(3):
                load(n)
            for b in range(B):
                sync.dma_start(ctxT[:, b], ctxT_in[b].rearrange("(c p) k -> p c k", p=P)).then_inc(ev(f"ctxT{b}"), 16)
                sync.dma_start(ctxN[:, b], ctx_in[b].rearrange("(t p) c -> p t c", p=P)).then_inc(ev(f"ctxN{b}"), 16)
                if b == 0:
                    load(3)
            for n in range(4, len(PLAN)):
                load(n)
                if PLAN[n][0] == "xat":
                    sync.wait_ge(ev("y_ps"), 1)
                    sync.dma_start(bias_rows[0:E, :], rows_in[E + 1:2 * E + 1, :]).then_inc(ev("rows2_in"), 16)
            sync.wait_ge(*made("result"))
            sync.dma_start(out, xn[:, :]).then_inc(ev("stored"), 16)
            sync.wait_ge(ev("stored"), 16)

        @block.gpsimd
        def _(pool):
            pool.dma_start(cols[:, :], cols_in).then_inc(ev("cols_in"), 16)
            pool.dma_start(vecs[:, :], vecs_in.partition_broadcast(P)).then_inc(ev("vecs_in"), 16)
            pool.dma_start(bias_rows[0:E + 1, :], rows_in[0:E + 1, :]).then_inc(ev("rows_in"), 16)
            pool.dma_start(gatew, gate_in).then_inc(ev("gatew_in"), 16)
            pool.wait_ge(ev("const_in"), 16)
            for n in range(N_RSQRT):
                pool.wait_ge(ev("var_ready"), n + 1)
                src, dst, wide = (ssq, rqk, 8) if n == RSQRT_QK else (ve, rstd, 1)
                pool.tensor_tensor(dst, src, c_("neghalf").to_broadcast([P, wide]), ALU.pow)\
                    .then_inc(ev("rstd_ready"), 1)
                if n == 1:
                    pool.memset(PA, 0.0).then_inc(ev("pa_zero"), 1)
                if n == 6:
                    for m in range(4):
                        pool.memset(probs1[:, m, NCTX + NQ * (1 - m % 2):NCTX + NQ * (2 - m % 2)], 0.0)\
                            .then_inc(ev("pads_zero"), 1)
                if n == 7:
                    pool.memset(XP[:, :, :, 0:TAPS - 1], 0.0).then_inc(ev("xp_zero"), 1)

        @block.scalar
        def _(act):
            turned = [0]

            def keep_xT(ps):
                turned[0] += 1
                act.wait_ge(ev("xT_ps"), turned[0])
                act.copy(xT[:, :, :], ps[:, 0:DIM].rearrange("p (k t) -> p k t", k=KT)).then_inc(ev("xT_sb"), 1)

            def hidden(n, func):
                for hf in range(2):
                    act.wait_ge(ev("pre_ps"), 2 * n + hf + 1)
                    act.activation(U[:, hf * 512:(hf + 1) * 512], bank(4 + hf), func).then_inc(ev("u_ready"), 1)

            keep_xT(bank(4))
            act.wait_ge(ev("qT_ps"), 1)
            act.mul(qT[:, 0:4, :], bank(6).rearrange("p (j t) -> p j t", j=4), DH0 ** -0.5).then_inc(*tick("qT_sbA"))
            for h in range(0, H0, 2):
                act.wait_ge(ev("qp_ps"), h + 1)
                act.copy(qp[:, :, :, h, :], bank(h % 4).rearrange("p (c b q) -> p c b q", c=CT, b=B))\
                    .then_inc(ev("qp_sbA"), 1)

            def keep_probs(r):
                half, b, j = row(r)
                act.wait_ge(ev("pt_ps"), 2 * r + 1)
                act.copy(pt[:, 0:4, (r % 4) * P:(r % 4 + 1) * P], bank(4).rearrange("p (t m) -> p t m", t=4))\
                    .then_inc(ev("pt_sbA"), 1)

            act.wait_ge(ev("null_sb"), 2)
            for r in range(ROWT + 1):
                if r >= 1:
                    keep_probs(r - 1)
                if r < ROWT:
                    half, b, j = row(r)
                    m = b * PAIRS + j
                    act.wait_ge(ev("negm_ready"), r + 1)
                    if r >= 3:
                        act.wait_ge(ev("pt_ps"), 2 * (r - 2))
                    act.activation(probs0[:, r % 3, :], W[r % 2][:, :], ACT.Exp, bias=negm[:, m:m + 1],
                                   accum_out=stat[:, b, j, 1:2]).then_inc(ev("exp_done"), 1)
                    act.activation(stat[:, b, j, 0:1], null_s[:, m:m + 1], ACT.Exp, bias=negm[:, m:m + 1])\
                        .then_inc(ev("p0_done"), 1)
                if r in (4, 8, 12, 16):
                    g = r // 4 - 1
                    half, b = GROUPS[g]
                    for c in range(CT):
                        act.wait_ge(ev("op_ps"), 4 * g + c + 1)
                        if g == 2 and c == 0:
                            act.wait_ge(ev("hd_ps"), 1)
                        act.copy(op[:, c, :, b * NQ:(b + 1) * NQ],
                                 bank67("op_sb", 4 * g + c).rearrange("p (h q) -> p h q", h=8)).then_inc(ev("op_sb"), 1)
                if r == TURN0 + 1:
                    act.wait_ge(ev("oT0_ps"), 1)
                    act.copy(oT0[:, 0:4, :], bank(4).rearrange("p (t m) -> p t m", t=4)).then_inc(ev("oT0_sb"), 1)
            act.wait_ge(ev("oT0_ps"), 2)
            act.copy(oT0[:, 4:8, :], bank(4).rearrange("p (t m) -> p t m", t=4)).then_inc(ev("oT0_sb"), 1)

            keep_xT(bank(1))
            act.wait_ge(ev("qkv_ps"), 1)
            act.activation(SQ, bank(2), ACT.Square).then_inc(*tick("sq_ready"))
            act.wait_ge(ev("qkv_ps"), 2)
            act.copy(vsb[:, :], bank(3)[:, 0:DIM]).then_inc(ev("v_sb"), 1)
            act.wait_ge(*made("qkT_ps"))
            act.copy(QKT, bank(4).rearrange("p (t m) -> p t m", t=4)).then_inc(*tick("qkT_sb"))
            act.wait_ge(*made("simA_max"))
            act.activation(SA, SA, ACT.Exp, scale=DH0 ** -0.5).then_inc(*tick("simA_exp"))
            act.wait_ge(*made("ptA_ps"))
            act.copy(PTA, bank(7).rearrange("p (t m) -> p t m", t=4)).then_inc(*tick("ptA_sb"))
            keep_xT(bank(1))

            keep_xT(bank(0))
            act.wait_ge(*made("gh_ps"))
            act.wait_ge(ev("cols_in"), 16)
            for o in range(KT):
                act.activation(HG[:, o, :], bank(1)[:, o * P:(o + 1) * P], ACT.Relu, bias=p_("gate_b1")[:, o:o + 1])\
                    .then_inc(ev("hg_ready"), 1)
            act.wait_ge(ev("gT_ps"), 1)
            act.copy(GT[0:E + 1, :], bank(3)[0:E + 1, 0:TOK]).then_inc(*tick("gT_sb"))
            hidden(0, ACT.Gelu_apprx_tanh)

            keep_xT(bank(4))
            act.wait_ge(*made("v1_ps"))
            act.copy(vsb[:, :], bank(6)[:, 0:DIM]).then_inc(ev("v_sb"), 1)
            act.wait_ge(ev("self_ps"), 1)
            act.copy(SELF[:, 0], bank(4).rearrange("p (j q) -> p j q", j=PAIRS)).then_inc(ev("self_sb"), 1)
            act.wait_ge(ev("pads_zero"), 4)
            for r in range(ROWT + 1):
                if r >= 1:
                    for n, (t, bk) in enumerate(((0, 4), (6, 7))):
                        act.wait_ge(ev("pt1_ps"), 3 * (r - 1) + (1, 3)[n])
                        if r >= 3:
                            act.wait_ge(ev("pv1_ps"), r - 2)
                        act.copy(PT1[(r - 1) % 2][:, t:t + 3, :], bank(bk)[:, 0:3 * P].rearrange("p (t m) -> p t m", t=3))\
                            .then_inc(ev("pt1_sbA"), 1)
                if r < ROWT:
                    b, j = r % 2, r // 2
                    m = b * PAIRS + j
                    act.wait_ge(ev("negm1_ready"), r + 1)
                    if r >= 4:
                        act.wait_ge(ev("pt1_ps"), 3 * (r - 3))
                    act.activation(probs1[:, r % 4, 0:NCTX], W[r % 2][:, :], ACT.Exp, bias=negm[:, m:m + 1],
                                   accum_out=z1[:, m, 0:1]).then_inc(ev("exp1_ctx"), 1)
                    act.activation(probs1[:, r % 4, NCTX + NQ * b:NCTX + NQ * (b + 1)], SELF[:, b, j, :], ACT.Exp,
                                   bias=negm[:, m:m + 1], accum_out=z1[:, m, 1:2]).then_inc(ev("exp1_done"), 1)
            keep_xT(bank(4))

            act.activation(expA, v_("A_log"), ACT.Exp).then_inc(*tick("expA"))
            keep_xT(bank(0))
            act.wait_ge(*made("xbc_ps"))
            act.copy(XP[:, 4:6, :, TAPS - 1:], bank(3)[:, 0:2 * TOK].rearrange("p (t b q) -> p t b q", t=2, b=B))\
                .then_inc(*tick("xbc_sbA"))
            act.wait_ge(*made("xbc_sbA"))
            act.wait_ge(*made("xbc_sbV"))
            for t in range(CHT):
                act.activation(C1[:, t, :].rearrange("p (b q) -> p b q", b=B), XP[:, t, :, TAPS - 1:], ACT.Identity,
                               bias=p_("conv_b")[:, t:t + 1], scale=cw[:, t, TAPS - 1:TAPS]).then_inc(ev("tap3"), 1)
            act.wait_ge(*made("dtn_ready"))
            act.activation(dte, dtn, ACT.Exp).then_inc(*tick("dte"))
            act.wait_ge(*made("conv_done"))
            act.activation(TH, C1.rearrange("p t m -> p (t m)"), ACT.Tanh, scale=0.5).then_inc(*tick("conv_tanh"))
            act.wait_ge(*made("z_ps"))
            act.activation(ZT, bank(4), ACT.Tanh, scale=0.5).then_inc(*tick("z_tanh"))
            act.wait_ge(*made("dte"))
            act.activation(dte, dte, ACT.Ln, bias=1.0).then_inc(*tick("dtl"))
            act.wait_ge(*made("decay_ps"))
            act.activation(EX, W[1][:, :].rearrange("p (h t) -> p h t", h=NH), ACT.Exp).then_inc(*tick("ex_ready"))
            act.wait_ge(*made("G_ps"))
            act.mul(GM, bank(6)[:, 0:TOK], 0.25).then_inc(*tick("gm_ready"))
            act.wait_ge(*made("ygT_ps"))
            act.copy(YGT, bank(0).rearrange("p (t m) -> p t m", t=4)).then_inc(*tick("ygT_sb"))
            keep_xT(bank(0))
            act.wait_ge(*made("pq_ps"))
            act.copy(PQ[0:SD], bank(2)[0:SD, 0:2 * TOK].rearrange("p (n t) -> p n t", n=2)).then_inc(*tick("pq_sb"))
            act.wait_ge(*made("scz"))
            act.activation(sct, scz, ACT.Tanh, scale=0.5).then_inc(*tick("sct"))
            act.wait_ge(*made("km_ps"))
            act.copy(KM[0:SD, :], bank(3)[0:SD, 0:TOK]).then_inc(*tick("km_sb"))
            act.wait_ge(*made("vm_ps"))
            act.copy(VM, bank(4)[:, 0:DIM]).then_inc(*tick("vm_sb"))
            act.wait_ge(*made("lmax"))
            act.activation(PM, LG, ACT.Exp, bias=lmax, accum_out=zsum).then_inc(*tick("pm_exp"))
            act.wait_ge(*made("pmT_ps"))
            act.copy(PMT, bank(0)[:, 0:P]).then_inc(*tick("pmT_sb"))
            act.wait_ge(*made("retT_ps"))
            act.copy(RETT, bank(3)[:, 0:DIM].rearrange("p (k t) -> p k t", k=KT)).then_inc(*tick("retT_sb"))
            act.wait_ge(*made("gate_ps"))
            act.activation(GTH, bank(6)[:, 0:DIM], ACT.Tanh, scale=0.5).then_inc(*tick("gate_tanh"))

            keep_xT(bank(0))
            act.wait_ge(*made("rneg"))
            act.activation(rl, rl, ACT.Exp, bias=rneg, accum_out=rz).then_inc(*tick("rz"))
            act.wait_ge(*made("maskT_ps"))
            act.copy(MASKT[0:E, :], bank(0)[0:E, 0:TOK]).then_inc(*tick("maskT_sb"))
            for hf in range(2):
                act.wait_ge(ev("xm_ps"), 2 * hf + 1)
                act.copy(XE[:, 4 * hf:4 * hf + 4, 0, :], bank((1, 2)[hf]).rearrange("p (e t) -> p e t", e=4))\
                    .then_inc(ev("xm_sbA"), 1)
            hidden(1, ACT.Gelu)

        @block.vector
        def _(dve):
            steps, asked, given = [0], [0], [0]

            def step(ins):
                steps[0] += 1
                ins.then_inc(ev("vector_step"), 1)
                dve.wait_ge(ev("vector_step"), steps[0])

            def rsqrt(ins):
                asked[0] += 1
                ins.then_inc(ev("var_ready"), 1)
                dve.wait_ge(ev("rstd_ready"), asked[0])

            def norm(src, dst, eps):
                step(dve.bn_stats(st6, src))
                step(dve.bn_aggr(mv, st6))
                rsqrt(dve.tensor_scalar(ve, mv[:, 1:2], eps, None, ALU.add))
                return dve.tensor_scalar(dst, src, mv[:, 0:1], rstd, ALU.subtract, ALU.mult)

            def give(ins):
                given[0] += 1
                ins.then_inc(ev("xn_ready"), 1)

            def use_hidden(n):
                for hf in range(2):
                    dve.wait_ge(ev("uT_ps"), 2 * n + hf + 1)
                    dve.tensor_copy(UT[:, 4 * hf:4 * hf + 4, :], bank(6 + hf).rearrange("p (t m) -> p t m", t=4))\
                        .then_inc(ev("uT_sb"), 1)

            dve.wait_ge(ev("x_in"), 16)
            give(norm(x[:, :], xn[:, :], 1e-5))
            dve.wait_ge(ev("vecs_in"), 16)
            step(dve.tensor_tensor(x[:, :], x[:, :], v_("ln_bias"), ALU.add))
            dve.wait_ge(ev("qT_ps"), 2)
            dve.tensor_scalar(qT[:, 4:8, :], bank(7).rearrange("p (j t) -> p j t", j=4), DH0 ** -0.5, None, ALU.mult)\
                .then_inc(*tick("qT_sbV"))
            for h in range(1, H0, 2):
                dve.wait_ge(ev("qp_ps"), h + 1)
                dve.tensor_copy(qp[:, :, :, h, :], bank(h % 4).rearrange("p (c b q) -> p c b q", c=CT, b=B))\
                    .then_inc(ev("qp_sbV"), 1)
            dve.wait_ge(*made("null_ps"))
            dve.tensor_copy(null_s[0:NQ, :], bank(5)[0:NQ, 0:16]).then_inc(ev("null_sb"), 1)
            dve.tensor_copy(null_s[NQ:P, :], bank(4)[NQ:P, 0:16]).then_inc(ev("null_sb"), 1)
            dve.wait_ge(ev("null_sb"), 2)

            def join_heads(half):
                dve.wait_ge(ev("st_ps"), half + 1)
                dve.tensor_copy(tokstat, bank67("st_sb", half)[:, 0:16].rearrange("p (h j s) -> p h j s", h=2, j=4))\
                    .then_inc(ev("st_sb"), 1)
                dve.wait_ge(ev("st_sb"), half + 1)
                step(dve.tensor_tensor(rinv0, tokstat[:, :, :, 0], tokstat[:, :, :, 1], ALU.add))
                step(dve.reciprocal(rinv0, rinv0))
                step(dve.tensor_tensor(w_null, tokstat[:, :, :, 0], rinv0, ALU.mult))
                step(dve.tensor_tensor(tmp0.rearrange("p (j h d) -> p j h d", j=4, h=2),
                                       bc(w_null.rearrange("p h j -> p j h"), 3, DH0),
                                       bc(bc(v_("nv"), 1, 2), 1, 4), ALU.mult))
                dve.wait_ge(ev("hd_ps"), half + 1)
                if half:
                    dve.wait_ge(ev("oT0_ps"), 1)
                dve.tensor_tensor(heads0.rearrange("p (j h d) -> p j h d", j=4, h=2),
                                  bank67("hd_sb", half).rearrange("p (j h d) -> p j h d", j=4, h=2),
                                  bc(rinv0.rearrange("p h j -> p j h"), 3, DH0), ALU.mult).then_inc(ev("hd_sb"), 1)
                dve.wait_ge(ev("hd_sb"), half + 1)
                dve.tensor_tensor(heads0, heads0, tmp0, ALU.add).then_inc(ev("hd_ready"), 1)

            for r in range(ROWT + 1):
                if r >= 1:
                    dve.wait_ge(ev("pt_ps"), 2 * r)
                    dve.tensor_copy(pt[:, 4:8, ((r - 1) % 4) * P:((r - 1) % 4 + 1) * P],
                                    bank(5).rearrange("p (t m) -> p t m", t=4)).then_inc(ev("pt_sbV"), 1)
                if r < ROWT:
                    half, b, j = row(r)
                    m = b * PAIRS + j
                    dve.wait_ge(ev("sim_done"), r + 1)
                    step(dve.tensor_reduce(mx, W[r % 2][:, :], AX_X, ALU.max))
                    dve.tensor_scalar(negm[:, m:m + 1], mx, null_s[:, m:m + 1], -1.0, ALU.max, ALU.mult)\
                        .then_inc(ev("negm_ready"), 1)
                if r == 9:
                    join_heads(0)
            join_heads(1)
            dve.wait_ge(*made("out0_ps"))
            step(norm(bank(0)[:, 0:DIM], xn[:, :], 1e-6))
            step(dve.tensor_tensor(xn[:, :], xn[:, :], v_("ln_scale"), ALU.mult))
            step(dve.tensor_tensor(x[:, :], x[:, :], xn[:, :], ALU.add))

            step(norm(x[:, :], hn[:, :], 1e-5))
            step(norm(hn[:, :], xn[:, :], 1e-5))
            step(dve.tensor_tensor(xn[:, :], xn[:, :], v_("ln_g"), ALU.mult))
            give(dve.tensor_tensor(xn[:, :], xn[:, :], v_("ln_b"), ALU.add))
            step(dve.tensor_tensor(x[:, :], x[:, :], v_("bo"), ALU.add))
            dve.wait_ge(*made("sq_ready"))
            step(dve.tensor_reduce(ssq, SQ.rearrange("p (h d) -> p h d", h=8), AX_X, ALU.add))
            rsqrt(dve.tensor_scalar(ssq, ssq, 1.0 / DH0, 1e-16, ALU.mult, ALU.max))
            step(dve.tensor_tensor(QK.rearrange("p (h d) -> p h d", h=8), bank(2).rearrange("p (h d) -> p h d", h=8),
                                   bc(rqk, 2, DH0), ALU.mult))
            qk4 = QK.rearrange("p (n h d) -> p n h d", n=2, h=HA)
            dve.tensor_tensor(qk4, qk4, bc(v_("qk_gamma").rearrange("p (n d) -> p n d", n=2), 2, HA), ALU.mult)\
                .then_inc(*tick("qk_ready"))
            dve.wait_ge(*made("simA_ps"))
            sa4 = SA.rearrange("p (i m) q -> p i m q", m=2)
            for b in range(B):
                for m in range(2):
                    ins = dve.tensor_copy(sa4[b * NQ:(b + 1) * NQ, :, m, :],
                                          bank(5 + m)[b * NQ:(b + 1) * NQ, 0:2 * TOK]
                                          .rearrange("p (i t) -> p i t", i=2)[:, :, b * NQ:(b + 1) * NQ])
            step(ins)
            step(dve.tensor_reduce(smax, SA, AX_X, ALU.max))
            dve.tensor_tensor(SA, SA, bc(smax, 2, NQ), ALU.subtract).then_inc(*tick("simA_max"))
            dve.wait_ge(*made("simA_exp"))
            step(dve.tensor_reduce(ssum, SA, AX_X, ALU.add))
            step(dve.reciprocal(srec, ssum))
            dve.wait_ge(ev("pa_zero"), 1)
            for b in range(B):
                lo, hi = b * NQ, (b + 1) * NQ
                ins = dve.tensor_tensor(PA[lo:hi, :, lo:hi], SA[lo:hi], bc(srec[lo:hi], 2, NQ), ALU.mult)
            ins.then_inc(*tick("probsA"))
            dve.wait_ge(*made("pvA_ps"))
            give(dve.tensor_copy(xn[:, :], bank(0)[:, 0:DIM]))
            dve.wait_ge(*made("outA_ps"))
            step(dve.tensor_tensor(x[:, :], bank(2)[:, 0:DIM], x[:, :], ALU.add))

            give(norm(x[:, :], hn[:, :], 1e-5))
            dve.wait_ge(ev("hg_ready"), 2)
            step(dve.tensor_reduce(hmean, HG.rearrange("p k (b s) -> p k b s", b=B), AX_X, ALU.add))
            dve.wait_ge(ev("cols_in"), 16)
            dve.tensor_tensor(HM.rearrange("p k (b e) -> p k b e", b=B),
                              bc(p_("gw2").rearrange("p (k e) -> p k e", k=KT), 2, B), bc(hmean, 3, E), ALU.mult)\
                .then_inc(*tick("hm_ready"))
            dve.wait_ge(*made("g_ps"))
            step(dve.scalar_tensor_tensor(out=gmix, in0=bank(2)[:, 0:B * E].rearrange("p (b e) -> p b e", b=B),
                                          scalar=1.0 / NQ, in1=bc(v_("gate_b2"), 1, B), op0=ALU.mult, op1=ALU.add))
            dve.tensor_copy(gtok[0:NQ, 0:E], gmix[0:NQ, 0, :]).then_inc(ev("gtok_ready"), 1)
            dve.tensor_copy(gtok[NQ:P, 0:E], gmix[NQ:P, 1, :]).then_inc(ev("gtok_ready"), 1)
            dve.tensor_copy(gtok[:, E:E + 1], c_("ones")[:, 0:1]).then_inc(ev("gtok_ready"), 1)
            for e in range(E):
                dve.tensor_tensor(XE[:, e].rearrange("p k (b s) -> p k b s", b=B),
                                  xT[:, :, :].rearrange("p k (b s) -> p k b s", b=B),
                                  bc(bc(gmix[:, :, e], 1, KT), 3, NQ), ALU.mult).then_inc(ev("xe_ready"), 1)
            use_hidden(0)
            for n in range(E + 1):
                dve.wait_ge(ev("y_ps"), n + 1)
                if n == 0:
                    dve.tensor_tensor(x[:, :], bank(0)[:, 0:DIM], x[:, :], ALU.add).then_inc(ev("y_used"), 1)
                else:
                    dve.scalar_tensor_tensor(out=x[:, :], in0=bank(n % 4)[:, 0:DIM], scalar=gtok[:, n - 1:n],
                                             in1=x[:, :], op0=ALU.mult, op1=ALU.add).then_inc(ev("y_used"), 1)
                dve.wait_ge(ev("y_used"), n + 1)

            give(norm(x[:, :], hn[:, :], 1e-5))
            step(dve.tensor_tensor(x[:, :], x[:, :], v_("b_proj"), ALU.add))
            dve.wait_ge(*made("qk1_ps"))
            step(dve.tensor_copy(Q1, bank(5)[:, 0:2 * TOK].rearrange("p (i t) -> p i t", i=2)))
            dve.tensor_copy(K1, bank(5)[:, 2 * TOK:].rearrange("p (i t) -> p i t", i=2)).then_inc(*tick("k1_sb"))
            for i in range(2):
                for b in range(B):
                    dve.tensor_tensor(QZ[:, i, b], bc(Q1[:, i, b * NQ:(b + 1) * NQ], 1, 8), bc(c_("hmask"), 2, NQ),
                                      ALU.mult).then_inc(ev("qz_ready"), 1)
            dve.wait_ge(ev("self_ps"), 2)
            dve.tensor_copy(SELF[:, 1], bank(7).rearrange("p (j q) -> p j q", j=PAIRS)).then_inc(ev("self_sb"), 1)
            dve.wait_ge(ev("self_sb"), 2)
            step(dve.tensor_reduce(selfmax, SELF.rearrange("p b j q -> p (b j) q"), AX_X, ALU.max))
            for r in range(ROWT + 1):
                if r >= 1:
                    dve.wait_ge(ev("pt1_ps"), 3 * (r - 1) + 2)
                    if r >= 3:
                        dve.wait_ge(ev("pv1_ps"), r - 2)
                    dve.tensor_copy(PT1[(r - 1) % 2][:, 3:6, :], bank(5)[:, 0:3 * P].rearrange("p (t m) -> p t m", t=3))\
                        .then_inc(ev("pt1_sbV"), 1)
                if r < ROWT:
                    m = (r % 2) * PAIRS + r // 2
                    dve.wait_ge(ev("sim1_done"), r + 1)
                    step(dve.tensor_reduce(mx, W[r % 2][:, :], AX_X, ALU.max))
                    dve.tensor_scalar(negm[:, m:m + 1], mx, selfmax[:, m:m + 1], -1.0, ALU.max, ALU.mult)\
                        .then_inc(ev("negm1_ready"), 1)
            dve.wait_ge(ev("exp1_done"), ROWT)
            step(dve.tensor_tensor(z1s, z1[:, :, 0], z1[:, :, 1], ALU.add))
            step(dve.reciprocal(rinv1, z1s))
            dve.wait_ge(ev("pv1_ps"), ROWT)
            dve.tensor_tensor(O1.rearrange("p b j h d -> p (b j) (h d)"), bank(6).rearrange("p (m n) -> p m n", m=ROWT),
                              bc(rinv1, 2, 2 * DH1), ALU.mult).then_inc(*tick("o1_ready"))
            dve.wait_ge(*made("o1tok_ps"))
            give(dve.tensor_copy(xn[:, :], bank(0)[:, 0:DIM]))
            dve.wait_ge(*made("out1_ps"))
            step(dve.tensor_tensor(x[:, :], bank(1)[:, 0:DIM], x[:, :], ALU.add))

            step(norm(x[:, :], hn[:, :], 1e-5))
            step(dve.tensor_tensor_reduce(out=xn[:, :], in0=hn[:, :], in1=hn[:, :], scale=1.0, scalar=0.0,
                                          op0=ALU.mult, op1=ALU.add, accum_out=ms))
            rsqrt(dve.tensor_scalar(ve, ms, 1.0 / DIM, 1e-5, ALU.mult, ALU.add))
            give(dve.scalar_tensor_tensor(out=xn[:, :], in0=hn[:, :], scalar=rstd, in1=v_("norm_w"), op0=ALU.mult,
                                          op1=ALU.mult))
            step(dve.tensor_tensor(x[:, :], x[:, :], hn[:, :], ALU.add))
            dve.wait_ge(*made("xbc_ps"))
            dve.wait_ge(ev("xp_zero"), 1)
            dve.tensor_copy(XP[:, 0:4, :, TAPS - 1:], bank(2).rearrange("p (t b q) -> p t b q", t=4, b=B))\
                .then_inc(*tick("xbc_sbV"))
            dve.wait_ge(*made("dt_ps"))
            step(dve.tensor_tensor(dta, bank(5)[:, 0:NH], v_("dt_bias"), ALU.add))
            step(dve.tensor_scalar(dneg, dta, -1.0, None, ALU.mult))
            dve.tensor_tensor(dtn, dta, dneg, ALU.min).then_inc(*tick("dtn_ready"))
            step(dve.tensor_scalar(dtm, dta, 0.0, None, ALU.max))
            dve.wait_ge(*made("xbc_sbA"))
            for k in range(TAPS - 1):
                for t in range(CHT):
                    if k == 0:
                        dve.wait_ge(ev("tap3"), t + 1)
                    c1 = C1[:, t, :].rearrange("p (b q) -> p b q", b=B)
                    ins = dve.scalar_tensor_tensor(out=c1, in0=XP[:, t, :, k:k + NQ], scalar=cw[:, t, k:k + 1], in1=c1,
                                                   op0=ALU.mult, op1=ALU.add)
                    if k < TAPS - 2 and t == CHT - 1:
                        step(ins)
            ins.then_inc(*tick("conv_done"))
            dve.wait_ge(*made("dtl"))
            step(dve.tensor_tensor(dt, dtm, dte, ALU.add))
            step(dve.tensor_tensor(dtAn, dt, expA, ALU.mult))
            dve.tensor_scalar(dtA, dtAn, -1.0, None, ALU.mult).then_inc(*tick("dtA_ready"))
            dve.wait_ge(*made("conv_tanh"))
            dve.scalar_tensor_tensor(out=XC.rearrange("p t m -> p (t m)"), in0=TH, scalar=1.0,
                                     in1=C1.rearrange("p t m -> p (t m)"), op0=ALU.add, op1=ALU.mult)\
                .then_inc(*tick("xs_act"))
            dve.wait_ge(*made("z_tanh"))
            step(dve.scalar_tensor_tensor(out=ZS, in0=ZT, scalar=1.0, in1=bank(4), op0=ALU.add, op1=ALU.mult))
            dve.wait_ge(*made("xs_ps"))
            step(dve.tensor_scalar(XS, bank(1), 0.5, None, ALU.mult))
            xs3 = XS.rearrange("p (h d) -> p h d", h=NH)
            step(dve.tensor_tensor(DTX.rearrange("p (h d) -> p h d", h=NH), xs3, bc(dt, 2, HD), ALU.mult))
            step(dve.tensor_tensor(DX.rearrange("p (h d) -> p h d", h=NH), xs3, bc(v_("D_param"), 2, HD), ALU.mult))
            dve.wait_ge(*made("ex_ready"))
            dve.wait_ge(*made("gm_ready"))
            dve.tensor_tensor(MT, EX, bc(GM, 1, NH), ALU.mult).then_inc(*tick("M_ready"))
            dve.wait_ge(*made("ym_ps"))
            step(dve.tensor_tensor(Y2, bank(7), DX, ALU.add))
            step(dve.scalar_tensor_tensor(out=Y2, in0=Y2, scalar=0.5, in1=ZS, op0=ALU.mult, op1=ALU.mult))
            step(dve.tensor_tensor_reduce(out=YG, in0=Y2, in1=Y2, scale=1.0, scalar=0.0, op0=ALU.mult, op1=ALU.add,
                                          accum_out=ms))
            rsqrt(dve.tensor_scalar(ve, ms, 1.0 / DIN, 1e-5, ALU.mult, ALU.add))
            dve.scalar_tensor_tensor(out=YG, in0=Y2, scalar=rstd, in1=v_("gnorm_w"), op0=ALU.mult, op1=ALU.mult)\
                .then_inc(*tick("yg_ready"))
            dve.wait_ge(*made("y_tok_ps"))
            give(dve.tensor_copy(xn[:, :], bank(2)[:, 0:DIM]))
            dve.wait_ge(ev("xn_ready"), given[0])
            step(dve.tensor_tensor(x[:, :], x[:, :], xn[:, :], ALU.add))

            dve.wait_ge(*made("sc_ps"))
            dve.scalar_tensor_tensor(out=SCB[:, 0:SD], in0=bank(1)[:, 0:SD], scalar=0.0, in1=v_("sw2"), op0=ALU.max,
                                     op1=ALU.mult, accum_out=scz).then_inc(*tick("scz"))
            dve.wait_ge(*made("sct"))
            step(dve.tensor_scalar(score, sct, 0.5, 0.5, ALU.mult, ALU.add))
            dve.tensor_scalar(SCB, c_("ones"), score, None, ALU.mult).then_inc(*tick("scb_ready"))
            dve.wait_ge(*made("scT_ps"))
            step(dve.tensor_copy(SCT, bank(7)[:, 0:P]))
            dve.scalar_tensor_tensor(out=CMP, in0=SCT, scalar=score, in1=c_("same"), op0=ALU.is_lt, op1=ALU.mult)
            step(dve.scalar_tensor_tensor(out=CMP2, in0=SCT, scalar=score, in1=c_("tie"), op0=ALU.is_equal,
                                          op1=ALU.mult))
            dve.tensor_tensor(CMP, CMP, CMP2, ALU.add).then_inc(*tick("cmp_ready"))
            step(dve.tensor_tensor_reduce(out=KEEP, in0=SCT, in1=c_("same"), scale=1.0, scalar=0.0, op0=ALU.mult,
                                          op1=ALU.add, accum_out=msum))
            step(dve.tensor_scalar(mtrue, msum, 1.0 / NQ, 0.3, ALU.mult, ALU.is_gt))
            dve.wait_ge(*made("rank_ps"))
            step(dve.scalar_tensor_tensor(out=KEEP, in0=bank(1)[:, 0:P], scalar=float(POOL), in1=c_("same"),
                                          op0=ALU.is_lt, op1=ALU.mult))
            step(dve.scalar_tensor_tensor(out=KEEPS, in0=SCT, scalar=0.5, in1=KEEP, op0=ALU.is_gt, op1=ALU.mult,
                                          accum_out=cnt))
            dve.tensor_scalar(PEN, KEEPS, -1.0, 1e9, ALU.add, ALU.mult)
            dve.wait_ge(*made("lg_ps"))
            step(dve.scalar_tensor_tensor(out=LG, in0=bank(5)[:, 0:P], scalar=RETDIM ** -0.5, in1=KEEPS, op0=ALU.mult,
                                          op1=ALU.mult))
            step(dve.tensor_tensor(LG, LG, PEN, ALU.add))
            dve.tensor_reduce(lmax, LG, AX_X, ALU.max, negate=True).then_inc(*tick("lmax"))
            step(dve.scalar_tensor_tensor(out=rm, in0=cnt, scalar=0.0, in1=mtrue, op0=ALU.is_gt, op1=ALU.mult))
            step(dve.tensor_scalar(rm, rm, 0.5, None, ALU.mult))
            dve.wait_ge(*made("pm_exp"))
            step(dve.reciprocal(zrec, zsum))
            dve.tensor_scalar(PM, PM, zrec, None, ALU.mult).then_inc(*tick("pm_ready"))
            dve.wait_ge(*made("ret_ps"))
            dve.tensor_copy(RET, bank(2)[:, 0:DIM]).then_inc(*tick("ret_sb"))
            dve.wait_ge(*made("ret_sb"))
            dve.wait_ge(*made("gate_tanh"))
            step(dve.scalar_tensor_tensor(out=G1, in0=GTH, scalar=1.0, in1=RET, op0=ALU.add, op1=ALU.mult))
            step(dve.scalar_tensor_tensor(out=x[:, :], in0=G1, scalar=rm, in1=x[:, :], op0=ALU.mult, op1=ALU.add))

            give(norm(x[:, :], hn[:, :], 1e-5))
            dve.wait_ge(*made("route_ps"))
            step(dve.tensor_tensor(rl, bank(1)[:, 0:E], v_("br"), ALU.add))
            step(dve.tensor_reduce(rmax, rl, AX_X, ALU.max))
            step(dve.scalar_tensor_tensor(out=req, in0=rl, scalar=rmax, in1=c_("dec"), op0=ALU.is_equal, op1=ALU.mult))
            step(dve.tensor_reduce(rsel, req, AX_X, ALU.max))
            dve.tensor_scalar(mask, req, rsel, None, ALU.is_equal).then_inc(*tick("mask_ready"))
            dve.wait_ge(*made("mask_ready"))
            dve.tensor_tensor(DM.rearrange("p (e t) -> p e t", e=E), bc(ident, 1, E), bc(mask, 2, TOK), ALU.mult)\
                .then_inc(*tick("dm_ready"))
            dve.tensor_scalar(rneg, rmax, -1.0, None, ALU.mult).then_inc(*tick("rneg"))
            for hf in range(2):
                dve.wait_ge(ev("xm_ps"), 2 * hf + 2)
                dve.tensor_copy(XE[:, 4 * hf:4 * hf + 4, 1, :], bank((7, 3)[hf]).rearrange("p (e t) -> p e t", e=4))\
                    .then_inc(ev("xm_sbV"), 1)
            dve.wait_ge(*made("rz"))
            step(dve.reciprocal(gate, rz))
            use_hidden(1)
            for n in range(E + 1):
                m = E + 1 + n
                dve.wait_ge(ev("y_ps"), m + 1)
                if n == 0:
                    dve.tensor_copy(ACC, bank(0)[:, 0:DIM]).then_inc(ev("y_used"), 1)
                else:
                    dve.scalar_tensor_tensor(out=ACC, in0=bank(n % 4)[:, 0:DIM], scalar=mask[:, n - 1:n], in1=ACC,
                                             op0=ALU.mult, op1=ALU.add).then_inc(ev("y_used"), 1)
                dve.wait_ge(ev("y_used"), m + 1)
            dve.scalar_tensor_tensor(out=xn[:, :], in0=ACC, scalar=gate, in1=x[:, :], op0=ALU.mult, op1=ALU.add)\
                .then_inc(*tick("result"))

        @block.tensor
        def _(pe):
            turned = [0]

            def need(u):
                pe.wait_ge(ev(f"place{PLACE[u]}"), LANDED[u])

            def turn_x(dst, src, let_go=False):
                turned[0] += 1
                pe.wait_ge(ev("xn_ready"), turned[0])
                mm = pe.transpose(dst[:, 0:P], src[:, 0:P], ident)
                if let_go:
                    mm.then_inc(ev("units_used"), 1)
                pe.transpose(dst[:, P:2 * P], src[:, P:2 * P], ident).then_inc(ev("xT_ps"), 1)
                pe.wait_ge(ev("xT_sb"), turned[0])

            pe.wait_ge(ev("const_in"), 16)
            turn_x(bank(4), xn)
            wq = unit("wq").rearrange("p (k n) -> p k n", k=KT)
            need("wq")
            for j in range(PAIRS):
                for k in range(KT):
                    mm = pe.matmul(W[3][:, j * P:(j + 1) * P], wq[:, k, j * P:(j + 1) * P], xT[:, k, :],
                                   start=(k == 0), stop=(k == KT - 1))
                if j == PAIRS // 2 - 1:
                    mm.then_inc(ev("qT_ps"), 1)
            mm.then_inc(ev("qT_ps"), 1)
            pe.wait_ge(*made("qT_sbA"))
            pe.wait_ge(*made("qT_sbV"))
            for h in range(H0):
                j, o = h // 2, DH0 * (h % 2)
                u = "wk0" if j < 4 else "wk1"
                if h in (0, 8):
                    need(u)
                wk = unit(u).rearrange("p (j c) -> p j c", j=4)
                if h >= 4:
                    pe.wait_ge(ev("qp_sbA" if h % 2 == 0 else "qp_sbV"), (h - 4) // 2 + 1)
                for c in range(CT):
                    mm = pe.matmul(bank(h % 4)[:, c * P:(c + 1) * P], wk[o:o + DH0, j % 4, c * P:(c + 1) * P],
                                   qT[o:o + DH0, j, :], start=True, stop=True)
                mm.then_inc(ev("qp_ps"), 1)
            pe.wait_ge(ev("cols_in"), 16)
            for b in range(B):
                for j in range(PAIRS):
                    for hh in range(2):
                        o = DH0 * hh
                        mm = pe.matmul(bank(5 - hh)[o:o + NQ, b * PAIRS + j:b * PAIRS + j + 1],
                                       qT[o:o + DH0, j, b * NQ:(b + 1) * NQ], p_("nk")[o:o + DH0, :],
                                       start=True, stop=True)
                        if b == 0 and j < 3 and hh == 0:
                            mm.then_inc(ev("units_used"), 1)
            mm.then_inc(*tick("null_ps"))

            def sim(r):
                half, b, j = row(r)
                if r == 0:
                    pe.wait_ge(ev("qp_sbA"), H0 // 2)
                    pe.wait_ge(ev("qp_sbV"), H0 // 2)
                if r % 4 == 0 and r < 8:
                    pe.wait_ge(ev(f"ctxT{b}"), 16)
                if r >= 2:
                    pe.wait_ge(ev("exp_done"), r - 1)
                for kh in range(2):
                    for c in range(CT):
                        mm = pe.matmul(W[r % 2][:, kh * 512:(kh + 1) * 512],
                                       qp[:, c, b, 2 * j:2 * j + 2, :].rearrange("p h q -> p (h q)"),
                                       ctxT[:, b, c, kh * 512:(kh + 1) * 512], start=(c == 0), stop=(c == CT - 1))
                mm.then_inc(ev("sim_done"), 1)

            def turn_probs(r):
                pe.wait_ge(ev("exp_done"), r + 1)
                for c in range(2):
                    if r == 0:
                        pe.wait_ge(ev("null_sb"), 2)
                    else:
                        pe.wait_ge(ev("pt_sbA" if c == 0 else "pt_sbV"), r)
                    if r == TURN0 + 1 and c == 0:
                        pe.wait_ge(ev("oT0_sb"), 1)
                    for t in range(4):
                        mm = pe.transpose(bank(4 + c)[:, t * P:(t + 1) * P],
                                          probs0[:, r % 3, (4 * c + t) * P:(4 * c + t + 1) * P], ident)
                    mm.then_inc(ev("pt_ps"), 1)

            def free67(kind, n):
                at = uses67.index((kind, n))
                if at >= 2:
                    before, m = uses67[at - 2]
                    pe.wait_ge(ev(before), m + 1)
                return bank67(kind, n)

            def attend(g):
                half, b = GROUPS[g]
                pe.wait_ge(ev(f"ctxN{b}"), 16)
                pe.wait_ge(ev("pt_sbA"), 4 * (g + 1))
                pe.wait_ge(ev("pt_sbV"), 4 * (g + 1))
                for c in range(CT):
                    ps = free67("op_sb", 4 * g + c)
                    for t in range(KEYT):
                        mm = pe.matmul(ps, ctxN[:, b, t, c * P:(c + 1) * P], pt[:, t, :],
                                       start=(t == 0), stop=(t == KEYT - 1))
                    mm.then_inc(ev("op_ps"), 1)

            def project_heads(half):
                ps = free67("st_sb", half)
                pe.wait_ge(ev("p0_done"), 8 * (half + 1))
                for hh in range(2):
                    for b in range(B):
                        mm = pe.matmul(ps[b * NQ:(b + 1) * NQ, hh * 8:hh * 8 + 8], ident[:, hh * NQ:(hh + 1) * NQ],
                                       stat[:, b, 4 * half:4 * half + 4, :].rearrange("p j s -> p (j s)"),
                                       start=True, stop=True)
                mm.then_inc(ev("st_ps"), 1)
                pe.wait_ge(ev("op_sb"), 8 * (half + 1))
                if half == 0:
                    need("wv0")
                    need("wv1")
                ps = free67("hd_sb", half)
                for h in range(8):
                    for c in range(CT):
                        wv = unit("wv0" if c < 2 else "wv1").rearrange("p (c n) -> p c n", c=2)
                        hg = 8 * half + h
                        mm = pe.matmul(ps[:, h * DH0:(h + 1) * DH0], op[:, c, h, :],
                                       wv[:, c % 2, hg * DH0:(hg + 1) * DH0], start=(c == 0), stop=(c == CT - 1))
                mm.then_inc(ev("hd_ps"), 1)

            def turn_heads(half):
                pe.wait_ge(ev("pt_sbA"), TURN0 + 1 if half == 0 else ROWT)
                pe.wait_ge(ev("hd_ready"), half + 1)
                for t in range(4):
                    mm = pe.transpose(bank(4)[:, t * P:(t + 1) * P], heads0[:, t * P:(t + 1) * P], ident)
                    if half == 1 and t < 2:
                        mm.then_inc(ev("units_used"), 1)
                mm.then_inc(ev("oT0_ps"), 1)

            for r in range(ROWT + 1):
                if r < ROWT:
                    sim(r)
                if r >= 1:
                    turn_probs(r - 1)
                if r in (4, 8, 12, 16):
                    attend(r // 4 - 1)
                if r == 9:
                    project_heads(0)
                if r == TURN0 + 1:
                    turn_heads(0)
            project_heads(1)
            turn_heads(1)
            pe.wait_ge(ev("oT0_sb"), 2)
            need("wout")
            wo = unit("wout").rearrange("p (j n) -> p j n", j=PAIRS)
            for j in range(PAIRS):
                mm = pe.matmul(bank(0)[:, 0:DIM], oT0[:, j, :], wo[:, j, :], start=(j == 0), stop=(j == PAIRS - 1))
            mm.then_inc(*tick("out0_ps"))

            turn_x(bank(1), xn, let_go=True)
            need("att")
            wa = unit("att")[:, 0:KT * 768].rearrange("p (k n) -> p k n", k=KT)
            wo = unit("att")[:, KT * 768:].rearrange("p (k n) -> p k n", k=KT)
            for lo, hi in ((0, 512), (512, 768)):
                for k in range(KT):
                    mm = pe.matmul(W[1][:, lo:hi], xT[:, k, :], wa[:, k, lo:hi], start=(k == 0), stop=(k == KT - 1))
                mm.then_inc(ev("qkv_ps"), 1)
            pe.wait_ge(*made("qk_ready"))
            for t in range(4):
                mm = pe.transpose(bank(4)[:, t * P:(t + 1) * P], QK[:, t * P:(t + 1) * P], ident)
            mm.then_inc(*tick("qkT_ps"))
            pe.wait_ge(*made("qkT_sb"))
            for h in range(HA):
                o = DH0 * (h % 2)
                mm = pe.matmul(bank(5 + h % 2)[:, (h // 2) * P:(h // 2 + 1) * P], QKT[o:o + DH0, h // 2, :],
                               QKT[o:o + DH0, 2 + h // 2, :], start=True, stop=True)
            mm.then_inc(*tick("simA_ps"))
            pe.wait_ge(*made("probsA"))
            for h in range(HA):
                mm = pe.transpose(bank(7)[:, h * P:(h + 1) * P], PA[:, h, :], ident)
            mm.then_inc(*tick("ptA_ps"))
            pe.wait_ge(*made("ptA_sb"))
            pe.wait_ge(ev("v_sb"), 1)
            for h in range(HA):
                mm = pe.matmul(bank(0)[:, h * DH0:(h + 1) * DH0], PTA[:, h, :], vsb[:, h * DH0:(h + 1) * DH0],
                               start=True, stop=True)
            mm.then_inc(*tick("pvA_ps"))
            turn_x(bank(1), xn)
            for k in range(KT):
                mm = pe.matmul(bank(2)[:, 0:DIM], xT[:, k, :], wo[:, k, :], start=(k == 0), stop=(k == KT - 1))
            mm.then_inc(*tick("outA_ps"))

            turn_x(bank(0), hn, let_go=True)
            pe.wait_ge(ev("gatew_in"), 16)
            for o in range(KT):
                for k in range(KT):
                    mm = pe.matmul(bank(1)[:, o * P:(o + 1) * P], gatew[:, k, o * P:(o + 1) * P], xT[:, k, :],
                                   start=(k == 0), stop=(k == KT - 1))
            mm.then_inc(*tick("gh_ps"))

            def layer1(u, lhs, start):
                w = unit(u).rearrange("p (k n) -> p k n", k=KT)
                need(u)
                for hf in range(2):
                    for k in range(KT):
                        mm = pe.matmul(bank(4 + hf), lhs(k), w[:, k, hf * 512:(hf + 1) * 512],
                                       start=start and k == 0, stop=False)
                mm.then_inc(ev("units_used"), 1)

            layer1("f1b", lambda k: xT[:, k, :], True)
            pe.wait_ge(*made("hm_ready"))
            for k in range(KT):
                mm = pe.matmul(bank(2)[:, 0:B * E], c_("ones"), HM[:, k, :], start=(k == 0), stop=(k == KT - 1))
            mm.then_inc(*tick("g_ps"))
            for e in range(E):
                pe.wait_ge(ev("xe_ready"), e + 1)
                layer1(f"f1e{e}", lambda k: XE[:, e, k, :], False)
                if e == 0:
                    pe.wait_ge(ev("gtok_ready"), 3)
                    pe.transpose(bank(3)[0:E + 1, 0:P], gtok, ident).then_inc(ev("gT_ps"), 1)
            pe.wait_ge(*made("gT_sb"))
            pe.wait_ge(ev("rows_in"), 16)

            def finish_layer1(lhs, n):
                for hf in range(2):
                    pe.matmul(bank(4 + hf), lhs, bias_rows[0:n, 512 * hf:512 * (hf + 1)], start=False, stop=True)\
                        .then_inc(ev("pre_ps"), 1)

            def turn_hidden(n):
                for hf in range(2):
                    pe.wait_ge(ev("u_ready"), 2 * n + hf + 1)
                    for t in range(4):
                        mm = pe.transpose(bank(6 + hf)[:, t * P:(t + 1) * P],
                                          U[:, (4 * hf + t) * P:(4 * hf + t + 1) * P], ident)
                    mm.then_inc(ev("uT_ps"), 1)

            def layer2(u, n):
                w = unit(u).rearrange("p (t n) -> p t n", t=FT)
                need(u)
                if n % (E + 1) >= 4:
                    pe.wait_ge(ev("y_used"), n - 3)
                for t in range(FT):
                    mm = pe.matmul(bank(n % (E + 1) % 4)[:, 0:DIM], UT[:, t, :], w[:, t, :], start=(t == 0),
                                   stop=(t == FT - 1 and u != "f2b"))
                    if t == 0 and u[:3] == "f2e" and u != "f2e0":
                        mm.then_inc(ev("units_used"), 1)
                return mm

            finish_layer1(GT[0:E + 1, :], E + 1)
            turn_hidden(0)
            pe.wait_ge(ev("uT_sb"), 2)
            layer2("f2b", 0).then_inc(ev("units_used"), 1)
            pe.matmul(bank(0)[:, 0:DIM], GT[0:E + 1, :], bias_rows[0:E + 1, F:], start=False, stop=True)\
                .then_inc(ev("y_ps"), 1)
            for e in range(E):
                layer2(f"f2e{e}", e + 1).then_inc(ev("y_ps"), 1)

            turn_x(bank(4), hn, let_go=True)
            need("xat")
            wx = unit("xat")[:, 0:KT * 768].rearrange("p (k n) -> p k n", k=KT)
            wp = unit("xat")[:, KT * 768:].rearrange("p (k n) -> p k n", k=KT)
            for i in range(4):
                for k in range(KT):
                    mm = pe.matmul(bank(5)[:, i * P:(i + 1) * P], wx[:, k, i * P:(i + 1) * P], xT[:, k, :],
                                   start=(k == 0), stop=(k == KT - 1))
            mm.then_inc(*tick("qk1_ps"))
            for k in range(KT):
                mm = pe.matmul(bank(6)[:, 0:DIM], xT[:, k, :], wx[:, k, 512:768], start=(k == 0), stop=(k == KT - 1))
            mm.then_inc(*tick("v1_ps"))
            pe.wait_ge(*made("k1_sb"))
            pe.wait_ge(ev("qz_ready"), 4)
            pe.wait_ge(ev("v_sb"), 2)
            for b in range(B):
                for j in range(PAIRS):
                    i, jj = j // 4, j % 4
                    mm = pe.matmul(bank(4 + 3 * b)[:, j * NQ:(j + 1) * NQ],
                                   QZ[:, i, b, 2 * jj:2 * jj + 2, :].rearrange("p h q -> p (h q)"),
                                   K1[:, i, b * NQ:(b + 1) * NQ], start=True, stop=True)
                mm.then_inc(ev("self_ps"), 1)

            def sim1(r):
                b, j = r % 2, r // 2
                i, jj = j // 4, j % 4
                if r >= 2:
                    pe.wait_ge(ev("exp1_done"), r - 1)
                for kh in range(2):
                    mm = pe.matmul(W[r % 2][:, kh * 512:(kh + 1) * 512],
                                   QZ[:, i, b, 2 * jj:2 * jj + 2, :].rearrange("p h q -> p (h q)"),
                                   ctxT[:, b, i, kh * 512:(kh + 1) * 512], start=True, stop=True)
                mm.then_inc(ev("sim1_done"), 1)

            def turn1(r):
                pe.wait_ge(ev("exp1_done"), r + 1)
                for c in range(3):
                    if r >= 1:
                        pe.wait_ge(ev("pt1_sb" + "AVA"[c]), (2 * r if c != 1 else r))
                    elif c == 0:
                        pe.wait_ge(ev("self_sb"), 2)
                    for t in range(3):
                        mm = pe.transpose(bank((4, 5, 7)[c])[:, t * P:(t + 1) * P],
                                          probs1[:, r % 4, (3 * c + t) * P:(3 * c + t + 1) * P], ident)
                    mm.then_inc(ev("pt1_ps"), 1)

            def attend1(r):
                b, j = r % 2, r // 2
                pe.wait_ge(ev("pt1_sbA"), 2 * (r + 1))
                pe.wait_ge(ev("pt1_sbV"), r + 1)
                for t in range(9):
                    rhs = ctxN[:, b, t, DIM + 32 * j:DIM + 32 * j + 32] if t < 8 else vsb[:, 32 * j:32 * j + 32]
                    mm = pe.matmul(bank(6)[:, (b * PAIRS + j) * 32:(b * PAIRS + j + 1) * 32], PT1[r % 2][:, t, :], rhs,
                                   start=(t == 0), stop=(t == 8))
                mm.then_inc(ev("pv1_ps"), 1)

            for r in range(ROWT + 2):
                if r < ROWT:
                    sim1(r)
                if 1 <= r <= ROWT:
                    turn1(r - 1)
                if r >= 2:
                    attend1(r - 2)
            pe.wait_ge(*made("o1_ready"))
            for hh in range(2):
                for b in range(B):
                    mm = pe.matmul(bank(0)[b * NQ:(b + 1) * NQ, 0:DIM].rearrange("p (j h d) -> p h j d", j=PAIRS, h=2)[:, hh],
                                   ident[:, hh * NQ:(hh + 1) * NQ], O1[:, b, :, hh, :], start=True, stop=True)
            mm.then_inc(*tick("o1tok_ps"))
            turn_x(bank(4), xn)
            for k in range(KT):
                mm = pe.matmul(bank(1)[:, 0:DIM], xT[:, k, :], wp[:, k, :], start=(k == 0), stop=(k == KT - 1))
            mm.then_inc(*tick("out1_ps"))

            turn_x(bank(0), xn, let_go=True)
            need("mb1")
            wx = unit("mb1")[:, 0:KT * CONV].rearrange("p (k n) -> p k n", k=KT)
            wd = unit("mb1")[:, KT * CONV:KT * (CONV + NH)].rearrange("p (k n) -> p k n", k=KT)
            need("mb2")
            wz = unit("mb2")[:, 0:KT * DIN].rearrange("p (k n) -> p k n", k=KT)
            wo2 = unit("mb2")[:, KT * DIN:].rearrange("p (k n) -> p k n", k=DIN // P)
            need("mb3")
            w3 = unit("mb3")
            for t in range(CHT):
                for k in range(KT):
                    mm = pe.matmul(W[1][:, t * P:(t + 1) * P], wx[:, k, t * P:(t + 1) * P], xT[:, k, :],
                                   start=(k == 0), stop=(k == KT - 1))
            mm.then_inc(*tick("xbc_ps"))
            for k in range(KT):
                mm = pe.matmul(bank(5)[:, 0:NH], xT[:, k, :], wd[:, k, :], start=(k == 0), stop=(k == KT - 1))
            mm.then_inc(*tick("dt_ps"))
            for k in range(KT):
                mm = pe.matmul(bank(4), xT[:, k, :], wz[:, k, :], start=(k == 0), stop=(k == KT - 1))
                if k == 0:
                    mm.then_inc(ev("units_used"), 1)
            mm.then_inc(*tick("z_ps"))
            pe.wait_ge(*made("dtA_ready"))
            for h in range(NH):
                bk = bank(2 + h // 4)
                if h == 0:
                    pe.wait_ge(*made("xbc_sbA"))
                    pe.wait_ge(*made("xbc_sbV"))
                if h % 4 == 0:
                    pe.matmul(bk, ident, bc(c_("neg"), 1, 4), start=True, stop=False, skip_group_check=True)
                ps = bk[:, (h % 4) * P:(h % 4 + 1) * P]
                pe.matmul(ps, dtA[:, h:h + 1].to_broadcast([P, P]), c_("causal"), start=False, stop=False, skip_group_check=True)
                mm = pe.matmul(ps, c_("causal"), dtAn[:, h:h + 1].to_broadcast([P, P]), start=False, stop=(h % 4 == 3), skip_group_check=True)
            mm.then_inc(*tick("decay_ps"))
            pe.wait_ge(*made("xs_act"))
            pe.matmul(bank(6)[:, 0:P], XC[:, 4, :], XC[:, 5, :], start=True, stop=True).then_inc(*tick("G_ps"))
            for t in range(4):
                mm = pe.transpose(bank(1)[:, t * P:(t + 1) * P], XC[:, t, :], ident)
            mm.then_inc(*tick("xs_ps"))
            pe.wait_ge(*made("M_ready"))
            for h in range(NH):
                mm = pe.matmul(bank(7)[:, h * HD:(h + 1) * HD], MT[:, h, :], DTX[:, h * HD:(h + 1) * HD], start=True, stop=True)
            mm.then_inc(*tick("ym_ps"))
            pe.wait_ge(*made("yg_ready"))
            for t in range(4):
                mm = pe.transpose(bank(0)[:, t * P:(t + 1) * P], YG[:, t * P:(t + 1) * P], ident)
            mm.then_inc(*tick("ygT_ps"))
            pe.wait_ge(*made("ygT_sb"))
            for t in range(4):
                mm = pe.matmul(bank(2)[:, 0:DIM], YGT[:, t, :], wo2[:, t, :], start=(t == 0), stop=(t == 3))
            mm.then_inc(*tick("y_tok_ps"))
            turn_x(bank(0), xn, let_go=True)
            sw1 = w3[:, 0:128].rearrange("p (k n) -> p k n", k=KT)
            summ = w3[:, 128:256].rearrange("p (k n) -> p k n", k=KT)
            qw = w3[:, 256:384].rearrange("p (k n) -> p k n", k=KT)
            kw = w3[0:SD, 384:448]
            vw = w3[0:SD, 448:704]
            gw2 = w3[:, 704:1728].rearrange("p (k n) -> p k n", k=4)
            for k in range(KT):
                mm = pe.matmul(bank(1)[:, 0:SD], xT[:, k, :], sw1[:, k, :], start=(k == 0), stop=(k == KT - 1))
            mm.then_inc(*tick("sc_ps"))
            for n, w in enumerate((summ, qw)):
                for k in range(KT):
                    mm = pe.matmul(bank(2)[0:SD, n * P:(n + 1) * P], w[:, k, :], xT[:, k, :],
                                   start=(k == 0), stop=(k == KT - 1))
            mm.then_inc(*tick("pq_ps"))
            for k in range(KT):
                pe.matmul(bank(6)[:, 0:DIM], xT[:, k, :], gw2[:, k, :], start=(k == 0), stop=False)
            pe.wait_ge(*made("pq_sb"))
            pe.matmul(bank(3)[0:SD, 0:P], kw, PQ[0:SD, 0, :], start=True, stop=True).then_inc(*tick("km_ps"))
            pe.matmul(bank(4)[:, 0:DIM], PQ[0:SD, 0, :], vw, start=True, stop=True).then_inc(*tick("vm_ps"))
            pe.wait_ge(*made("km_sb"))
            pe.matmul(bank(5)[:, 0:P], PQ[0:SD, 1, :], KM[0:SD, :], start=True, stop=True).then_inc(*tick("lg_ps"))
            pe.wait_ge(*made("scb_ready"))
            pe.transpose(bank(7)[:, 0:P], SCB, ident).then_inc(*tick("scT_ps"))
            pe.wait_ge(*made("cmp_ready"))
            pe.matmul(bank(1)[:, 0:P], c_("ones"), CMP, start=True, stop=True).then_inc(*tick("rank_ps"))
            pe.wait_ge(*made("pm_ready"))
            pe.transpose(bank(0)[:, 0:P], PM, ident).then_inc(*tick("pmT_ps"))
            pe.wait_ge(*made("pmT_sb"))
            pe.wait_ge(*made("vm_sb"))
            pe.matmul(bank(2)[:, 0:DIM], PMT, VM, start=True, stop=True).then_inc(*tick("ret_ps"))
            pe.wait_ge(*made("ret_sb"))
            for k in range(KT):
                mm = pe.transpose(bank(3)[:, k * P:(k + 1) * P], RET[:, k * P:(k + 1) * P], ident)
            mm.then_inc(*tick("retT_ps"))
            pe.wait_ge(*made("retT_sb"))
            for k in range(KT):
                mm = pe.matmul(bank(6)[:, 0:DIM], RETT[:, k, :], gw2[:, 2 + k, :], start=False, stop=(k == 1))
            mm.then_inc(*tick("gate_ps"))

            turn_x(bank(0), hn, let_go=True)
            wr = p_("wr").rearrange("p (k e) -> p k e", k=KT)
            for k in range(KT):
                mm = pe.matmul(bank(1)[:, 0:E], xT[:, k, :], wr[:, k, :], start=(k == 0), stop=(k == KT - 1))
            mm.then_inc(*tick("route_ps"))
            pe.wait_ge(*made("mask_ready"))
            pe.transpose(bank(0)[0:E, 0:P], mask, ident).then_inc(*tick("maskT_ps"))
            pe.wait_ge(*made("dm_ready"))
            for hf in range(2):
                for k in range(KT):
                    bk = bank(((1, 7), (2, 3))[hf][k])
                    pe.matmul(bk, hn[:, k * P:(k + 1) * P], DM[:, hf * 512:(hf + 1) * 512], start=True, stop=True)\
                        .then_inc(ev("xm_ps"), 1)
            for e in range(E):
                if e % 4 == 0:
                    pe.wait_ge(ev("xm_sbA"), e // 4 + 1)
                    pe.wait_ge(ev("xm_sbV"), e // 4 + 1)
                layer1(f"m1e{e}", lambda k: XE[:, e, k, :], e == 0)
            pe.wait_ge(*made("maskT_sb"))
            pe.wait_ge(ev("rows2_in"), 16)
            finish_layer1(MASKT[0:E, :], E)
            turn_hidden(1)
            pe.wait_ge(ev("uT_sb"), 4)
            pe.matmul(bank(0)[:, 0:DIM], MASKT[0:E, :], bias_rows[0:E, F:], start=True, stop=True)\
                .then_inc(ev("y_ps"), 1)
            for e in range(E):
                layer2(f"m2e{e}", E + 2 + e).then_inc(ev("y_ps"), 1)


def _unit(*parts):
    flat = []
    for a, rows in parts:
        tiles = a.shape[0] // rows
        a = a.reshape(tiles, rows, a.shape[1]).transpose(1, 0, 2).reshape(rows, -1)
        flat.append(a if rows == P else np.concatenate([a, np.zeros((P - rows, a.shape[1]), a.dtype)]))
    a = np.concatenate(flat, axis=1)
    return np.concatenate([a, np.zeros((P, UNIT - a.shape[1]), a.dtype)], axis=1)


def _columns(a):
    return a.reshape(a.shape[0] // P, P, -1).transpose(1, 0, 2).reshape(P, -1)


def _lay_units(i):
    wk, wv = i["L0_xattn_Wkv"][:, :INNER].T, i["L0_xattn_Wkv"][:, INNER:]
    att = np.concatenate([i["L0_attn_Wq"], i["L0_attn_Wk"], i["L0_attn_Wv"]]).T
    inw = i["L1_attn_in_w"].T
    u = {"wq": [(i["L0_xattn_Wq"], P)], "wk0": [(wk[:512], P)], "wk1": [(wk[512:], P)],
         "wv0": [(wv[:256], P)], "wv1": [(wv[256:], P)], "wout": [(i["L0_xattn_Wout"], P)],
         "att": [(att, P), (i["L0_attn_Wo"].T, P)],
         "f1b": [(i["L0_ffn_W1"].T, P)], "f2b": [(i["L0_ffn_W2"].T, P)],
         "xat": [(i["L1_xattn_w_qkv"].T, P), (i["L1_xattn_w_proj"].T, P)],
         "mb1": [(inw[:, DIN:DIN + CONV], P), (inw[:, DIN + CONV:], P)],
         "mb2": [(inw[:, :DIN], P), (i["L1_attn_out_w"].T, P)],
         "mb3": [(i["L1_attn_scorer_w1"].T, P), (i["L1_attn_summ_w"].T, P), (i["L1_attn_q_w"].T, P),
                 (i["L1_attn_k_w"].T, SD), (i["L1_attn_v_w"].T, SD), (i["L1_attn_gate_w"].T, P)]}
    for e in range(E):
        u[f"f1e{e}"] = [(i["L0_ffn_TW1"][e].T, P)]
        u[f"f2e{e}"] = [(i["L0_ffn_TW2"][e].T, P)]
        u[f"m1e{e}"] = [(i["L1_ffn_W1"][e], P)]
        u[f"m2e{e}"] = [(i["L1_ffn_W2"][e], P)]
    return np.stack([_unit(*u[name]) for name in UNITS])


def _lay_constants():
    t = np.arange(P)
    same = (t[:, None] // NQ == t[None, :] // NQ)
    causal = same & (t[:, None] <= t[None, :])
    c = {"ident": np.eye(P), "ones": np.ones((P, P)), "same": same, "causal": causal,
         "tie": same & (t[:, None] < t[None, :]), "neg": np.where(causal, 0.0, -1e30),
         "hmask": np.where(t[:, None] // DH1 == np.arange(8)[None, :], DH1 ** -0.5, 0.0),
         "neghalf": np.full((P, 1), -0.5), "dec": np.tile(np.arange(E, 0, -1), (P, 1))}
    return np.concatenate([np.asarray(c[name], np.float32) for name in CONST], axis=1)


def kernel(**inputs):
    import concourse.bacc as bacc
    from concourse.bass_utils import run_bass_kernel_spmd as run

    i = {name: np.asarray(a) for name, a in inputs.items()}
    nk = i["L0_xattn_null_kv"][0][:, None]
    c = {"gate_b1": _columns(i["L0_ffn_gate_b1"]), "conv_w": _columns(i["L1_attn_conv_w"]),
         "conv_b": _columns(i["L1_attn_conv_b"]), "nk": np.concatenate([nk, nk]),
         "gw2": _columns(i["L0_ffn_gate_w2"].T), "wr": _columns(i["L1_ffn_Wr"])}
    v = {"ln_scale": i["L0_xattn_ln_scale"], "ln_bias": i["L0_xattn_ln_bias"], "ln_g": i["L0_attn_ln_g"],
         "ln_b": i["L0_attn_ln_b"], "bo": i["L0_attn_bo"],
         "qk_gamma": np.concatenate([i["L0_attn_q_gamma"], i["L0_attn_k_gamma"]]), "gate_b2": i["L0_ffn_gate_b2"],
         "nv": i["L0_xattn_null_kv"][1], "b_proj": i["L1_xattn_b_proj"], "norm_w": i["L1_attn_norm_w"],
         "gnorm_w": i["L1_attn_gnorm_w"], "dt_bias": i["L1_attn_dt_bias"], "A_log": i["L1_attn_A_log"],
         "D_param": i["L1_attn_D_param"], "sw2": i["L1_attn_scorer_w2"][0], "br": i["L1_ffn_br"]}
    biases = np.concatenate([
        np.concatenate([i["L0_ffn_Tb1"], i["L0_ffn_b1"][None]]), i["L1_ffn_b1"]])
    biases2 = np.concatenate([np.concatenate([i["L0_ffn_Tb2"], i["L0_ffn_b2"][None]]), i["L1_ffn_b2"]])
    arrays = {
        "x": i["x"].reshape(TOK, DIM),
        "ctx": i["ctx_2048"],
        "ctxT": i["ctx_2048"].transpose(0, 2, 1),
        "units": _lay_units(i),
        "constants": _lay_constants(),
        "columns": np.concatenate([c[name] for name in COLS], axis=1),
        "vectors": np.concatenate([v[name] for name in VECS]),
        "bias_rows_in": np.concatenate([biases, biases2], axis=1),
        "gate_w1": _columns(i["L0_ffn_gate_w1"].T).reshape(P, KT, DIM),
    }
    arrays = {name + "_dram": np.ascontiguousarray(a) for name, a in arrays.items()}
    nc = bacc.Bacc("TRN2", target_bir_lowering=False, num_devices=1)
    args = [nc.dram_tensor(name, a.shape, mybir.dt.from_np(a.dtype), kind="ExternalInput").ap()
            for name, a in arrays.items()]
    result = nc.dram_tensor("result_dram", (TOK, DIM), F32, kind="ExternalOutput").ap()
    perceiver_kernel(nc, *args, result)
    r = run(nc, [arrays], core_ids=[0])
    return r.results[0]["result_dram"].reshape(B, NQ, DIM)
```

```python
from contextlib import ExitStack

import concourse.bass as bass
import numpy as np
from concourse import mybir

ALU = mybir.AluOpType
ACT = mybir.ActivationFunctionType
F32 = mybir.dt.float32
F32R = mybir.dt.float32r
AX_X = mybir.AxisListType.X

P = 128
B, NQ, DIM = 2, 64, 256
TOK = B * NQ
NCTX, CTX = 1024, 512
KT = DIM // P
CT = CTX // P
KEYT = NCTX // P
H0, DH0 = 16, 64
INNER = H0 * DH0
PAIRS = H0 // 2
HA = 4
F, E = 1024, 8
FT = F // P
H1, DH1 = 16, 16
DIN, DST, NH, HD = 512, 128, 8, 64
CONV, TAPS = DIN + 2 * DST, 4
CHT = CONV // P
PAD = NQ + TAPS - 1
POOL, SD, RETDIM = 50, 64, 16
UNIT = 2048

UNITS = (["wq", "wk0", "wk1", "wv0", "wv1", "wout", "att", "f1b"] + [f"f1e{e}" for e in range(E)]
         + ["f2b"] + [f"f2e{e}" for e in range(E)] + ["xat", "mb1", "mb2", "mb3"]
         + [f"m1e{e}" for e in range(E)] + [f"m2e{e}" for e in range(E)])
RELEASE = {u: n + 1 for n, u in enumerate(UNITS)}
NR, NA, NB, NC = 4, 5, 4, 4

CONST = {}
COLS = {}
VECS = {}


def _lay(table, items):
    at = 0
    for name, n in items:
        table[name] = (at, at + n)
        at += n
    return at


NCONST = _lay(CONST, [("ident", P), ("ones", P), ("same", P), ("causal", P), ("tie", P), ("neg", P),
                      ("hmask", 8), ("neghalf", 1), ("dec", E), ("fold", NQ), ("headof", 2)])
NCOLS = _lay(COLS, [("gate_b1", KT), ("conv_w", CHT * TAPS), ("conv_b", CHT), ("nk", 1), ("gw2", KT * E),
                    ("wr", KT * E)])
NVECS = _lay(VECS, [("ln_scale", DIM), ("ln_bias", DIM), ("ln_g", DIM), ("ln_b", DIM), ("bo", DIM),
                    ("qk_gamma", 2 * DH0), ("gate_b2", E), ("nv", DH0), ("b_proj", DIM), ("norm_w", DIM),
                    ("gnorm_w", DIN), ("dt_bias", NH), ("A_log", NH), ("D_param", NH), ("sw2", SD), ("br", E)])
BIAS1, BIAS2 = (0, F), (F, F + DIM)
NROWS = F + DIM
N_RSQRT, RSQRT_QK = 11, 4
ROWT = B * PAIRS
GROUPS = ROWT // 2
CHUNKS, CHUNK = 16, 1024
TURN = PAIRS
SPLIT_AT = {0: (4, 5), 1: (6,), 2: (7,), TURN - 1: (8, 9), TURN: (12, 13), TURN + 1: (14,), TURN + 2: (15,)}
SPLIT_AT_Q = {(b, 2 * k + 1): n for b, first in ((0, 0), (1, 10)) for k, n in enumerate(range(first, 4 + 8 * b))}


def plan_places():
    last, plan = {}, []

    def put(unit, place, after=None):
        need = RELEASE[last[place]] if place in last else 0
        if after:
            need = max(need, RELEASE[after])
        last[place] = unit
        plan.append((unit, place, need))

    for unit, place in zip(UNITS[:7], (0, 1, 2, 3, 0, 1, 2)):
        put(unit, place)
    cycle = list(range(NR, NR + NA + NB)) + [3, 0, 1, 2]
    units = UNITS[UNITS.index("f1b"):]
    freed = units.index("xat") + 11
    for n, unit in enumerate(units[:freed]):
        place = cycle[n % len(cycle)]
        put(unit, place, after="wout" if n < len(cycle) and place >= NR else None)
    for n in range(NC):
        put(units[freed + n], NR + NA + NB + n, after="xat")
    for n, unit in enumerate(units[freed + NC:]):
        put(unit, cycle[(freed + n) % len(cycle)])
    return plan


PLAN = plan_places()
PLACE = {unit: place for unit, place, _ in PLAN}
LANDED = {unit: 16 * sum(1 for _, q, _ in PLAN[:n + 1] if q == place) for n, (unit, place, _) in enumerate(PLAN)}


def bc(ap, axis, n):
    shape = list(ap.shape)
    shape.insert(axis, n)
    return ap.unsqueeze(axis).to_broadcast(shape)


def cut(base, at, *free):
    n = 1
    for f in free:
        n *= f
    ap = base[:, at:at + n]
    if len(free) == 1:
        return ap
    axes = "abcd"[:len(free)]
    return ap.rearrange(f"p ({' '.join(axes)}) -> p {' '.join(axes)}", **dict(zip(axes, free)))


ONCE = {
    "tensor_made": [
        "null_ps", "out0_ps", "qkT_ps", "simA_ps", "ptA_ps", "pvA_ps", "outA_ps", "gh_ps", "g_ps",
        "qk1_ps", "v1_ps", "o1tok_ps", "out1_ps", "xbc_ps", "dt_ps", "z_ps", "decay_ps", "G_ps",
        "xs_ps", "ym_ps", "ygT_ps", "y_tok_ps", "sc_ps", "pq_ps", "km_ps", "vm_ps", "lg_ps",
        "scT_ps", "rank_ps", "pmT_ps", "ret_ps", "retT_ps", "gate_ps", "route_ps", "maskT_ps"],
    "scalar_made": [
        "sq_ready", "qkT_sb", "simA_exp", "ptA_sb", "gT_sb", "expA", "xbc_sbA", "dte",
        "conv_tanh", "z_tanh", "dtl", "ex_ready", "gm_ready", "ygT_sb", "pq_sb", "sct", "km_sb",
        "vm_sb", "pm_exp", "pmT_sb", "retT_sb", "gate_tanh", "rz", "maskT_sb"],
    "vector_made": [
        "null_sb", "nv_ready", "qk_ready", "simA_max", "probsA", "hm_ready", "k1_sb", "o1_ready", "xbc_sbV",
        "dtn_ready", "conv_done", "dtA_ready", "xs_act", "M_ready", "yg_ready", "scz", "scb_ready",
        "cmp_ready", "lmax", "pm_ready", "ret_sb", "mask_ready", "dm_ready", "rneg", "result"],
}


def perceiver_kernel(nc, x_in, ctx_in, ctxT_in, units_in, const_in, cols_in, vecs_in, rows_in, gate_in, out):
    with ExitStack() as stack:
        def sb(name, *free):
            return stack.enter_context(nc.sbuf_tensor(name, [P, *free], F32))

        names = {}

        def ev(name):
            if name not in names:
                names[name] = stack.enter_context(nc.semaphore(name))
            return names[name]

        ticked = {kind: [] for kind in ONCE}

        def made(name):
            kind = next(k for k, results in ONCE.items() if name in results)
            return ev(kind), ONCE[kind].index(name) + 1

        def tick(name):
            kind = next(k for k, results in ONCE.items() if name in results)
            ticked[kind].append(name)
            assert ticked[kind] == ONCE[kind][:len(ticked[kind])], "ONCE is not in the program's order"
            return ev(kind), 1

        with ExitStack() as pairs:
            def pair(name, *free):
                return [pairs.enter_context(nc.sbuf_tensor(name + half, [P, *free], F32R)) for half in ("_hi", "_lo")]

            CXT = pair("ctx_turned", CT, NCTX)
            CXN = pair("ctx_split", KEYT, CTX)
            QP = pair("q_keys", CT, PAIRS, P)
            PT = pair("probs_turned", KEYT, 2 * P)
        ctxmem = sb("ctxmem", (NB + NC) * UNIT)
        ctxT = cut(ctxmem, 0, B, KT, NCTX)
        ctxN = cut(ctxmem, B * KT * NCTX, B, KEYT, DIM)
        arena = sb("arena", 8 * UNIT)
        fixed = sb("fixed", NR * UNIT)
        pbuf = sb("pbuf", 4 * 1152)
        work = sb("work", PAIRS * TOK)
        const = sb("const", NCONST)
        cols = sb("cols", NCOLS)
        vecs = sb("vecs", NVECS)
        bias_rows = sb("bias_rows", NROWS)
        x = sb("x", DIM)
        hn = sb("hn", DIM)
        xn = sb("xn", DIM)
        xT = sb("xT", KT, TOK)
        vsb = sb("vsb", DIM)
        small = sb("small", 320)

        def c_(name):
            return const[:, CONST[name][0]:CONST[name][1]]

        def p_(name):
            return cols[:, COLS[name][0]:COLS[name][1]]

        def v_(name):
            return vecs[:, VECS[name][0]:VECS[name][1]]

        def unit(name):
            n = PLACE[name]
            if n < NR:
                return fixed[:, n * UNIT:(n + 1) * UNIT]
            if n < NR + NA:
                return arena[:, (n - NR) * UNIT:(n - NR + 1) * UNIT]
            n = (n - NR - NA + NC) % (NB + NC)
            return ctxmem[:, n * UNIT:(n + 1) * UNIT]

        ident = c_("ident")
        cw = p_("conv_w").rearrange("p (t k) -> p t k", t=CHT)
        W = [stack.enter_context(nc.psum_tensor(f"W{n}", [P, 1024], F32)) for n in range(4)]

        def bank(n):
            return W[n // 2][:, 512 * (n % 2):512 * (n % 2) + 512]

        st6, mv = cut(small, 0, 6), cut(small, 6, 2)
        ve, rstd = cut(small, 8, 1), cut(small, 9, 1)
        mx = cut(small, 10, 2)
        zs = cut(small, 12, 2)
        stat = cut(small, 16, ROWT, 2)
        null_s = cut(small, 48, B * PAIRS)
        negm = cut(small, 64, B * PAIRS)
        rinv0, w_null = cut(small, 80, ROWT), cut(small, 96, ROWT)
        ssq, rqk = cut(small, 112, 8), cut(small, 120, 8)
        smax, ssum, srec = cut(small, 128, 4), cut(small, 132, 4), cut(small, 136, 4)
        hmean = cut(small, 140, KT, B)
        gmix = cut(small, 144, B, E)
        gtok = cut(small, 160, E + 1)
        selfmax = cut(small, 176, B * PAIRS)
        z1 = cut(small, 192, B * PAIRS, 2)
        z1s, rinv1 = cut(small, 224, B * PAIRS), cut(small, 240, B * PAIRS)
        dta, dtm, dtn, dte = (cut(small, 256 + 8 * n, NH) for n in range(4))
        dt, expA, dtA, dtAn = (cut(small, 128 + 8 * n, NH) for n in range(4))
        dneg = cut(small, 160, NH)
        scz, sct, score, msum, mtrue, cnt, rm = (cut(small, 288 + n, 1) for n in range(7))
        ms, lmax, zsum, zrec = (cut(small, 296 + n, 1) for n in range(4))
        rl, req, mask = (cut(small, 176 + 8 * n, E) for n in range(3))
        rmax, rsel, rneg, rz, gate = (cut(small, 304 + n, 1) for n in range(5))

        top = arena[:, 6 * UNIT:]
        op = [cut(top, 1024 * n, CT, 4, NQ) for n in range(2)]
        oT0 = cut(top, 2048, PAIRS, TOK)
        probs0 = cut(pbuf, 0, 2, NCTX)
        stage = [cut(top, 3072, CHUNK), cut(pbuf, 2048, CHUNK)]
        QB = [cut(work, 0, PAIRS, P), cut(pbuf, 3072, PAIRS, P)]
        NVL = cut(vsb, 0, 2, DH0)
        DW = [cut(hn, P * n, 2, NQ) for n in range(2)]
        gatew = cut(pbuf, 4096, KT, DIM)
        scr = arena[:, NA * UNIT:]
        QK, QKT, PA = cut(scr, 0, 512), cut(scr, 512, 4, TOK), cut(scr, 1024, HA, TOK)
        SA, PTA, SQ = cut(scr, 1536, HA, NQ), cut(scr, 1792, HA, TOK), cut(scr, 2304, 512)
        XE = cut(scr, 0, E, KT, TOK)
        U, UT = cut(scr, 2048, F), cut(scr, 3072, FT, TOK)
        HG, HM, GT = cut(scr, 4096, KT, TOK), cut(scr, 4352, KT, B * E), cut(scr, 4400, TOK)
        DM, MASKT, ACC = cut(scr, 4096, E * TOK), cut(scr, 5120, TOK), cut(scr, 5248, DIM)
        QZ = cut(scr, 0, 2, B, 8, NQ)
        PT1 = [cut(scr, 2048 + 1152 * n, 9, TOK) for n in range(2)]
        SELF, O1, K1 = cut(scr, 4352, B, PAIRS, NQ), cut(scr, 5376, B, PAIRS, 2, DH1), cut(scr, 5888, 2, TOK)
        probs1 = cut(pbuf, 0, 4, 1152)
        Q1 = cut(work, 0, 2, TOK)
        XP, C1 = cut(scr, 0, CHT, B, PAD), cut(scr, 832, CHT, TOK)
        XC, TH = cut(scr, 1600, CHT, TOK), cut(scr, 2368, CHT * TOK)
        ZS, ZT, XS = cut(scr, 3136, DIN), cut(scr, 3648, DIN), cut(scr, 4160, DIN)
        DTX, Y2, GM = cut(scr, 4672, DIN), cut(scr, 5184, DIN), cut(scr, 5696, TOK)
        DX = cut(scr, 0, DIN)
        EX, MT = cut(pbuf, 0, NH, TOK), cut(pbuf, 1024, NH, TOK)
        YG, YGT = cut(pbuf, 2048, DIN), cut(pbuf, 2560, 4, TOK)
        PQ, KM, VM = cut(pbuf, 3072, 2, TOK), cut(pbuf, 3328, TOK), cut(pbuf, 3456, DIM)
        SCB, SCT, CMP, CMP2, KEEP, KEEPS = (cut(pbuf, 3712 + P * n, P) for n in range(6))
        LG, PEN, PM, PMT = (cut(work, P * n, P) for n in range(4))
        RET, RETT = cut(work, 512, DIM), cut(work, 768, KT, TOK)
        GTH, G1 = cut(scr, 832, DIM), cut(scr, 1088, DIM)

        uses67 = []
        for g in range(GROUPS):
            if 2 * g + 2 == TURN:
                uses67 += [("ql_sb", PAIRS + j) for j in range(PAIRS)]
            uses67 += [("op_sb", CT * g + c) for c in range(CT)] + [("oT_sb", g)]

        def bank67(kind, n):
            return bank(6 + uses67.index((kind, n)) % 2)

        def qp_bank(b, j):
            ps = bank(j % 4) if b == 0 else bank67("ql_sb", PAIRS + j)
            return ps.rearrange("p (c m) -> p c m", c=CT)

        def chunk_of(n, part):
            k = n % 4
            return CXT[part][:, k, :] if n % 8 < 4 else CXN[part][:, 2 * k:2 * k + 2, :]

        def stage_of(n):
            return stage[n % 2] if n % 8 < 4 else stage[n % 2].rearrange("p (t c) -> p t c", t=2)

        def f32(ap):
            return ap.bitcast(F32)

        block = stack.enter_context(nc.Block())

        @block.sync
        def _(sync):
            sync.dma_start(x[:, :], x_in).then_inc(ev("x_in"), 16)
            sync.dma_start(const[:, :], const_in).then_inc(ev("const_in"), 16)

            def load(n):
                name, place, used = PLAN[n]
                if used:
                    sync.wait_ge(ev("units_used"), used)
                sync.dma_start(unit(name), units_in[UNITS.index(name)]).then_inc(ev(f"place{place}"), 16)

            for n in range(3):
                load(n)
            sync.wait_ge(ev("ctx_lo"), 2)
            for n in range(3, len(PLAN)):
                load(n)
                if PLAN[n][0] == "f1e3":
                    for b in range(B):
                        sync.dma_start(ctxT[:, b], ctxT_in[b, 0:DIM].rearrange("(c p) k -> p c k", p=P))\
                            .then_inc(ev("ctxT_in"), 16)
                        sync.dma_start(ctxN[:, b], ctx_in[b, :, DIM:].rearrange("(t p) c -> p t c", p=P))\
                            .then_inc(ev("ctxN_in"), 16)
                if PLAN[n][0] == "xat":
                    sync.wait_ge(ev("y_ps"), 1)
                    sync.dma_start(bias_rows[0:E, :], rows_in[E + 1:2 * E + 1, :]).then_inc(ev("rows2_in"), 16)
            sync.wait_ge(*made("result"))
            sync.dma_start(out, xn[:, :]).then_inc(ev("stored"), 16)
            sync.wait_ge(ev("stored"), 16)

        @block.gpsimd
        def _(pool):
            def load_chunk(n):
                b, k = n // 8, n % 4
                if n >= 2:
                    pool.wait_ge(ev("ctx_lo"), n - 1)
                if n % 8 < 4:
                    pool.dma_start(stage[n % 2], ctxT_in[b, k * P:(k + 1) * P]).then_inc(ev(f"chunk{n % 2}"), 16)
                else:
                    pool.dma_start(stage[n % 2].rearrange("p (t c) -> p t c", t=2),
                                   ctx_in[b, 2 * k * P:2 * (k + 1) * P].rearrange("(t p) c -> p t c", p=P))\
                        .then_inc(ev(f"chunk{n % 2}"), 16)

            load_chunk(0)
            pool.wait_ge(ev("const_in"), 16)
            for n in range(N_RSQRT):
                pool.wait_ge(ev("var_ready"), n + 1)
                src, dst, wide = (ssq, rqk, 8) if n == RSQRT_QK else (ve, rstd, 1)
                pool.tensor_tensor(dst, src, c_("neghalf").to_broadcast([P, wide]), ALU.pow)\
                    .then_inc(ev("rstd_ready"), 1)
                if n == 0:
                    for k in range(1, CHUNKS):
                        load_chunk(k)
                        if k == 1:
                            pool.dma_start(cols[:, :], cols_in).then_inc(ev("cols_in"), 16)
                        if k == 7:
                            pool.dma_start(vecs[:, :], vecs_in.partition_broadcast(P)).then_inc(ev("vecs_in"), 16)
                            pool.dma_start(bias_rows[0:E + 1, :], rows_in[0:E + 1, :]).then_inc(ev("rows_in"), 16)
                            pool.dma_start(gatew, gate_in).then_inc(ev("gatew_in"), 16)
                if n == 1:
                    pool.memset(PA, 0.0).then_inc(ev("pa_zero"), 1)
                if n == 6:
                    for m in range(4):
                        pool.memset(probs1[:, m, NCTX + NQ * (1 - m % 2):NCTX + NQ * (2 - m % 2)], 0.0)\
                            .then_inc(ev("pads_zero"), 1)
                if n == 7:
                    pool.memset(XP[:, :, :, 0:TAPS - 1], 0.0).then_inc(ev("xp_zero"), 1)

        @block.scalar
        def _(act):
            turned = [0]

            def keep_xT(ps):
                turned[0] += 1
                act.wait_ge(ev("xT_ps"), turned[0])
                act.copy(xT[:, :, :], ps[:, 0:DIM].rearrange("p (k t) -> p k t", k=KT)).then_inc(ev("xT_sb"), 1)

            def hidden(n, func):
                for hf in range(2):
                    act.wait_ge(ev("pre_ps"), 2 * n + hf + 1)
                    act.activation(U[:, hf * 512:(hf + 1) * 512], bank(4 + hf), func).then_inc(ev("u_ready"), 1)

            keep_xT(bank(4))
            act.wait_ge(ev("qT_ps"), 1)
            act.wait_ge(ev("qb_zero"), B)
            for b in range(B):
                act.mul(QB[b][0:DH0, :, 0:NQ], W[3][0:DH0].rearrange("p (j t) -> p j t", j=PAIRS)[:, :, b * NQ:(b + 1) * NQ],
                        DH0 ** -0.5).then_inc(ev("q_sbA"), 1)

            def keep_hi(n):
                act.wait_ge(ev(f"chunk{n % 2}"), 16 * (n // 2 + 1))
                if n == 8:
                    act.wait_ge(ev("sim_done"), TURN)
                if n == 12:
                    act.wait_ge(ev("op_ps"), CT * GROUPS // 2)
                act.copy(chunk_of(n, 0), stage_of(n)).then_inc(ev("ctx_hi"), 1)

            def keep_q_hi(b):
                if b:
                    act.wait_ge(ev("sim_done"), TURN)
                for j in range(PAIRS):
                    act.wait_ge(ev("qp_ps"), b * PAIRS + j + 1)
                    act.copy(QP[0][:, :, j, :], qp_bank(b, j)).then_inc(ev("qh_sb"), 1)
                    if (b, j) in SPLIT_AT_Q:
                        keep_hi(SPLIT_AT_Q[b, j])

            def keep_probs_hi(r):
                for c in range(2):
                    act.wait_ge(ev("pt_ps"), 2 * r + c + 1)
                    act.copy(PT[0][:, 4 * c:4 * c + 4, (r % 2) * P:(r % 2 + 1) * P],
                             bank(4 + c).rearrange("p (t m) -> p t m", t=4)).then_inc(ev("ph_sb"), 1)

            def keep_op(g):
                for c in range(CT):
                    act.wait_ge(ev("op_ps"), CT * g + c + 1)
                    if g >= 2 and c == 0:
                        act.wait_ge(ev("oT_ps"), g - 1)
                    act.copy(op[g % 2][:, c], bank67("op_sb", CT * g + c)[:, 0:2 * P].rearrange("p (h q) -> p h q", h=4))\
                        .then_inc(ev("op_sb"), 1)

            def softmax0(r):
                for n in SPLIT_AT.get(r, ()):
                    keep_hi(n)
                act.wait_ge(ev("negm_ready"), r + 1)
                if r >= 2:
                    act.wait_ge(ev("pt_ps"), 2 * (r - 1))
                act.activation(probs0[:, r % 2, :], W[r % 2][:, :], ACT.Exp, bias=negm[:, r:r + 1],
                               accum_out=stat[:, r, 1:2]).then_inc(ev("exp_done"), 1)
                act.activation(stat[:, r, 0:1], null_s[:, r:r + 1], ACT.Exp, bias=negm[:, r:r + 1])\
                    .then_inc(ev("p0_done"), 1)
                act.wait_ge(ev("rinv_ready"), r + 1)
                act.mul(probs0[:, r % 2, :], probs0[:, r % 2, :], rinv0[:, r:r + 1]).then_inc(ev("probs_ready"), 1)

            keep_q_hi(0)
            act.wait_ge(*made("null_sb"))
            for r in range(ROWT + 1):
                if r == TURN:
                    keep_probs_hi(r - 1)
                    keep_q_hi(1)
                    keep_op(r // 2 - 1)
                if r < ROWT:
                    softmax0(r)
                if r == TURN:
                    continue
                if r % 2 == 1 and r >= 3 and r != TURN + 1:
                    keep_op((r - 3) // 2)
                if r >= 1:
                    keep_probs_hi(r - 1)
            keep_op(GROUPS - 1)

            keep_xT(bank(1))
            act.wait_ge(ev("qkv_ps"), 1)
            act.activation(SQ, bank(2), ACT.Square).then_inc(*tick("sq_ready"))
            act.wait_ge(ev("qkv_ps"), 2)
            act.copy(vsb[:, :], bank(3)[:, 0:DIM]).then_inc(ev("v_sb"), 1)
            act.wait_ge(*made("qkT_ps"))
            act.copy(QKT, bank(4).rearrange("p (t m) -> p t m", t=4)).then_inc(*tick("qkT_sb"))
            act.wait_ge(*made("simA_max"))
            act.activation(SA, SA, ACT.Exp, scale=DH0 ** -0.5).then_inc(*tick("simA_exp"))
            act.wait_ge(*made("ptA_ps"))
            act.copy(PTA, bank(7).rearrange("p (t m) -> p t m", t=4)).then_inc(*tick("ptA_sb"))
            keep_xT(bank(1))

            keep_xT(bank(0))
            act.wait_ge(*made("gh_ps"))
            act.wait_ge(ev("cols_in"), 16)
            for o in range(KT):
                act.activation(HG[:, o, :], bank(1)[:, o * P:(o + 1) * P], ACT.Relu, bias=p_("gate_b1")[:, o:o + 1])\
                    .then_inc(ev("hg_ready"), 1)
            act.wait_ge(ev("gT_ps"), 1)
            act.copy(GT[0:E + 1, :], bank(3)[0:E + 1, 0:TOK]).then_inc(*tick("gT_sb"))
            hidden(0, ACT.Gelu_apprx_tanh)

            keep_xT(bank(4))
            act.wait_ge(*made("v1_ps"))
            act.copy(vsb[:, :], bank(6)[:, 0:DIM]).then_inc(ev("v_sb"), 1)
            act.wait_ge(ev("self_ps"), 1)
            act.copy(SELF[:, 0], bank(4).rearrange("p (j q) -> p j q", j=PAIRS)).then_inc(ev("self_sb"), 1)
            act.wait_ge(ev("pads_zero"), 4)
            for r in range(ROWT + 2):
                if r >= 2:
                    q = r - 2
                    for n, (t, bk) in enumerate(((0, 4), (6, 7))):
                        act.wait_ge(ev("pt1_ps"), 3 * q + (1, 3)[n])
                        if q >= 2:
                            act.wait_ge(ev("pv1_ps"), q - 1)
                        act.copy(PT1[q % 2][:, t:t + 3, :], bank(bk)[:, 0:3 * P].rearrange("p (t m) -> p t m", t=3))\
                            .then_inc(ev("pt1_sbA"), 1)
                if r < ROWT:
                    b, j = r % 2, r // 2
                    m = b * PAIRS + j
                    act.wait_ge(ev("negm1_ready"), r + 1)
                    if r >= 4:
                        act.wait_ge(ev("pt1_ps"), 3 * (r - 3))
                    act.activation(probs1[:, r % 4, 0:NCTX], W[r % 2][:, :], ACT.Exp, bias=negm[:, m:m + 1],
                                   accum_out=z1[:, m, 0:1]).then_inc(ev("exp1_ctx"), 1)
                    act.activation(probs1[:, r % 4, NCTX + NQ * b:NCTX + NQ * (b + 1)], SELF[:, b, j, :], ACT.Exp,
                                   bias=negm[:, m:m + 1], accum_out=z1[:, m, 1:2]).then_inc(ev("exp1_done"), 1)
            keep_xT(bank(4))

            act.activation(expA, v_("A_log"), ACT.Exp).then_inc(*tick("expA"))
            keep_xT(bank(0))
            act.wait_ge(*made("xbc_ps"))
            act.copy(XP[:, 4:6, :, TAPS - 1:], bank(3)[:, 0:2 * TOK].rearrange("p (t b q) -> p t b q", t=2, b=B))\
                .then_inc(*tick("xbc_sbA"))
            act.wait_ge(*made("xbc_sbA"))
            act.wait_ge(*made("xbc_sbV"))
            for t in range(CHT):
                act.activation(C1[:, t, :].rearrange("p (b q) -> p b q", b=B), XP[:, t, :, TAPS - 1:], ACT.Identity,
                               bias=p_("conv_b")[:, t:t + 1], scale=cw[:, t, TAPS - 1:TAPS]).then_inc(ev("tap3"), 1)
            act.wait_ge(*made("dtn_ready"))
            act.activation(dte, dtn, ACT.Exp).then_inc(*tick("dte"))
            act.wait_ge(*made("conv_done"))
            act.activation(TH, C1.rearrange("p t m -> p (t m)"), ACT.Tanh, scale=0.5).then_inc(*tick("conv_tanh"))
            act.wait_ge(*made("z_ps"))
            act.activation(ZT, bank(4), ACT.Tanh, scale=0.5).then_inc(*tick("z_tanh"))
            act.wait_ge(*made("dte"))
            act.activation(dte, dte, ACT.Ln, bias=1.0).then_inc(*tick("dtl"))
            act.wait_ge(*made("decay_ps"))
            act.activation(EX, W[1][:, :].rearrange("p (h t) -> p h t", h=NH), ACT.Exp).then_inc(*tick("ex_ready"))
            act.wait_ge(*made("G_ps"))
            act.mul(GM, bank(6)[:, 0:TOK], 0.25).then_inc(*tick("gm_ready"))
            act.wait_ge(*made("ygT_ps"))
            act.copy(YGT, bank(0).rearrange("p (t m) -> p t m", t=4)).then_inc(*tick("ygT_sb"))
            keep_xT(bank(0))
            act.wait_ge(*made("pq_ps"))
            act.copy(PQ[0:SD], bank(2)[0:SD, 0:2 * TOK].rearrange("p (n t) -> p n t", n=2)).then_inc(*tick("pq_sb"))
            act.wait_ge(*made("scz"))
            act.activation(sct, scz, ACT.Tanh, scale=0.5).then_inc(*tick("sct"))
            act.wait_ge(*made("km_ps"))
            act.copy(KM[0:SD, :], bank(3)[0:SD, 0:TOK]).then_inc(*tick("km_sb"))
            act.wait_ge(*made("vm_ps"))
            act.copy(VM, bank(4)[:, 0:DIM]).then_inc(*tick("vm_sb"))
            act.wait_ge(*made("lmax"))
            act.activation(PM, LG, ACT.Exp, bias=lmax, accum_out=zsum).then_inc(*tick("pm_exp"))
            act.wait_ge(*made("pmT_ps"))
            act.copy(PMT, bank(0)[:, 0:P]).then_inc(*tick("pmT_sb"))
            act.wait_ge(*made("retT_ps"))
            act.copy(RETT, bank(3)[:, 0:DIM].rearrange("p (k t) -> p k t", k=KT)).then_inc(*tick("retT_sb"))
            act.wait_ge(*made("gate_ps"))
            act.activation(GTH, bank(6)[:, 0:DIM], ACT.Tanh, scale=0.5).then_inc(*tick("gate_tanh"))

            keep_xT(bank(0))
            act.wait_ge(*made("rneg"))
            act.activation(rl, rl, ACT.Exp, bias=rneg, accum_out=rz).then_inc(*tick("rz"))
            act.wait_ge(*made("maskT_ps"))
            act.copy(MASKT[0:E, :], bank(0)[0:E, 0:TOK]).then_inc(*tick("maskT_sb"))
            for hf in range(2):
                act.wait_ge(ev("xm_ps"), 2 * hf + 1)
                act.copy(XE[:, 4 * hf:4 * hf + 4, 0, :], bank((1, 2)[hf]).rearrange("p (e t) -> p e t", e=4))\
                    .then_inc(ev("xm_sbA"), 1)
            hidden(1, ACT.Gelu)

        @block.vector
        def _(dve):
            steps, asked, given = [0], [0], [0]

            def step(ins):
                steps[0] += 1
                ins.then_inc(ev("vector_step"), 1)
                dve.wait_ge(ev("vector_step"), steps[0])

            def rsqrt(ins):
                asked[0] += 1
                ins.then_inc(ev("var_ready"), 1)
                dve.wait_ge(ev("rstd_ready"), asked[0])

            def norm(src, dst, eps):
                step(dve.bn_stats(st6, src))
                step(dve.bn_aggr(mv, st6))
                rsqrt(dve.tensor_scalar(ve, mv[:, 1:2], eps, None, ALU.add))
                return dve.tensor_scalar(dst, src, mv[:, 0:1], rstd, ALU.subtract, ALU.mult)

            def give(ins):
                given[0] += 1
                ins.then_inc(ev("xn_ready"), 1)

            def use_hidden(n):
                for hf in range(2):
                    dve.wait_ge(ev("uT_ps"), 2 * n + hf + 1)
                    dve.tensor_copy(UT[:, 4 * hf:4 * hf + 4, :], bank(6 + hf).rearrange("p (t m) -> p t m", t=4))\
                        .then_inc(ev("uT_sb"), 1)

            for b in range(B):
                dve.memset(QB[b], 0.0).then_inc(ev("qb_zero"), 1)
            dve.wait_ge(ev("x_in"), 16)
            give(norm(x[:, :], xn[:, :], 1e-5))
            dve.wait_ge(ev("qT_ps"), 1)
            dve.wait_ge(ev("qb_zero"), B)
            for b in range(B):
                dve.tensor_scalar(QB[b][DH0:P, :, NQ:P],
                                  W[3][DH0:P].rearrange("p (j t) -> p j t", j=PAIRS)[:, :, b * NQ:(b + 1) * NQ],
                                  DH0 ** -0.5, None, ALU.mult).then_inc(ev("q_sbV"), 1)

            def keep_lo(n):
                dve.wait_ge(ev("ctx_hi"), n + 1)
                dve.tensor_tensor(chunk_of(n, 1), stage_of(n), f32(chunk_of(n, 0)), ALU.subtract)\
                    .then_inc(ev("ctx_lo"), 1)

            def keep_q_lo(b):
                for j in range(PAIRS):
                    dve.wait_ge(ev("qh_sb"), b * PAIRS + j + 1)
                    dve.tensor_tensor(QP[1][:, :, j, :], qp_bank(b, j), f32(QP[0][:, :, j, :]), ALU.subtract)\
                        .then_inc(ev("ql_sb"), 1)
                    if (b, j) in SPLIT_AT_Q:
                        keep_lo(SPLIT_AT_Q[b, j])

            def keep_probs_lo(r):
                for c in range(2):
                    dve.wait_ge(ev("ph_sb"), 2 * r + c + 1)
                    at = (slice(None), slice(4 * c, 4 * c + 4), slice((r % 2) * P, (r % 2 + 1) * P))
                    dve.tensor_tensor(PT[1][at], bank(4 + c).rearrange("p (t m) -> p t m", t=4), f32(PT[0][at]),
                                      ALU.subtract).then_inc(ev("pl_sb"), 1)

            def keep_heads(g):
                dve.wait_ge(ev("oT_ps"), g + 1)
                b, j = g // (GROUPS // B), 2 * (g % (GROUPS // B))
                dve.tensor_copy(oT0[:, j:j + 2, b * NQ:(b + 1) * NQ],
                                bank67("oT_sb", g)[:, 0:P].rearrange("p (j q) -> p j q", j=2)).then_inc(ev("oT_sb"), 1)

            def softmax0(r):
                dve.wait_ge(ev("sim_done"), r + 1)
                step(dve.tensor_reduce(mx[:, r % 2:r % 2 + 1], W[r % 2][:, :], AX_X, ALU.max))
                dve.tensor_scalar(negm[:, r:r + 1], mx[:, r % 2:r % 2 + 1], null_s[:, r:r + 1], -1.0, ALU.max, ALU.mult)\
                    .then_inc(ev("negm_ready"), 1)
                for n in SPLIT_AT.get(r, ()):
                    keep_lo(n)
                dve.wait_ge(ev("p0_done"), r + 1)
                z = zs[:, r % 2:r % 2 + 1]
                step(dve.tensor_tensor(z, stat[:, r, 0:1], stat[:, r, 1:2], ALU.add))
                dve.reciprocal(rinv0[:, r:r + 1], z).then_inc(ev("rinv_ready"), 1)

            def null_probs(g):
                dve.wait_ge(ev("rinv_ready"), 2 * g + 2)
                step(dve.tensor_tensor(w_null[:, 2 * g:2 * g + 2], stat[:, 2 * g:2 * g + 2, 0], rinv0[:, 2 * g:2 * g + 2],
                                       ALU.mult))
                if g >= 2:
                    dve.wait_ge(ev("oT_ps"), g - 1)
                dve.tensor_tensor(DW[g % 2], bc(c_("fold"), 1, 2), bc(w_null[:, 2 * g:2 * g + 2], 2, NQ), ALU.mult)\
                    .then_inc(ev("dw_ready"), 1)

            keep_q_lo(0)
            dve.wait_ge(*made("null_ps"))
            dve.tensor_copy(null_s, bank(5)[:, 0:ROWT]).then_inc(*tick("null_sb"))
            dve.wait_ge(*made("null_sb"))
            for r in range(ROWT + 1):
                if r == TURN:
                    keep_heads(r // 2 - 2)
                    keep_probs_lo(r - 1)
                    keep_q_lo(1)
                if r < ROWT:
                    softmax0(r)
                if r == TURN:
                    continue
                if r == 2:
                    dve.wait_ge(ev("vecs_in"), 16)
                    dve.tensor_tensor(NVL, bc(v_("nv"), 1, 2), bc(c_("headof"), 2, DH0), ALU.mult).then_inc(*tick("nv_ready"))
                    step(dve.tensor_tensor(x[:, :], x[:, :], v_("ln_bias"), ALU.add))
                if r % 2 == 1:
                    null_probs(r // 2)
                if r % 2 == 0 and r >= 4:
                    keep_heads(r // 2 - 2)
                if r >= 1:
                    keep_probs_lo(r - 1)
            keep_heads(GROUPS - 1)
            dve.wait_ge(*made("out0_ps"))
            step(norm(bank(0)[:, 0:DIM], xn[:, :], 1e-6))
            step(dve.tensor_tensor(xn[:, :], xn[:, :], v_("ln_scale"), ALU.mult))
            step(dve.tensor_tensor(x[:, :], x[:, :], xn[:, :], ALU.add))

            step(norm(x[:, :], hn[:, :], 1e-5))
            step(norm(hn[:, :], xn[:, :], 1e-5))
            step(dve.tensor_tensor(xn[:, :], xn[:, :], v_("ln_g"), ALU.mult))
            give(dve.tensor_tensor(xn[:, :], xn[:, :], v_("ln_b"), ALU.add))
            step(dve.tensor_tensor(x[:, :], x[:, :], v_("bo"), ALU.add))
            dve.wait_ge(*made("sq_ready"))
            step(dve.tensor_reduce(ssq, SQ.rearrange("p (h d) -> p h d", h=8), AX_X, ALU.add))
            rsqrt(dve.tensor_scalar(ssq, ssq, 1.0 / DH0, 1e-16, ALU.mult, ALU.max))
            step(dve.tensor_tensor(QK.rearrange("p (h d) -> p h d", h=8), bank(2).rearrange("p (h d) -> p h d", h=8),
                                   bc(rqk, 2, DH0), ALU.mult))
            qk4 = QK.rearrange("p (n h d) -> p n h d", n=2, h=HA)
            dve.tensor_tensor(qk4, qk4, bc(v_("qk_gamma").rearrange("p (n d) -> p n d", n=2), 2, HA), ALU.mult)\
                .then_inc(*tick("qk_ready"))
            dve.wait_ge(*made("simA_ps"))
            sa4 = SA.rearrange("p (i m) q -> p i m q", m=2)
            for b in range(B):
                for m in range(2):
                    ins = dve.tensor_copy(sa4[b * NQ:(b + 1) * NQ, :, m, :],
                                          bank(5 + m)[b * NQ:(b + 1) * NQ, 0:2 * TOK]
                                          .rearrange("p (i t) -> p i t", i=2)[:, :, b * NQ:(b + 1) * NQ])
            step(ins)
            step(dve.tensor_reduce(smax, SA, AX_X, ALU.max))
            dve.tensor_tensor(SA, SA, bc(smax, 2, NQ), ALU.subtract).then_inc(*tick("simA_max"))
            dve.wait_ge(*made("simA_exp"))
            step(dve.tensor_reduce(ssum, SA, AX_X, ALU.add))
            step(dve.reciprocal(srec, ssum))
            dve.wait_ge(ev("pa_zero"), 1)
            for b in range(B):
                lo, hi = b * NQ, (b + 1) * NQ
                ins = dve.tensor_tensor(PA[lo:hi, :, lo:hi], SA[lo:hi], bc(srec[lo:hi], 2, NQ), ALU.mult)
            ins.then_inc(*tick("probsA"))
            dve.wait_ge(*made("pvA_ps"))
            give(dve.tensor_copy(xn[:, :], bank(0)[:, 0:DIM]))
            dve.wait_ge(*made("outA_ps"))
            step(dve.tensor_tensor(x[:, :], bank(2)[:, 0:DIM], x[:, :], ALU.add))

            give(norm(x[:, :], hn[:, :], 1e-5))
            dve.wait_ge(ev("hg_ready"), 2)
            step(dve.tensor_reduce(hmean, HG.rearrange("p k (b s) -> p k b s", b=B), AX_X, ALU.add))
            dve.wait_ge(ev("cols_in"), 16)
            dve.tensor_tensor(HM.rearrange("p k (b e) -> p k b e", b=B),
                              bc(p_("gw2").rearrange("p (k e) -> p k e", k=KT), 2, B), bc(hmean, 3, E), ALU.mult)\
                .then_inc(*tick("hm_ready"))
            dve.wait_ge(*made("g_ps"))
            step(dve.scalar_tensor_tensor(out=gmix, in0=bank(2)[:, 0:B * E].rearrange("p (b e) -> p b e", b=B),
                                          scalar=1.0 / NQ, in1=bc(v_("gate_b2"), 1, B), op0=ALU.mult, op1=ALU.add))
            dve.tensor_copy(gtok[0:NQ, 0:E], gmix[0:NQ, 0, :]).then_inc(ev("gtok_ready"), 1)
            dve.tensor_copy(gtok[NQ:P, 0:E], gmix[NQ:P, 1, :]).then_inc(ev("gtok_ready"), 1)
            dve.tensor_copy(gtok[:, E:E + 1], c_("ones")[:, 0:1]).then_inc(ev("gtok_ready"), 1)
            for e in range(E):
                dve.tensor_tensor(XE[:, e].rearrange("p k (b s) -> p k b s", b=B),
                                  xT[:, :, :].rearrange("p k (b s) -> p k b s", b=B),
                                  bc(bc(gmix[:, :, e], 1, KT), 3, NQ), ALU.mult).then_inc(ev("xe_ready"), 1)
            use_hidden(0)
            for n in range(E + 1):
                dve.wait_ge(ev("y_ps"), n + 1)
                if n == 0:
                    dve.tensor_tensor(x[:, :], bank(0)[:, 0:DIM], x[:, :], ALU.add).then_inc(ev("y_used"), 1)
                else:
                    dve.scalar_tensor_tensor(out=x[:, :], in0=bank(n % 4)[:, 0:DIM], scalar=gtok[:, n - 1:n],
                                             in1=x[:, :], op0=ALU.mult, op1=ALU.add).then_inc(ev("y_used"), 1)
                dve.wait_ge(ev("y_used"), n + 1)

            give(norm(x[:, :], hn[:, :], 1e-5))
            step(dve.tensor_tensor(x[:, :], x[:, :], v_("b_proj"), ALU.add))
            dve.wait_ge(*made("qk1_ps"))
            step(dve.tensor_copy(Q1, bank(5)[:, 0:2 * TOK].rearrange("p (i t) -> p i t", i=2)))
            dve.tensor_copy(K1, bank(5)[:, 2 * TOK:].rearrange("p (i t) -> p i t", i=2)).then_inc(*tick("k1_sb"))
            for i in range(2):
                for b in range(B):
                    dve.tensor_tensor(QZ[:, i, b], bc(Q1[:, i, b * NQ:(b + 1) * NQ], 1, 8), bc(c_("hmask"), 2, NQ),
                                      ALU.mult).then_inc(ev("qz_ready"), 1)
            dve.wait_ge(ev("self_ps"), 2)
            dve.tensor_copy(SELF[:, 1], bank(7).rearrange("p (j q) -> p j q", j=PAIRS)).then_inc(ev("self_sb"), 1)
            dve.wait_ge(ev("self_sb"), 2)
            step(dve.tensor_reduce(selfmax, SELF.rearrange("p b j q -> p (b j) q"), AX_X, ALU.max))
            for r in range(ROWT + 2):
                if r < ROWT:
                    m = (r % 2) * PAIRS + r // 2
                    dve.wait_ge(ev("sim1_done"), r + 1)
                    step(dve.tensor_reduce(mx[:, r % 2:r % 2 + 1], W[r % 2][:, :], AX_X, ALU.max))
                    dve.tensor_scalar(negm[:, m:m + 1], mx[:, r % 2:r % 2 + 1], selfmax[:, m:m + 1], -1.0, ALU.max, ALU.mult)\
                        .then_inc(ev("negm1_ready"), 1)
                if r >= 2:
                    q = r - 2
                    dve.wait_ge(ev("pt1_ps"), 3 * q + 2)
                    if q >= 2:
                        dve.wait_ge(ev("pv1_ps"), q - 1)
                    dve.tensor_copy(PT1[q % 2][:, 3:6, :], bank(5)[:, 0:3 * P].rearrange("p (t m) -> p t m", t=3))\
                        .then_inc(ev("pt1_sbV"), 1)
            dve.wait_ge(ev("exp1_done"), ROWT)
            step(dve.tensor_tensor(z1s, z1[:, :, 0], z1[:, :, 1], ALU.add))
            step(dve.reciprocal(rinv1, z1s))
            dve.wait_ge(ev("pv1_ps"), ROWT)
            dve.tensor_tensor(O1.rearrange("p b j h d -> p (b j) (h d)"), bank(6).rearrange("p (m n) -> p m n", m=ROWT),
                              bc(rinv1, 2, 2 * DH1), ALU.mult).then_inc(*tick("o1_ready"))
            dve.wait_ge(*made("o1tok_ps"))
            give(dve.tensor_copy(xn[:, :], bank(0)[:, 0:DIM]))
            dve.wait_ge(*made("out1_ps"))
            step(dve.tensor_tensor(x[:, :], bank(1)[:, 0:DIM], x[:, :], ALU.add))

            step(norm(x[:, :], hn[:, :], 1e-5))
            step(dve.tensor_tensor_reduce(out=xn[:, :], in0=hn[:, :], in1=hn[:, :], scale=1.0, scalar=0.0,
                                          op0=ALU.mult, op1=ALU.add, accum_out=ms))
            rsqrt(dve.tensor_scalar(ve, ms, 1.0 / DIM, 1e-5, ALU.mult, ALU.add))
            give(dve.scalar_tensor_tensor(out=xn[:, :], in0=hn[:, :], scalar=rstd, in1=v_("norm_w"), op0=ALU.mult,
                                          op1=ALU.mult))
            step(dve.tensor_tensor(x[:, :], x[:, :], hn[:, :], ALU.add))
            dve.wait_ge(*made("xbc_ps"))
            dve.wait_ge(ev("xp_zero"), 1)
            dve.tensor_copy(XP[:, 0:4, :, TAPS - 1:], bank(2).rearrange("p (t b q) -> p t b q", t=4, b=B))\
                .then_inc(*tick("xbc_sbV"))
            dve.wait_ge(*made("dt_ps"))
            step(dve.tensor_tensor(dta, bank(5)[:, 0:NH], v_("dt_bias"), ALU.add))
            step(dve.tensor_scalar(dneg, dta, -1.0, None, ALU.mult))
            dve.tensor_tensor(dtn, dta, dneg, ALU.min).then_inc(*tick("dtn_ready"))
            step(dve.tensor_scalar(dtm, dta, 0.0, None, ALU.max))
            dve.wait_ge(*made("xbc_sbA"))
            for k in range(TAPS - 1):
                for t in range(CHT):
                    if k == 0:
                        dve.wait_ge(ev("tap3"), t + 1)
                    c1 = C1[:, t, :].rearrange("p (b q) -> p b q", b=B)
                    ins = dve.scalar_tensor_tensor(out=c1, in0=XP[:, t, :, k:k + NQ], scalar=cw[:, t, k:k + 1], in1=c1,
                                                   op0=ALU.mult, op1=ALU.add)
                    if k < TAPS - 2 and t == CHT - 1:
                        step(ins)
            ins.then_inc(*tick("conv_done"))
            dve.wait_ge(*made("dtl"))
            step(dve.tensor_tensor(dt, dtm, dte, ALU.add))
            step(dve.tensor_tensor(dtAn, dt, expA, ALU.mult))
            dve.tensor_scalar(dtA, dtAn, -1.0, None, ALU.mult).then_inc(*tick("dtA_ready"))
            dve.wait_ge(*made("conv_tanh"))
            dve.scalar_tensor_tensor(out=XC.rearrange("p t m -> p (t m)"), in0=TH, scalar=1.0,
                                     in1=C1.rearrange("p t m -> p (t m)"), op0=ALU.add, op1=ALU.mult)\
                .then_inc(*tick("xs_act"))
            dve.wait_ge(*made("z_tanh"))
            step(dve.scalar_tensor_tensor(out=ZS, in0=ZT, scalar=1.0, in1=bank(4), op0=ALU.add, op1=ALU.mult))
            dve.wait_ge(*made("xs_ps"))
            step(dve.tensor_scalar(XS, bank(1), 0.5, None, ALU.mult))
            xs3 = XS.rearrange("p (h d) -> p h d", h=NH)
            step(dve.tensor_tensor(DTX.rearrange("p (h d) -> p h d", h=NH), xs3, bc(dt, 2, HD), ALU.mult))
            step(dve.tensor_tensor(DX.rearrange("p (h d) -> p h d", h=NH), xs3, bc(v_("D_param"), 2, HD), ALU.mult))
            dve.wait_ge(*made("ex_ready"))
            dve.wait_ge(*made("gm_ready"))
            dve.tensor_tensor(MT, EX, bc(GM, 1, NH), ALU.mult).then_inc(*tick("M_ready"))
            dve.wait_ge(*made("ym_ps"))
            step(dve.tensor_tensor(Y2, bank(7), DX, ALU.add))
            step(dve.scalar_tensor_tensor(out=Y2, in0=Y2, scalar=0.5, in1=ZS, op0=ALU.mult, op1=ALU.mult))
            step(dve.tensor_tensor_reduce(out=YG, in0=Y2, in1=Y2, scale=1.0, scalar=0.0, op0=ALU.mult, op1=ALU.add,
                                          accum_out=ms))
            rsqrt(dve.tensor_scalar(ve, ms, 1.0 / DIN, 1e-5, ALU.mult, ALU.add))
            dve.scalar_tensor_tensor(out=YG, in0=Y2, scalar=rstd, in1=v_("gnorm_w"), op0=ALU.mult, op1=ALU.mult)\
                .then_inc(*tick("yg_ready"))
            dve.wait_ge(*made("y_tok_ps"))
            give(dve.tensor_copy(xn[:, :], bank(2)[:, 0:DIM]))
            dve.wait_ge(ev("xn_ready"), given[0])
            step(dve.tensor_tensor(x[:, :], x[:, :], xn[:, :], ALU.add))

            dve.wait_ge(*made("sc_ps"))
            dve.scalar_tensor_tensor(out=SCB[:, 0:SD], in0=bank(1)[:, 0:SD], scalar=0.0, in1=v_("sw2"), op0=ALU.max,
                                     op1=ALU.mult, accum_out=scz).then_inc(*tick("scz"))
            dve.wait_ge(*made("sct"))
            step(dve.tensor_scalar(score, sct, 0.5, 0.5, ALU.mult, ALU.add))
            dve.tensor_scalar(SCB, c_("ones"), score, None, ALU.mult).then_inc(*tick("scb_ready"))
            dve.wait_ge(*made("scT_ps"))
            step(dve.tensor_copy(SCT, bank(7)[:, 0:P]))
            dve.scalar_tensor_tensor(out=CMP, in0=SCT, scalar=score, in1=c_("same"), op0=ALU.is_lt, op1=ALU.mult)
            step(dve.scalar_tensor_tensor(out=CMP2, in0=SCT, scalar=score, in1=c_("tie"), op0=ALU.is_equal,
                                          op1=ALU.mult))
            dve.tensor_tensor(CMP, CMP, CMP2, ALU.add).then_inc(*tick("cmp_ready"))
            step(dve.tensor_tensor_reduce(out=KEEP, in0=SCT, in1=c_("same"), scale=1.0, scalar=0.0, op0=ALU.mult,
                                          op1=ALU.add, accum_out=msum))
            step(dve.tensor_scalar(mtrue, msum, 1.0 / NQ, 0.3, ALU.mult, ALU.is_gt))
            dve.wait_ge(*made("rank_ps"))
            step(dve.scalar_tensor_tensor(out=KEEP, in0=bank(1)[:, 0:P], scalar=float(POOL), in1=c_("same"),
                                          op0=ALU.is_lt, op1=ALU.mult))
            step(dve.scalar_tensor_tensor(out=KEEPS, in0=SCT, scalar=0.5, in1=KEEP, op0=ALU.is_gt, op1=ALU.mult,
                                          accum_out=cnt))
            dve.tensor_scalar(PEN, KEEPS, -1.0, 1e9, ALU.add, ALU.mult)
            dve.wait_ge(*made("lg_ps"))
            step(dve.scalar_tensor_tensor(out=LG, in0=bank(5)[:, 0:P], scalar=RETDIM ** -0.5, in1=KEEPS, op0=ALU.mult,
                                          op1=ALU.mult))
            step(dve.tensor_tensor(LG, LG, PEN, ALU.add))
            dve.tensor_reduce(lmax, LG, AX_X, ALU.max, negate=True).then_inc(*tick("lmax"))
            step(dve.scalar_tensor_tensor(out=rm, in0=cnt, scalar=0.0, in1=mtrue, op0=ALU.is_gt, op1=ALU.mult))
            step(dve.tensor_scalar(rm, rm, 0.5, None, ALU.mult))
            dve.wait_ge(*made("pm_exp"))
            step(dve.reciprocal(zrec, zsum))
            dve.tensor_scalar(PM, PM, zrec, None, ALU.mult).then_inc(*tick("pm_ready"))
            dve.wait_ge(*made("ret_ps"))
            dve.tensor_copy(RET, bank(2)[:, 0:DIM]).then_inc(*tick("ret_sb"))
            dve.wait_ge(*made("ret_sb"))
            dve.wait_ge(*made("gate_tanh"))
            step(dve.scalar_tensor_tensor(out=G1, in0=GTH, scalar=1.0, in1=RET, op0=ALU.add, op1=ALU.mult))
            step(dve.scalar_tensor_tensor(out=x[:, :], in0=G1, scalar=rm, in1=x[:, :], op0=ALU.mult, op1=ALU.add))

            give(norm(x[:, :], hn[:, :], 1e-5))
            dve.wait_ge(*made("route_ps"))
            step(dve.tensor_tensor(rl, bank(1)[:, 0:E], v_("br"), ALU.add))
            step(dve.tensor_reduce(rmax, rl, AX_X, ALU.max))
            step(dve.scalar_tensor_tensor(out=req, in0=rl, scalar=rmax, in1=c_("dec"), op0=ALU.is_equal, op1=ALU.mult))
            step(dve.tensor_reduce(rsel, req, AX_X, ALU.max))
            dve.tensor_scalar(mask, req, rsel, None, ALU.is_equal).then_inc(*tick("mask_ready"))
            dve.wait_ge(*made("mask_ready"))
            dve.tensor_tensor(DM.rearrange("p (e t) -> p e t", e=E), bc(ident, 1, E), bc(mask, 2, TOK), ALU.mult)\
                .then_inc(*tick("dm_ready"))
            dve.tensor_scalar(rneg, rmax, -1.0, None, ALU.mult).then_inc(*tick("rneg"))
            for hf in range(2):
                dve.wait_ge(ev("xm_ps"), 2 * hf + 2)
                dve.tensor_copy(XE[:, 4 * hf:4 * hf + 4, 1, :], bank((7, 3)[hf]).rearrange("p (e t) -> p e t", e=4))\
                    .then_inc(ev("xm_sbV"), 1)
            dve.wait_ge(*made("rz"))
            step(dve.reciprocal(gate, rz))
            use_hidden(1)
            for n in range(E + 1):
                m = E + 1 + n
                dve.wait_ge(ev("y_ps"), m + 1)
                if n == 0:
                    dve.tensor_copy(ACC, bank(0)[:, 0:DIM]).then_inc(ev("y_used"), 1)
                else:
                    dve.scalar_tensor_tensor(out=ACC, in0=bank(n % 4)[:, 0:DIM], scalar=mask[:, n - 1:n], in1=ACC,
                                             op0=ALU.mult, op1=ALU.add).then_inc(ev("y_used"), 1)
                dve.wait_ge(ev("y_used"), m + 1)
            dve.scalar_tensor_tensor(out=xn[:, :], in0=ACC, scalar=gate, in1=x[:, :], op0=ALU.mult, op1=ALU.add)\
                .then_inc(*tick("result"))

        @block.tensor
        def _(pe):
            turned = [0]

            def need(u):
                pe.wait_ge(ev(f"place{PLACE[u]}"), LANDED[u])

            def turn_x(dst, src, let_go=False):
                turned[0] += 1
                pe.wait_ge(ev("xn_ready"), turned[0])
                mm = pe.transpose(dst[:, 0:P], src[:, 0:P], ident)
                if let_go:
                    mm.then_inc(ev("units_used"), 1)
                pe.transpose(dst[:, P:2 * P], src[:, P:2 * P], ident).then_inc(ev("xT_ps"), 1)
                pe.wait_ge(ev("xT_sb"), turned[0])

            pe.wait_ge(ev("const_in"), 16)
            turn_x(bank(4), xn)
            wq = unit("wq").rearrange("p (k n) -> p k n", k=KT)
            need("wq")
            for j in range(PAIRS):
                for k in range(KT):
                    mm = pe.matmul(W[3][:, j * P:(j + 1) * P], wq[:, k, j * P:(j + 1) * P], xT[:, k, :],
                                   start=(k == 0), stop=(k == KT - 1))
            mm.then_inc(ev("qT_ps"), 1)

            def query_keys(b):
                pe.wait_ge(ev("q_sbA"), b + 1)
                pe.wait_ge(ev("q_sbV"), b + 1)
                for j in range(PAIRS):
                    u = "wk0" if j < 4 else "wk1"
                    wk = unit(u).rearrange("p (j c) -> p j c", j=4)
                    if b == 0:
                        if j % 4 == 0:
                            need(u)
                        if j >= 4:
                            pe.wait_ge(ev("ql_sb"), j - 3)
                    else:
                        free67("ql_sb", PAIRS + j)
                    for c in range(CT):
                        mm = pe.matmul(qp_bank(b, j)[:, c, :], wk[:, j % 4, c * P:(c + 1) * P], QB[b][:, j, :],
                                       start=True, stop=True)
                    mm.then_inc(ev("qp_ps"), 1)

            def sim(r):
                b, j = r // PAIRS, r % PAIRS
                if j == 0:
                    pe.wait_ge(ev("ql_sb"), (b + 1) * PAIRS)
                if r >= 2:
                    pe.wait_ge(ev("exp_done"), r - 1)
                for kh in range(2):
                    for c in range(CT):
                        if j == 0 and kh == 0:
                            pe.wait_ge(ev("ctx_lo"), 8 * b + c + 1)
                        for n, (a, z) in enumerate(((0, 0), (0, 1), (1, 0))):
                            mm = pe.matmul(W[r % 2][:, kh * 512:(kh + 1) * 512], QP[a][:, c, j, :],
                                           CXT[z][:, c, kh * 512:(kh + 1) * 512], start=(c == 0 and n == 0),
                                           stop=(c == CT - 1 and n == 2))
                mm.then_inc(ev("sim_done"), 1)

            def turn_probs(r):
                pe.wait_ge(ev("probs_ready"), r + 1)
                for c in range(2):
                    if r == 0:
                        pe.wait_ge(*made("null_sb"))
                    else:
                        pe.wait_ge(ev("pl_sb"), 2 * r - 1 + c)
                    for t in range(4):
                        mm = pe.transpose(bank(4 + c)[:, t * P:(t + 1) * P],
                                          probs0[:, r % 2, (4 * c + t) * P:(4 * c + t + 1) * P], ident)
                    mm.then_inc(ev("pt_ps"), 1)

            def free67(kind, n):
                at = uses67.index((kind, n))
                if at >= 2:
                    before, m = uses67[at - 2]
                    pe.wait_ge(ev(before), m + 1)
                return bank67(kind, n)

            def attend(g):
                pe.wait_ge(ev("pl_sb"), 4 * (g + 1))
                if g % (GROUPS // B) == 0:
                    pe.wait_ge(ev("ctx_lo"), 8 if g == 0 else CHUNKS)
                for c in range(CT):
                    ps = free67("op_sb", CT * g + c)[:, 0:2 * P]
                    for t in range(KEYT):
                        for n, (a, z) in enumerate(((0, 0), (0, 1), (1, 0))):
                            mm = pe.matmul(ps, CXN[a][:, t, c * P:(c + 1) * P], PT[z][:, t, :],
                                           start=(t == 0 and n == 0), stop=(t == KEYT - 1 and n == 2))
                            if 2 * g + 2 == TURN and c == 0 and t == 0 and n < 2:
                                mm.then_inc(ev("units_used"), 1)
                    mm.then_inc(ev("op_ps"), 1)

            def project_heads(g):
                if g == 0:
                    need("wv0")
                    need("wv1")
                    pe.wait_ge(*made("nv_ready"))
                ps = free67("oT_sb", g)
                pe.wait_ge(ev("dw_ready"), g + 1)
                pe.matmul(ps[:, 0:P], NVL.rearrange("p h d -> p (h d)"), DW[g % 2].rearrange("p j q -> p (j q)"),
                          start=True, stop=False, skip_group_check=True)
                pe.wait_ge(ev("op_sb"), CT * (g + 1))
                for jj in range(2):
                    for c in range(CT):
                        wv = unit("wv0" if c < 2 else "wv1").rearrange("p (c n) -> p c n", c=2)
                        for hh in range(2):
                            h = 4 * (g % (GROUPS // B)) + 2 * jj + hh
                            mm = pe.matmul(ps[hh * DH0:(hh + 1) * DH0, jj * NQ:(jj + 1) * NQ],
                                           wv[:, c % 2, h * DH0:(h + 1) * DH0], op[g % 2][:, c, 2 * jj + hh, :],
                                           start=False, stop=(c == CT - 1), skip_group_check=True)
                        if g == GROUPS - 1 and jj == 1 and c == 1:
                            mm.then_inc(ev("units_used"), 1)
                mm.then_inc(ev("oT_ps"), 1)

            query_keys(0)
            pe.wait_ge(ev("cols_in"), 16)
            pe.wait_ge(ev("q_sbA"), B)
            pe.wait_ge(ev("q_sbV"), B)
            for r in range(ROWT):
                mm = pe.matmul(bank(5)[:, r:r + 1], QB[r // PAIRS][:, r % PAIRS, :], p_("nk"), start=True, stop=True)
                if r == 0:
                    mm.then_inc(ev("units_used"), 1)
            mm.then_inc(*tick("null_ps"))
            for r in range(ROWT + 1):
                if r == TURN:
                    project_heads(r // 2 - 2)
                    turn_probs(r - 1)
                    query_keys(1)
                    attend(r // 2 - 1)
                if r < ROWT:
                    sim(r)
                if r == TURN:
                    continue
                if r % 2 == 1 and r >= 3 and r != TURN + 1:
                    attend((r - 3) // 2)
                if r % 2 == 0 and r >= 4:
                    project_heads(r // 2 - 2)
                if r >= 1:
                    turn_probs(r - 1)

            need("wout")
            wo = unit("wout").rearrange("p (j n) -> p j n", j=PAIRS)

            def project_out(pairs):
                for j in pairs:
                    mm = pe.matmul(bank(0)[:, 0:DIM], oT0[:, j, :], wo[:, j, :], start=(j == 0), stop=(j == PAIRS - 1))
                    if j == PAIRS - 2:
                        mm.then_inc(ev("units_used"), 1)
                return mm

            pe.wait_ge(ev("oT_sb"), GROUPS - 1)
            pe.wait_ge(ev("exp_done"), ROWT)
            project_out(range(PAIRS - 2))
            attend(GROUPS - 1)
            project_heads(GROUPS - 1)
            pe.wait_ge(ev("oT_sb"), GROUPS)
            project_out(range(PAIRS - 2, PAIRS)).then_inc(*tick("out0_ps"))

            turn_x(bank(1), xn, let_go=True)
            need("att")
            wa = unit("att")[:, 0:KT * 768].rearrange("p (k n) -> p k n", k=KT)
            wo = unit("att")[:, KT * 768:].rearrange("p (k n) -> p k n", k=KT)
            for lo, hi in ((0, 512), (512, 768)):
                for k in range(KT):
                    mm = pe.matmul(W[1][:, lo:hi], xT[:, k, :], wa[:, k, lo:hi], start=(k == 0), stop=(k == KT - 1))
                mm.then_inc(ev("qkv_ps"), 1)
            pe.wait_ge(*made("qk_ready"))
            for t in range(4):
                mm = pe.transpose(bank(4)[:, t * P:(t + 1) * P], QK[:, t * P:(t + 1) * P], ident)
            mm.then_inc(*tick("qkT_ps"))
            pe.wait_ge(*made("qkT_sb"))
            for h in range(HA):
                o = DH0 * (h % 2)
                mm = pe.matmul(bank(5 + h % 2)[:, (h // 2) * P:(h // 2 + 1) * P], QKT[o:o + DH0, h // 2, :],
                               QKT[o:o + DH0, 2 + h // 2, :], start=True, stop=True)
            mm.then_inc(*tick("simA_ps"))
            pe.wait_ge(*made("probsA"))
            for h in range(HA):
                mm = pe.transpose(bank(7)[:, h * P:(h + 1) * P], PA[:, h, :], ident)
            mm.then_inc(*tick("ptA_ps"))
            pe.wait_ge(*made("ptA_sb"))
            pe.wait_ge(ev("v_sb"), 1)
            for h in range(HA):
                mm = pe.matmul(bank(0)[:, h * DH0:(h + 1) * DH0], PTA[:, h, :], vsb[:, h * DH0:(h + 1) * DH0],
                               start=True, stop=True)
            mm.then_inc(*tick("pvA_ps"))
            turn_x(bank(1), xn)
            for k in range(KT):
                mm = pe.matmul(bank(2)[:, 0:DIM], xT[:, k, :], wo[:, k, :], start=(k == 0), stop=(k == KT - 1))
            mm.then_inc(*tick("outA_ps"))

            turn_x(bank(0), hn, let_go=True)
            pe.wait_ge(ev("gatew_in"), 16)
            for o in range(KT):
                for k in range(KT):
                    mm = pe.matmul(bank(1)[:, o * P:(o + 1) * P], gatew[:, k, o * P:(o + 1) * P], xT[:, k, :],
                                   start=(k == 0), stop=(k == KT - 1))
            mm.then_inc(*tick("gh_ps"))

            def layer1(u, lhs, start):
                w = unit(u).rearrange("p (k n) -> p k n", k=KT)
                need(u)
                for hf in range(2):
                    for k in range(KT):
                        mm = pe.matmul(bank(4 + hf), lhs(k), w[:, k, hf * 512:(hf + 1) * 512],
                                       start=start and k == 0, stop=False)
                mm.then_inc(ev("units_used"), 1)

            layer1("f1b", lambda k: xT[:, k, :], True)
            pe.wait_ge(*made("hm_ready"))
            for k in range(KT):
                mm = pe.matmul(bank(2)[:, 0:B * E], c_("ones"), HM[:, k, :], start=(k == 0), stop=(k == KT - 1))
            mm.then_inc(*tick("g_ps"))
            for e in range(E):
                pe.wait_ge(ev("xe_ready"), e + 1)
                layer1(f"f1e{e}", lambda k: XE[:, e, k, :], False)
                if e == 0:
                    pe.wait_ge(ev("gtok_ready"), 3)
                    pe.transpose(bank(3)[0:E + 1, 0:P], gtok, ident).then_inc(ev("gT_ps"), 1)
            pe.wait_ge(*made("gT_sb"))
            pe.wait_ge(ev("rows_in"), 16)

            def finish_layer1(lhs, n):
                for hf in range(2):
                    pe.matmul(bank(4 + hf), lhs, bias_rows[0:n, 512 * hf:512 * (hf + 1)], start=False, stop=True)\
                        .then_inc(ev("pre_ps"), 1)

            def turn_hidden(n):
                for hf in range(2):
                    pe.wait_ge(ev("u_ready"), 2 * n + hf + 1)
                    for t in range(4):
                        mm = pe.transpose(bank(6 + hf)[:, t * P:(t + 1) * P],
                                          U[:, (4 * hf + t) * P:(4 * hf + t + 1) * P], ident)
                    mm.then_inc(ev("uT_ps"), 1)

            def layer2(u, n):
                w = unit(u).rearrange("p (t n) -> p t n", t=FT)
                need(u)
                if n % (E + 1) >= 4:
                    pe.wait_ge(ev("y_used"), n - 3)
                for t in range(FT):
                    mm = pe.matmul(bank(n % (E + 1) % 4)[:, 0:DIM], UT[:, t, :], w[:, t, :], start=(t == 0),
                                   stop=(t == FT - 1 and u != "f2b"))
                    if t == 0 and u[:3] == "f2e" and u != "f2e0":
                        mm.then_inc(ev("units_used"), 1)
                return mm

            finish_layer1(GT[0:E + 1, :], E + 1)
            turn_hidden(0)
            pe.wait_ge(ev("uT_sb"), 2)
            layer2("f2b", 0).then_inc(ev("units_used"), 1)
            pe.matmul(bank(0)[:, 0:DIM], GT[0:E + 1, :], bias_rows[0:E + 1, F:], start=False, stop=True)\
                .then_inc(ev("y_ps"), 1)
            for e in range(E):
                layer2(f"f2e{e}", e + 1).then_inc(ev("y_ps"), 1)

            turn_x(bank(4), hn, let_go=True)
            need("xat")
            wx = unit("xat")[:, 0:KT * 768].rearrange("p (k n) -> p k n", k=KT)
            wp = unit("xat")[:, KT * 768:].rearrange("p (k n) -> p k n", k=KT)
            for i in range(4):
                for k in range(KT):
                    mm = pe.matmul(bank(5)[:, i * P:(i + 1) * P], wx[:, k, i * P:(i + 1) * P], xT[:, k, :],
                                   start=(k == 0), stop=(k == KT - 1))
            mm.then_inc(*tick("qk1_ps"))
            for k in range(KT):
                mm = pe.matmul(bank(6)[:, 0:DIM], xT[:, k, :], wx[:, k, 512:768], start=(k == 0), stop=(k == KT - 1))
            mm.then_inc(*tick("v1_ps"))
            pe.wait_ge(*made("k1_sb"))
            pe.wait_ge(ev("qz_ready"), 4)
            pe.wait_ge(ev("v_sb"), 2)
            for b in range(B):
                for j in range(PAIRS):
                    i, jj = j // 4, j % 4
                    mm = pe.matmul(bank(4 + 3 * b)[:, j * NQ:(j + 1) * NQ],
                                   QZ[:, i, b, 2 * jj:2 * jj + 2, :].rearrange("p h q -> p (h q)"),
                                   K1[:, i, b * NQ:(b + 1) * NQ], start=True, stop=True)
                mm.then_inc(ev("self_ps"), 1)

            def sim1(r):
                b, j = r % 2, r // 2
                i, jj = j // 4, j % 4
                if r >= 2:
                    pe.wait_ge(ev("exp1_done"), r - 1)
                for kh in range(2):
                    mm = pe.matmul(W[r % 2][:, kh * 512:(kh + 1) * 512],
                                   QZ[:, i, b, 2 * jj:2 * jj + 2, :].rearrange("p h q -> p (h q)"),
                                   ctxT[:, b, i, kh * 512:(kh + 1) * 512], start=True, stop=True)
                mm.then_inc(ev("sim1_done"), 1)

            def turn1(r):
                pe.wait_ge(ev("exp1_done"), r + 1)
                for c in range(3):
                    if r >= 1:
                        pe.wait_ge(ev("pt1_sb" + "AVA"[c]), (2 * r if c != 1 else r))
                    elif c == 0:
                        pe.wait_ge(ev("self_sb"), 2)
                    for t in range(3):
                        mm = pe.transpose(bank((4, 5, 7)[c])[:, t * P:(t + 1) * P],
                                          probs1[:, r % 4, (3 * c + t) * P:(3 * c + t + 1) * P], ident)
                    mm.then_inc(ev("pt1_ps"), 1)

            def attend1(r):
                b, j = r % 2, r // 2
                pe.wait_ge(ev("pt1_sbA"), 2 * (r + 1))
                pe.wait_ge(ev("pt1_sbV"), r + 1)
                for t in range(9):
                    rhs = ctxN[:, b, t, 32 * j:32 * j + 32] if t < 8 else vsb[:, 32 * j:32 * j + 32]
                    mm = pe.matmul(bank(6)[:, (b * PAIRS + j) * 32:(b * PAIRS + j + 1) * 32], PT1[r % 2][:, t, :], rhs,
                                   start=(t == 0), stop=(t == 8))
                mm.then_inc(ev("pv1_ps"), 1)

            pe.wait_ge(ev("ctxT_in"), 16 * B)
            pe.wait_ge(ev("ctxN_in"), 16 * B)
            for r in range(ROWT + 3):
                if r < ROWT:
                    sim1(r)
                if 2 <= r < ROWT + 2:
                    turn1(r - 2)
                if r >= 3:
                    attend1(r - 3)
            pe.wait_ge(*made("o1_ready"))
            for hh in range(2):
                for b in range(B):
                    mm = pe.matmul(bank(0)[b * NQ:(b + 1) * NQ, 0:DIM].rearrange("p (j h d) -> p h j d", j=PAIRS, h=2)[:, hh],
                                   ident[:, hh * NQ:(hh + 1) * NQ], O1[:, b, :, hh, :], start=True, stop=True)
            mm.then_inc(*tick("o1tok_ps"))
            turn_x(bank(4), xn)
            for k in range(KT):
                mm = pe.matmul(bank(1)[:, 0:DIM], xT[:, k, :], wp[:, k, :], start=(k == 0), stop=(k == KT - 1))
            mm.then_inc(*tick("out1_ps"))

            turn_x(bank(0), xn, let_go=True)
            need("mb1")
            wx = unit("mb1")[:, 0:KT * CONV].rearrange("p (k n) -> p k n", k=KT)
            wd = unit("mb1")[:, KT * CONV:KT * (CONV + NH)].rearrange("p (k n) -> p k n", k=KT)
            need("mb2")
            wz = unit("mb2")[:, 0:KT * DIN].rearrange("p (k n) -> p k n", k=KT)
            wo2 = unit("mb2")[:, KT * DIN:].rearrange("p (k n) -> p k n", k=DIN // P)
            need("mb3")
            w3 = unit("mb3")
            for t in range(CHT):
                for k in range(KT):
                    mm = pe.matmul(W[1][:, t * P:(t + 1) * P], wx[:, k, t * P:(t + 1) * P], xT[:, k, :],
                                   start=(k == 0), stop=(k == KT - 1))
            mm.then_inc(*tick("xbc_ps"))
            for k in range(KT):
                mm = pe.matmul(bank(5)[:, 0:NH], xT[:, k, :], wd[:, k, :], start=(k == 0), stop=(k == KT - 1))
            mm.then_inc(*tick("dt_ps"))
            for k in range(KT):
                mm = pe.matmul(bank(4), xT[:, k, :], wz[:, k, :], start=(k == 0), stop=(k == KT - 1))
                if k == 0:
                    mm.then_inc(ev("units_used"), 1)
            mm.then_inc(*tick("z_ps"))
            pe.wait_ge(*made("dtA_ready"))
            for h in range(NH):
                bk = bank(2 + h // 4)
                if h == 0:
                    pe.wait_ge(*made("xbc_sbA"))
                    pe.wait_ge(*made("xbc_sbV"))
                if h % 4 == 0:
                    pe.matmul(bk, ident, bc(c_("neg"), 1, 4), start=True, stop=False, skip_group_check=True)
                ps = bk[:, (h % 4) * P:(h % 4 + 1) * P]
                pe.matmul(ps, dtA[:, h:h + 1].to_broadcast([P, P]), c_("causal"), start=False, stop=False, skip_group_check=True)
                mm = pe.matmul(ps, c_("causal"), dtAn[:, h:h + 1].to_broadcast([P, P]), start=False, stop=(h % 4 == 3), skip_group_check=True)
            mm.then_inc(*tick("decay_ps"))
            pe.wait_ge(*made("xs_act"))
            pe.matmul(bank(6)[:, 0:P], XC[:, 4, :], XC[:, 5, :], start=True, stop=True).then_inc(*tick("G_ps"))
            for t in range(4):
                mm = pe.transpose(bank(1)[:, t * P:(t + 1) * P], XC[:, t, :], ident)
            mm.then_inc(*tick("xs_ps"))
            pe.wait_ge(*made("M_ready"))
            for h in range(NH):
                mm = pe.matmul(bank(7)[:, h * HD:(h + 1) * HD], MT[:, h, :], DTX[:, h * HD:(h + 1) * HD], start=True, stop=True)
            mm.then_inc(*tick("ym_ps"))
            pe.wait_ge(*made("yg_ready"))
            for t in range(4):
                mm = pe.transpose(bank(0)[:, t * P:(t + 1) * P], YG[:, t * P:(t + 1) * P], ident)
            mm.then_inc(*tick("ygT_ps"))
            pe.wait_ge(*made("ygT_sb"))
            for t in range(4):
                mm = pe.matmul(bank(2)[:, 0:DIM], YGT[:, t, :], wo2[:, t, :], start=(t == 0), stop=(t == 3))
            mm.then_inc(*tick("y_tok_ps"))
            turn_x(bank(0), xn, let_go=True)
            sw1 = w3[:, 0:128].rearrange("p (k n) -> p k n", k=KT)
            summ = w3[:, 128:256].rearrange("p (k n) -> p k n", k=KT)
            qw = w3[:, 256:384].rearrange("p (k n) -> p k n", k=KT)
            kw = w3[0:SD, 384:448]
            vw = w3[0:SD, 448:704]
            gw2 = w3[:, 704:1728].rearrange("p (k n) -> p k n", k=4)
            for k in range(KT):
                mm = pe.matmul(bank(1)[:, 0:SD], xT[:, k, :], sw1[:, k, :], start=(k == 0), stop=(k == KT - 1))
            mm.then_inc(*tick("sc_ps"))
            for n, w in enumerate((summ, qw)):
                for k in range(KT):
                    mm = pe.matmul(bank(2)[0:SD, n * P:(n + 1) * P], w[:, k, :], xT[:, k, :],
                                   start=(k == 0), stop=(k == KT - 1))
            mm.then_inc(*tick("pq_ps"))
            for k in range(KT):
                pe.matmul(bank(6)[:, 0:DIM], xT[:, k, :], gw2[:, k, :], start=(k == 0), stop=False)
            pe.wait_ge(*made("pq_sb"))
            pe.matmul(bank(3)[0:SD, 0:P], kw, PQ[0:SD, 0, :], start=True, stop=True).then_inc(*tick("km_ps"))
            pe.matmul(bank(4)[:, 0:DIM], PQ[0:SD, 0, :], vw, start=True, stop=True).then_inc(*tick("vm_ps"))
            pe.wait_ge(*made("km_sb"))
            pe.matmul(bank(5)[:, 0:P], PQ[0:SD, 1, :], KM[0:SD, :], start=True, stop=True).then_inc(*tick("lg_ps"))
            pe.wait_ge(*made("scb_ready"))
            pe.transpose(bank(7)[:, 0:P], SCB, ident).then_inc(*tick("scT_ps"))
            pe.wait_ge(*made("cmp_ready"))
            pe.matmul(bank(1)[:, 0:P], c_("ones"), CMP, start=True, stop=True).then_inc(*tick("rank_ps"))
            pe.wait_ge(*made("pm_ready"))
            pe.transpose(bank(0)[:, 0:P], PM, ident).then_inc(*tick("pmT_ps"))
            pe.wait_ge(*made("pmT_sb"))
            pe.wait_ge(*made("vm_sb"))
            pe.matmul(bank(2)[:, 0:DIM], PMT, VM, start=True, stop=True).then_inc(*tick("ret_ps"))
            pe.wait_ge(*made("ret_sb"))
            for k in range(KT):
                mm = pe.transpose(bank(3)[:, k * P:(k + 1) * P], RET[:, k * P:(k + 1) * P], ident)
            mm.then_inc(*tick("retT_ps"))
            pe.wait_ge(*made("retT_sb"))
            for k in range(KT):
                mm = pe.matmul(bank(6)[:, 0:DIM], RETT[:, k, :], gw2[:, 2 + k, :], start=False, stop=(k == 1))
            mm.then_inc(*tick("gate_ps"))

            turn_x(bank(0), hn, let_go=True)
            wr = p_("wr").rearrange("p (k e) -> p k e", k=KT)
            for k in range(KT):
                mm = pe.matmul(bank(1)[:, 0:E], xT[:, k, :], wr[:, k, :], start=(k == 0), stop=(k == KT - 1))
            mm.then_inc(*tick("route_ps"))
            pe.wait_ge(*made("mask_ready"))
            pe.transpose(bank(0)[0:E, 0:P], mask, ident).then_inc(*tick("maskT_ps"))
            pe.wait_ge(*made("dm_ready"))
            for hf in range(2):
                for k in range(KT):
                    bk = bank(((1, 7), (2, 3))[hf][k])
                    pe.matmul(bk, hn[:, k * P:(k + 1) * P], DM[:, hf * 512:(hf + 1) * 512], start=True, stop=True)\
                        .then_inc(ev("xm_ps"), 1)
            for e in range(E):
                if e % 4 == 0:
                    pe.wait_ge(ev("xm_sbA"), e // 4 + 1)
                    pe.wait_ge(ev("xm_sbV"), e // 4 + 1)
                layer1(f"m1e{e}", lambda k: XE[:, e, k, :], e == 0)
            pe.wait_ge(*made("maskT_sb"))
            pe.wait_ge(ev("rows2_in"), 16)
            finish_layer1(MASKT[0:E, :], E)
            turn_hidden(1)
            pe.wait_ge(ev("uT_sb"), 4)
            pe.matmul(bank(0)[:, 0:DIM], MASKT[0:E, :], bias_rows[0:E, F:], start=True, stop=True)\
                .then_inc(ev("y_ps"), 1)
            for e in range(E):
                layer2(f"m2e{e}", E + 2 + e).then_inc(ev("y_ps"), 1)


def _unit(*parts):
    flat = []
    for a, rows in parts:
        tiles = a.shape[0] // rows
        a = a.reshape(tiles, rows, a.shape[1]).transpose(1, 0, 2).reshape(rows, -1)
        flat.append(a if rows == P else np.concatenate([a, np.zeros((P - rows, a.shape[1]), a.dtype)]))
    a = np.concatenate(flat, axis=1)
    return np.concatenate([a, np.zeros((P, UNIT - a.shape[1]), a.dtype)], axis=1)


def _columns(a):
    return a.reshape(a.shape[0] // P, P, -1).transpose(1, 0, 2).reshape(P, -1)


def _lay_units(i):
    wk, wv = i["L0_xattn_Wkv"][:, :INNER].T, i["L0_xattn_Wkv"][:, INNER:]
    att = np.concatenate([i["L0_attn_Wq"], i["L0_attn_Wk"], i["L0_attn_Wv"]]).T
    inw = i["L1_attn_in_w"].T
    u = {"wq": [(i["L0_xattn_Wq"], P)], "wk0": [(wk[:512], P)], "wk1": [(wk[512:], P)],
         "wv0": [(wv[:256], P)], "wv1": [(wv[256:], P)], "wout": [(i["L0_xattn_Wout"], P)],
         "att": [(att, P), (i["L0_attn_Wo"].T, P)],
         "f1b": [(i["L0_ffn_W1"].T, P)], "f2b": [(i["L0_ffn_W2"].T, P)],
         "xat": [(i["L1_xattn_w_qkv"].T, P), (i["L1_xattn_w_proj"].T, P)],
         "mb1": [(inw[:, DIN:DIN + CONV], P), (inw[:, DIN + CONV:], P)],
         "mb2": [(inw[:, :DIN], P), (i["L1_attn_out_w"].T, P)],
         "mb3": [(i["L1_attn_scorer_w1"].T, P), (i["L1_attn_summ_w"].T, P), (i["L1_attn_q_w"].T, P),
                 (i["L1_attn_k_w"].T, SD), (i["L1_attn_v_w"].T, SD), (i["L1_attn_gate_w"].T, P)]}
    for e in range(E):
        u[f"f1e{e}"] = [(i["L0_ffn_TW1"][e].T, P)]
        u[f"f2e{e}"] = [(i["L0_ffn_TW2"][e].T, P)]
        u[f"m1e{e}"] = [(i["L1_ffn_W1"][e], P)]
        u[f"m2e{e}"] = [(i["L1_ffn_W2"][e], P)]
    return np.stack([_unit(*u[name]) for name in UNITS])


def _lay_constants():
    t = np.arange(P)
    same = (t[:, None] // NQ == t[None, :] // NQ)
    causal = same & (t[:, None] <= t[None, :])
    c = {"ident": np.eye(P), "ones": np.ones((P, P)), "same": same, "causal": causal,
         "tie": same & (t[:, None] < t[None, :]), "neg": np.where(causal, 0.0, -1e30),
         "hmask": np.where(t[:, None] // DH1 == np.arange(8)[None, :], DH1 ** -0.5, 0.0),
         "neghalf": np.full((P, 1), -0.5), "dec": np.tile(np.arange(E, 0, -1), (P, 1)),
         "fold": t[:, None] % NQ == np.arange(NQ)[None, :], "headof": t[:, None] // DH0 == np.arange(2)[None, :]}
    return np.concatenate([np.asarray(c[name], np.float32) for name in CONST], axis=1)


def kernel(**inputs):
    import concourse.bacc as bacc
    from concourse.bass_utils import run_bass_kernel_spmd as run

    i = {name: np.asarray(a) for name, a in inputs.items()}
    nk = i["L0_xattn_null_kv"][0][:, None]
    c = {"gate_b1": _columns(i["L0_ffn_gate_b1"]), "conv_w": _columns(i["L1_attn_conv_w"]),
         "conv_b": _columns(i["L1_attn_conv_b"]), "nk": np.concatenate([nk, nk]),
         "gw2": _columns(i["L0_ffn_gate_w2"].T), "wr": _columns(i["L1_ffn_Wr"])}
    v = {"ln_scale": i["L0_xattn_ln_scale"], "ln_bias": i["L0_xattn_ln_bias"], "ln_g": i["L0_attn_ln_g"],
         "ln_b": i["L0_attn_ln_b"], "bo": i["L0_attn_bo"],
         "qk_gamma": np.concatenate([i["L0_attn_q_gamma"], i["L0_attn_k_gamma"]]), "gate_b2": i["L0_ffn_gate_b2"],
         "nv": i["L0_xattn_null_kv"][1], "b_proj": i["L1_xattn_b_proj"], "norm_w": i["L1_attn_norm_w"],
         "gnorm_w": i["L1_attn_gnorm_w"], "dt_bias": i["L1_attn_dt_bias"], "A_log": i["L1_attn_A_log"],
         "D_param": i["L1_attn_D_param"], "sw2": i["L1_attn_scorer_w2"][0], "br": i["L1_ffn_br"]}
    biases = np.concatenate([
        np.concatenate([i["L0_ffn_Tb1"], i["L0_ffn_b1"][None]]), i["L1_ffn_b1"]])
    biases2 = np.concatenate([np.concatenate([i["L0_ffn_Tb2"], i["L0_ffn_b2"][None]]), i["L1_ffn_b2"]])
    arrays = {
        "x": i["x"].reshape(TOK, DIM),
        "ctx": i["ctx_2048"],
        "ctxT": i["ctx_2048"].transpose(0, 2, 1),
        "units": _lay_units(i),
        "constants": _lay_constants(),
        "columns": np.concatenate([c[name] for name in COLS], axis=1),
        "vectors": np.concatenate([v[name] for name in VECS]),
        "bias_rows_in": np.concatenate([biases, biases2], axis=1),
        "gate_w1": _columns(i["L0_ffn_gate_w1"].T).reshape(P, KT, DIM),
    }
    arrays = {name + "_dram": np.ascontiguousarray(a) for name, a in arrays.items()}
    nc = bacc.Bacc("TRN2", target_bir_lowering=False, num_devices=1)
    args = [nc.dram_tensor(name, a.shape, mybir.dt.from_np(a.dtype), kind="ExternalInput").ap()
            for name, a in arrays.items()]
    result = nc.dram_tensor("result_dram", (TOK, DIM), F32, kind="ExternalOutput").ap()
    perceiver_kernel(nc, *args, result)
    r = run(nc, [arrays], core_ids=[0])
    return r.results[0]["result_dram"].reshape(B, NQ, DIM)
```

```python
from contextlib import ExitStack

import concourse.bass as bass
import numpy as np
from concourse import mybir

ALU = mybir.AluOpType
ACT = mybir.ActivationFunctionType
F32 = mybir.dt.float32
F32R = mybir.dt.float32r
AX_X = mybir.AxisListType.X

P = 128
B, NQ, DIM = 2, 64, 256
TOK = B * NQ
NCTX, CTX = 1024, 512
KT = DIM // P
CT = CTX // P
KEYT = NCTX // P
H0, DH0 = 16, 64
INNER = H0 * DH0
PAIRS = H0 // 2
HA = 4
F, E = 1024, 8
FT = F // P
H1, DH1 = 16, 16
DIN, DST, NH, HD = 512, 128, 8, 64
CONV, TAPS = DIN + 2 * DST, 4
CHT = CONV // P
PAD = NQ + TAPS - 1
POOL, SD, RETDIM = 50, 64, 16
QUARTERS = [(hf, k) for hf in range(2) for k in range(KT)]
XM = [(part, hf, k) for hf in range(2) for part in range(2) for k in range(KT)]
XM_BANK = (1, 7, 2, 3, 6, 0, 1, 7)
XM_AT = [[XM.index((part, hf, k)) for hf, k in QUARTERS] for part in range(2)]
GIVEN_MOE = 7
UNIT = 2048

TERMS = ((0, 0), (0, 1), (1, 0))

UNITS = (["wq", "wk0", "wk1", "wv0", "wv1", "wout", "att", "f1b"] + [f"f1e{e}" for e in range(E)]
         + ["f2b"] + [f"f2e{e}" for e in range(E)] + ["xat", "mb1", "mb2", "mb3"]
         + [f"m1e{e}" for e in range(E)] + [f"m2e{e}" for e in range(E)])
SPLIT = [u for u in UNITS if u[:3] in ("f1e", "f2b", "f2e", "m1e", "m2e")]
RELEASE = {u: n + 1 for n, u in enumerate([u for u in UNITS if u not in SPLIT])}
HALF, SLOTS = UNIT // 2, 4
MOE0 = 2 * SPLIT.index("m1e0")


def half_of(u, n):
    return 2 * SPLIT.index(u) + n


def _made_by(maker_of, p):
    maker = maker_of(p)
    return maker, 1 + sum(1 for q in range(p) if maker_of(q) == maker)


def hi_maker(p):
    return "gpsimd" if p == 0 or MOE0 <= p < MOE0 + SLOTS else "scalar"


def lo_maker(p):
    return "gpsimd" if hi_maker(p) == "gpsimd" or p == 1 or (p % 4 == 3 and p > SLOTS) else "vector"


def slot_free(p):
    if p < SLOTS:
        return "units_used", RELEASE["wout" if p < 2 else "att"]
    return half_used(p - SLOTS)


def hi_done(p):
    maker, n = _made_by(hi_maker, p)
    return "hi_by_" + maker, n


def lo_done(p):
    maker, n = _made_by(lo_maker, p)
    return "lo_by_" + maker, n


def half_used(p):
    u = SPLIT[p // 2]
    if u[1] == "2" and p % 2:
        e = -1 if u == "f2b" else int(u[3:])
        return "y_ps", e + 2 if u[0] == "f" else E + 2 + e + 1
    return "w_used", 1 + sum(1 for q in range(p) if not (SPLIT[q // 2][1] == "2" and q % 2))


NR, NA, NB, NC = 4, 5, 3, 4

CONST = {}
COLS = {}
VECS = {}


def _lay(table, items):
    at = 0
    for name, n in items:
        table[name] = (at, at + n)
        at += n
    return at


NCONST = _lay(CONST, [("ident", P), ("neghalf", 1), ("ones", P), ("same", P), ("causal", P), ("tie", P), ("neg", P),
                      ("hmask", 8), ("dec", E), ("fold", NQ), ("headof", 2), ("sum4", 2 * 32),
                      ("ownhead", 32)])
NCOLS = _lay(COLS, [("gate_b1", KT), ("conv_w", CHT * TAPS), ("conv_b", CHT), ("nk", 1), ("gw2", KT * E),
                    ("wr", KT * E), ("D", DIN // P), ("gnorm_w", DIN // P)])
NVECS = _lay(VECS, [("ln_scale", DIM), ("ln_bias", DIM), ("ln_g", DIM), ("ln_b", DIM), ("bo", DIM),
                    ("qk_gamma", 2 * DH0), ("gate_b2", E), ("nv", DH0), ("b_proj", DIM), ("norm_w", DIM),
                    ("dt_bias", NH), ("A_log", NH), ("sw2", SD), ("br", E)])
BIAS1, BIAS2 = (0, F), (F, F + DIM)
NROWS = F + DIM
N_RSQRT, RSQRT_QK, RSQRT_PAIR = 9, 3, 6
ROWT = B * PAIRS
GROUPS = ROWT // 2
CHUNKS, CHUNK = 16, 1024
TURN = PAIRS
SPLIT_AT = {0: (4, 5), 1: (6,), 2: (7,), TURN - 1: (8, 9), TURN: (12, 13), TURN + 1: (14,), TURN + 2: (15,)}
SPLIT_AT_Q = {(b, 2 * k + 1): n for b, first in ((0, 0), (1, 10)) for k, n in enumerate(range(first, 4 + 8 * b))}


def plan_places():
    last, plan = {}, []

    def put(unit, place, after=None):
        need = []
        before = last.get(place)
        if before in SPLIT:
            need += [lo_done(half_of(before, n)) for n in range(2)]
        count = max(RELEASE.get(before, 0), RELEASE.get(after, 0))
        if count:
            need.append(("units_used", count))
        last[place] = unit
        plan.append((unit, place, need))

    for unit, place in zip(UNITS[:7], (0, 1, 2, 3, 0, 1, 2)):
        put(unit, place)
    cycle = list(range(NR, NR + NA + NB))
    units = UNITS[UNITS.index("f1b"):]
    freed = units.index("xat") + 1 + len(cycle)
    for n, unit in enumerate(units[:freed]):
        place = cycle[n % len(cycle)]
        put(unit, place, after="wout" if n < len(cycle) else None)
    for n in range(NC):
        put(units[freed + n], NR + NA + NB + n, after="xat")
    for n, unit in enumerate(units[freed + NC:]):
        put(unit, cycle[(freed + n) % len(cycle)])
    return plan


PLAN = plan_places()
PLACE = {unit: place for unit, place, _ in PLAN}
LANDED = {unit: 16 * sum(1 for _, q, _ in PLAN[:n + 1] if q == place) for n, (unit, place, _) in enumerate(PLAN)}


def bc(ap, axis, n):
    shape = list(ap.shape)
    shape.insert(axis, n)
    return ap.unsqueeze(axis).to_broadcast(shape)


def cut(base, at, *free):
    n = 1
    for f in free:
        n *= f
    ap = base[:, at:at + n]
    if len(free) == 1:
        return ap
    axes = "abcd"[:len(free)]
    return ap.rearrange(f"p ({' '.join(axes)}) -> p {' '.join(axes)}", **dict(zip(axes, free)))


ONCE = {
    "tensor_made": [
        "null_ps", "out0_ps", "qkT_ps", "simA_ps", "ptA_ps", "outA_ps", "gh_ps", "g_ps",
        "q1_ps", "k1_ps", "v1_ps", "rb_ps", "o1T_ps", "out1_ps", "xbc_ps", "dt_ps", "z_ps", "decay_ps", "G_ps",
        "xs_ps", "ym_ps", "y_tok_ps", "ssq_ps", "sc_ps", "pq_ps", "km_ps", "vm_ps", "lg_ps",
        "scT_ps", "rank_ps", "pmT_ps", "retT_ps", "ret_ps", "gate_ps", "route_ps", "maskT_ps"],
    "scalar_made": [
        "sq_ready", "qkT_sb", "simA_exp", "ptA_sb", "gT_sb", "k1_sb", "rb_sb", "expA", "xbc_sbA", "dte",
        "dtl", "z_tanh", "conv_tanh", "cums", "ex_ready", "gm_ready", "ysq_ready", "pq_sb", "sct", "km_sb",
        "vm_sb", "pm_exp", "pmT_sb", "retT_sb", "gate_tanh", "hn_hi", "rz", "maskT_sb"],
    "vector_made": [
        "null_sb", "nv_ready", "qk_ready", "simA_max", "probsA", "hm_ready", "rsel_ready", "o1_ready", "xbc_sbV",
        "dtn_ready", "dtA_ready", "conv_done", "xs_act", "M_ready", "yg_ready", "ya_ready", "scz", "scb_ready",
        "cmp_ready", "lmax", "pm_ready", "hn_lo", "mask_ready", "rneg"],
}


def perceiver_kernel(nc, x_in, ctx_in, ctxT_in, units_in, const_in, cols_in, vecs_in, rows_in, gate_in, out):
    with ExitStack() as stack:
        def sb(name, *free):
            return stack.enter_context(nc.sbuf_tensor(name, [P, *free], F32))

        names = {}

        def ev(name):
            if name not in names:
                names[name] = stack.enter_context(nc.semaphore(name))
            return names[name]

        ticked = {kind: [] for kind in ONCE}

        def made(name):
            kind = next(k for k, results in ONCE.items() if name in results)
            return ev(kind), ONCE[kind].index(name) + 1

        def tick(name):
            kind = next(k for k, results in ONCE.items() if name in results)
            ticked[kind].append(name)
            assert ticked[kind] == ONCE[kind][:len(ticked[kind])], "ONCE is not in the program's order"
            return ev(kind), 1

        with ExitStack() as pairs:
            def pair(name, *free):
                return [pairs.enter_context(nc.sbuf_tensor(name + half, [P, *free], F32R)) for half in ("_hi", "_lo")]

            CXT = pair("ctx_turned", CT, NCTX)
            CXN = pair("ctx_split", KEYT, CTX)
            QP = pair("q_keys", CT, PAIRS, P)
            PT = pair("probs_turned", KEYT, 2 * P)
        ctxmem = sb("ctxmem", 8 * UNIT)
        ctxT = cut(ctxmem, 0, B, KT, NCTX)
        ctxN = cut(ctxmem, B * KT * NCTX, B, KEYT, DIM)
        arena = sb("arena", NA * UNIT)
        with ExitStack() as pairs:
            acts = pairs.enter_context(nc.sbuf_tensor("acts", [P, 3 * UNIT], F32R))
        scr = sb("scr", 3 * UNIT)
        with ExitStack() as pairs:
            WH, WL23, WL01 = [pairs.enter_context(nc.sbuf_tensor(name, [P, n, HALF], F32R))
                              for name, n in (("w_hi", SLOTS), ("w_lo23", 2), ("w_lo01", 2))]
        fixed = sb("fixed", NR * UNIT)
        pbuf = sb("pbuf", 4 * 1152)
        work = sb("work", PAIRS * TOK)
        const = sb("const", NCONST)
        cols = sb("cols", NCOLS)
        vecs = sb("vecs", NVECS)
        bias_rows = sb("bias_rows", NROWS)
        x = sb("x", DIM)
        hn = sb("hn", DIM)
        xn = sb("xn", DIM)
        xT = sb("xT", KT, TOK)
        vsb = sb("vsb", DIM)
        small = sb("small", 320)

        def c_(name):
            return const[:, CONST[name][0]:CONST[name][1]]

        def p_(name):
            return cols[:, COLS[name][0]:COLS[name][1]]

        def v_(name):
            return vecs[:, VECS[name][0]:VECS[name][1]]

        def unit(name):
            n = PLACE[name]
            if n < NR:
                return fixed[:, n * UNIT:(n + 1) * UNIT]
            if n < NR + NA:
                return arena[:, (n - NR) * UNIT:(n - NR + 1) * UNIT]
            n = (n - NR - NA + NC) % (NB + NC)
            return ctxmem[:, n * UNIT:(n + 1) * UNIT]

        ident = c_("ident")
        cw = p_("conv_w").rearrange("p (t k) -> p t k", t=CHT)
        W = [stack.enter_context(nc.psum_tensor(f"W{n}", [P, 1024], F32)) for n in range(4)]

        def bank(n):
            return W[n // 2][:, 512 * (n % 2):512 * (n % 2) + 512]

        st6, mv = cut(small, 0, 6), cut(small, 6, 2)
        ve, rstd = cut(small, 8, 1), cut(small, 9, 1)
        ve2, rstd2 = cut(small, 300, 2), cut(small, 302, 2)
        mx = cut(small, 10, 2)
        zs = cut(small, 12, 2)
        stat = cut(small, 16, ROWT, 2)
        null_s = cut(small, 48, B * PAIRS)
        negm = cut(small, 64, B * PAIRS)
        rinv0, w_null = cut(small, 80, ROWT), cut(small, 96, ROWT)
        ssq, rqk = cut(small, 112, 8), cut(small, 120, 8)
        smax, ssum, srec = cut(small, 128, 4), cut(small, 132, 4), cut(small, 136, 4)
        hmean = cut(small, 140, KT, B)
        gmix = cut(small, 144, B, E)
        gtok = cut(small, 160, E + 1)
        selfmax = cut(small, 176, B * PAIRS)
        z1 = cut(small, 192, B * PAIRS, 2)
        z1s, rinv1 = cut(small, 224, B * PAIRS), cut(small, 240, B * PAIRS)
        dta, dtm, dtn, dte = (cut(small, 256 + 8 * n, NH) for n in range(4))
        dt, expA, dtA, dtAn = (cut(small, 128 + 8 * n, NH) for n in range(4))
        dneg, cums = cut(small, 160, NH), cut(small, 168, NH)
        scz, sct, score, msum, mtrue, cnt, rm = (cut(small, 288 + n, 1) for n in range(7))
        lmax, zsum, zrec = (cut(small, 297 + n, 1) for n in range(3))
        rl, req, mask = (cut(small, 176 + 8 * n, E) for n in range(3))
        rmax, rsel, rneg, rz, gate = (cut(small, 304 + n, 1) for n in range(5))

        top = scr[:, UNIT:]
        op = [cut(top, 1024 * n, CT, 4, NQ) for n in range(2)]
        oT0 = cut(top, 2048, PAIRS, TOK)
        probs0 = cut(pbuf, 0, 2, NCTX)
        stage = [cut(top, 3072, CHUNK), cut(pbuf, 2048, CHUNK)] \
            + [cut(fixed, PLACE["wv0"] * UNIT + n * CHUNK, CHUNK) for n in range(2)]
        QB = [cut(work, 0, PAIRS, P), cut(pbuf, 3072, PAIRS, P)]
        NVL = cut(vsb, 0, 2, DH0)
        DW = [cut(hn, P * n, 2, NQ) for n in range(2)]
        gatew = cut(pbuf, 4096, KT, DIM)
        QK, QKT, PA = cut(scr, 0, 512), cut(scr, 512, 4, TOK), cut(scr, 1024, HA, TOK)
        SA, PTA, SQ = cut(scr, 1536, HA, NQ), cut(scr, 1792, HA, TOK), cut(scr, 2304, 512)
        XS = [cut(acts, UNIT * n, E, KT, TOK) for n in range(2)]
        UTS = [cut(acts, 2 * UNIT + F * n, FT, TOK) for n in range(2)]
        HNS = [cut(acts, 2 * UNIT + F + DIM * n, DIM) for n in range(2)]
        DM = cut(acts, 2 * UNIT, E * TOK)
        U = cut(work, 0, F)
        HG, HM, GT = cut(pbuf, 0, KT, TOK), cut(pbuf, 256, KT, B * E), cut(pbuf, 304, TOK)
        MASKT = cut(pbuf, 0, TOK)

        def w_slot(part, p):
            n = p % SLOTS
            return WH[:, n, :] if part == 0 else (WL01[:, n, :] if n < 2 else WL23[:, n - 2, :])

        def half_in(p):
            return unit(SPLIT[p // 2])[:, (p % 2) * HALF:(p % 2 + 1) * HALF]

        QZ = cut(scr, 0, 2, B, 8, NQ)
        PT1 = [cut(scr, 2048 + 1152 * n, 9, TOK) for n in range(2)]
        SELF, K1 = cut(scr, 4352, B, PAIRS, NQ), cut(scr, 5888, 2, TOK)
        PV = cut(ctxmem, (NB + NC) * UNIT, ROWT, P)
        RSEL, RB, OT1 = cut(work, 0, ROWT, 32), cut(work, 512, KT, TOK), cut(work, 768, KT, TOK)
        probs1 = cut(pbuf, 0, 4, 1152)
        XP, C1 = cut(scr, 0, CHT, B, PAD), cut(scr, 832, CHT, TOK)
        XC, TH = cut(scr, 1600, CHT, TOK), cut(scr, 2368, CHT * TOK)
        ZS, ZT, ZW = cut(scr, 3136, DIN), cut(scr, 3648, DIN), cut(scr, 4160, DIN)
        DTX, Y2, GM = cut(scr, 4672, DIN), cut(scr, 5184, DIN), cut(scr, 5696, TOK)
        DX = cut(scr, 0, DIN)
        EX, MT = cut(pbuf, 0, NH, TOK), cut(pbuf, 1024, NH, TOK)
        YA, YGT, YSQ = cut(pbuf, 2048, DIN), cut(pbuf, 2560, 4, TOK), cut(scr, 3648, DIN)
        PQ, KM, VM = cut(pbuf, 3072, 2, TOK), cut(pbuf, 3328, TOK), cut(pbuf, 3456, DIM)
        SCB, SCT, CMP, CMP2, KEEP, KEEPS = (cut(pbuf, 3712 + P * n, P) for n in range(6))
        LG, PEN, PM, PMT = (cut(work, P * n, P) for n in range(4))
        RET, RETT = cut(work, 512, DIM), cut(work, 768, KT, TOK)
        GTH, G1 = cut(scr, 832, DIM), cut(scr, 1088, DIM)

        uses67 = []
        for g in range(GROUPS):
            uses67 += [("op_sb", CT * g + c) for c in range(CT)] + [("oT_sb", g)]

        def bank67(kind, n):
            return bank(6 + uses67.index((kind, n)) % 2)

        def qp_bank(j):
            return bank(j % 4).rearrange("p (c m) -> p c m", c=CT)

        def chunk_of(n, part):
            k = n % 4
            return CXT[part][:, k, :] if n % 8 < 4 else CXN[part][:, 2 * k:2 * k + 2, :]

        def stage_no(n):
            return n if n < 4 else n % 2

        def chunk_in(n):
            return ev(f"chunk{stage_no(n)}"), 16 * (1 if n < 4 else n // 2)

        def stage_of(n):
            st = stage[stage_no(n)]
            return st if n % 8 < 4 else st.rearrange("p (t c) -> p t c", t=2)

        def f32(ap):
            return ap.bitcast(F32)

        block = stack.enter_context(nc.Block())

        @block.sync
        def _(sync):
            sync.dma_start(x[:, :], x_in).then_inc(ev("x_in"), 16)
            first = CONST["ones"][0]
            sync.dma_start(const[:, 0:first], const_in[:, 0:first]).then_inc(ev("const_in"), 16)

            def load(n):
                name, place, waits = PLAN[n]
                for sem, count in waits:
                    sync.wait_ge(ev(sem), count)
                sync.dma_start(unit(name), units_in[UNITS.index(name)]).then_inc(ev(f"place{place}"), 16)

            for n in range(3):
                load(n)
            sync.dma_start(const[:, first:], const_in[:, first:]).then_inc(ev("const2_in"), 16)
            sync.wait_ge(ev("ctx_lo"), 4)
            for n in range(3, len(PLAN)):
                load(n)
                if PLAN[n][0] == "f2e0":
                    for b in range(B):
                        sync.dma_start(ctxT[:, b], ctxT_in[b, 0:DIM].rearrange("(c p) k -> p c k", p=P))\
                            .then_inc(ev("ctxT_in"), 16)
                        sync.dma_start(ctxN[:, b], ctx_in[b, :, DIM:].rearrange("(t p) c -> p t c", p=P))\
                            .then_inc(ev("ctxN_in"), 16)
                if PLAN[n][0] == "xat":
                    sync.wait_ge(ev("y_ps"), 1)
                    sync.dma_start(bias_rows[0:E, :], rows_in[E + 1:2 * E + 1, :]).then_inc(ev("rows2_in"), 16)
            sync.wait_ge(ev("y_used"), 2 * (E + 1))
            sync.dma_start(out, x[:, :]).then_inc(ev("stored"), 16)
            sync.wait_ge(ev("stored"), 16)

        @block.gpsimd
        def _(pool):
            def load_chunk(n):
                b, k = n // 8, n % 4
                if n >= 4:
                    pool.wait_ge(ev("ctx_lo"), n - 3 if n < 6 else n - 1)
                src = ctxT_in[b, k * P:(k + 1) * P] if n % 8 < 4 else \
                    ctx_in[b, 2 * k * P:2 * (k + 1) * P].rearrange("(t p) c -> p t c", p=P)
                pool.dma_start(stage_of(n), src).then_inc(chunk_in(n)[0], 16)

            def keep_w(part, p):
                if part == 0:
                    u = SPLIT[p // 2]
                    pool.wait_ge(ev(f"place{PLACE[u]}"), LANDED[u])
                    pool.wait_ge(ev(slot_free(p)[0]), slot_free(p)[1])
                    pool.tensor_copy(w_slot(0, p), half_in(p)).then_inc(ev(hi_done(p)[0]), 1)
                else:
                    pool.wait_ge(ev(hi_done(p)[0]), hi_done(p)[1])
                    pool.tensor_tensor(w_slot(1, p), half_in(p), f32(w_slot(0, p)), ALU.subtract)\
                        .then_inc(ev(lo_done(p)[0]), 1)

            pool.wait_ge(ev("const_in"), 16)
            for n in range(N_RSQRT):
                pool.wait_ge(ev("var_ready"), n + 1)
                src, dst, wide = {RSQRT_QK: (ssq, rqk, 8), RSQRT_PAIR: (ve2, rstd2, 2)}.get(n, (ve, rstd, 1))
                pool.tensor_tensor(dst, src, c_("neghalf").to_broadcast([P, wide]), ALU.pow)\
                    .then_inc(ev("rstd_ready"), 1)
                if n == 0:
                    for k in range(CHUNKS):
                        load_chunk(k)
                        if k == 3:
                            pool.dma_start(cols[:, :], cols_in).then_inc(ev("cols_in"), 16)
                        if k == 7:
                            pool.dma_start(vecs[:, :], vecs_in.partition_broadcast(P)).then_inc(ev("vecs_in"), 16)
                            pool.dma_start(bias_rows[0:E + 1, :], rows_in[0:E + 1, :]).then_inc(ev("rows_in"), 16)
                            pool.dma_start(gatew, gate_in).then_inc(ev("gatew_in"), 16)
                if n == 1:
                    pool.memset(PA, 0.0).then_inc(ev("pa_zero"), 1)
                if n == RSQRT_QK:
                    keep_w(0, 0)
                    keep_w(1, 0)
                    keep_w(1, 1)
                if n == 4:
                    for p in range(SLOTS, MOE0):
                        if lo_maker(p) == "gpsimd":
                            keep_w(1, p)
                if n == 5:
                    for m in range(4):
                        pool.memset(probs1[:, m, NCTX + NQ * (1 - m % 2):NCTX + NQ * (2 - m % 2)], 0.0)\
                            .then_inc(ev("pads_zero"), 1)
                if n == 6:
                    pool.memset(XP[:, :, :, 0:TAPS - 1], 0.0).then_inc(ev("xp_zero"), 1)
                if n in (N_RSQRT - 3, N_RSQRT - 2):
                    for p in range(MOE0, MOE0 + 3) if n == N_RSQRT - 3 else [MOE0 + 3]:
                        keep_w(0, p)
                        keep_w(1, p)
                if n == N_RSQRT - 1:
                    for p in range(MOE0 + SLOTS, 2 * len(SPLIT)):
                        if lo_maker(p) == "gpsimd":
                            keep_w(1, p)

        @block.scalar
        def _(act):
            turned = [0]

            def keep_xT(ps):
                turned[0] += 1
                act.wait_ge(ev("xT_ps"), turned[0])
                act.copy(xT[:, :, :], ps[:, 0:DIM].rearrange("p (k t) -> p k t", k=KT)).then_inc(ev("xT_sb"), 1)

            def keep_w_hi(u, halves=(0, 1)):
                for p in [half_of(u, n) for n in halves]:
                    act.wait_ge(ev(f"place{PLACE[u]}"), LANDED[u])
                    act.wait_ge(ev(slot_free(p)[0]), slot_free(p)[1])
                    act.copy(w_slot(0, p), half_in(p)).then_inc(ev(hi_done(p)[0]), 1)

            def hidden(n, func):
                for hf in range(2):
                    if hf == 0:
                        act.wait_ge(ev("pre_ps"), n + 1)
                    else:
                        last = half_used(half_of(("f1e", "m1e")[n] + str(E - 1), 1))
                        act.wait_ge(ev(last[0]), last[1])
                    act.activation(U[:, hf * 512:(hf + 1) * 512], bank(4 + hf), func).then_inc(ev("u_ready"), 1)
                for hf in range(2):
                    act.wait_ge(ev("uT_ps"), 2 * n + hf + 1)
                    act.copy(UTS[0][:, 4 * hf:4 * hf + 4, :], bank(6 + hf).rearrange("p (t m) -> p t m", t=4))\
                        .then_inc(ev("uh_sb"), 1)

            keep_xT(bank(4))
            act.wait_ge(ev("qT_ps"), 1)
            act.wait_ge(ev("qb_zero"), B)
            for b in range(B):
                act.mul(QB[b][0:DH0, :, 0:NQ],
                        W[3][0:DH0].rearrange("p (j t) -> p j t", j=PAIRS)[:, :, b * NQ:(b + 1) * NQ], DH0 ** -0.5)\
                    .then_inc(ev("q_sbA"), 1)

            def keep_hi(n):
                act.wait_ge(*chunk_in(n))
                if n == 8:
                    act.wait_ge(ev("sim_done"), TURN)
                if n == 12:
                    act.wait_ge(ev("op_ps"), CT * GROUPS // 2)
                act.copy(chunk_of(n, 0), stage_of(n)).then_inc(ev("ctx_hi"), 1)

            def keep_q_hi(b):
                if b:
                    act.wait_ge(ev("sim_done"), TURN)
                for j in range(PAIRS):
                    act.wait_ge(ev("qp_ps"), b * PAIRS + j + 1)
                    act.copy(QP[0][:, :, j, :], qp_bank(j)).then_inc(ev("qh_sb"), 1)
                    if (b, j) in SPLIT_AT_Q:
                        keep_hi(SPLIT_AT_Q[b, j])

            def keep_probs_hi(r):
                for c in range(2):
                    act.wait_ge(ev("pt_ps"), 2 * r + c + 1)
                    act.copy(PT[0][:, 4 * c:4 * c + 4, (r % 2) * P:(r % 2 + 1) * P],
                             bank(4 + c).rearrange("p (t m) -> p t m", t=4)).then_inc(ev("ph_sb"), 1)

            def keep_op(g):
                for c in range(CT):
                    act.wait_ge(ev("op_ps"), CT * g + c + 1)
                    if g >= 2 and c == 0:
                        act.wait_ge(ev("oT_ps"), g - 1)
                    act.copy(op[g % 2][:, c], bank67("op_sb", CT * g + c)[:, 0:2 * P].rearrange("p (h q) -> p h q", h=4))\
                        .then_inc(ev("op_sb"), 1)

            def softmax0(r):
                for n in SPLIT_AT.get(r, ()):
                    keep_hi(n)
                act.wait_ge(ev("negm_ready"), r + 1)
                if r >= 2:
                    act.wait_ge(ev("pt_ps"), 2 * (r - 1))
                act.activation(probs0[:, r % 2, :], W[r % 2][:, :], ACT.Exp, bias=negm[:, r:r + 1],
                               accum_out=stat[:, r, 1:2]).then_inc(ev("exp_done"), 1)
                act.activation(stat[:, r, 0:1], null_s[:, r:r + 1], ACT.Exp, bias=negm[:, r:r + 1])\
                    .then_inc(ev("p0_done"), 1)
                act.wait_ge(ev("rinv_ready"), r + 1)
                act.mul(probs0[:, r % 2, :], probs0[:, r % 2, :], rinv0[:, r:r + 1]).then_inc(ev("probs_ready"), 1)

            keep_q_hi(0)
            act.wait_ge(*made("null_sb"))
            for r in range(ROWT + 1):
                if r == TURN:
                    keep_probs_hi(r - 1)
                    keep_q_hi(1)
                    keep_op(r // 2 - 1)
                if r < ROWT:
                    softmax0(r)
                if r == TURN:
                    continue
                if r % 2 == 1 and r >= 3 and r != TURN + 1:
                    keep_op((r - 3) // 2)
                if r >= 1:
                    keep_probs_hi(r - 1)
            keep_op(GROUPS - 1)

            keep_xT(bank(1))
            act.wait_ge(ev("qkv_ps"), 1)
            act.activation(SQ, bank(2), ACT.Square).then_inc(*tick("sq_ready"))
            act.wait_ge(ev("qkv_ps"), 2)
            act.copy(vsb[:, :], bank(3)[:, 0:DIM]).then_inc(ev("v_sb"), 1)
            act.wait_ge(*made("qkT_ps"))
            act.copy(QKT, bank(4).rearrange("p (t m) -> p t m", t=4)).then_inc(*tick("qkT_sb"))
            keep_w_hi("f1e0", [1])
            act.wait_ge(*made("simA_max"))
            act.activation(SA, SA, ACT.Exp, scale=DH0 ** -0.5).then_inc(*tick("simA_exp"))
            act.wait_ge(*made("ptA_ps"))
            act.copy(PTA, bank(7).rearrange("p (t m) -> p t m", t=4)).then_inc(*tick("ptA_sb"))
            keep_xT(bank(0))

            keep_xT(bank(0))
            keep_w_hi("f1e1", [0])
            act.wait_ge(*made("gh_ps"))
            act.wait_ge(ev("cols_in"), 16)
            for o in range(KT):
                act.activation(HG[:, o, :], bank(1)[:, o * P:(o + 1) * P], ACT.Relu, bias=p_("gate_b1")[:, o:o + 1])\
                    .then_inc(ev("hg_ready"), 1)
            keep_w_hi("f1e1", [1])
            act.wait_ge(ev("gmix_ready"), 1)
            for e in range(E):
                for b in range(B):
                    act.mul(XS[0][:, e, :, b * NQ:(b + 1) * NQ], xT[:, :, b * NQ:(b + 1) * NQ], gmix[:, b, e:e + 1])\
                        .then_inc(ev("xh_ready"), 1)
                if e >= 2:
                    keep_w_hi(f"f1e{e}")
                if e == 2:
                    act.wait_ge(ev("gT_ps"), 1)
                    act.copy(GT[0:E + 1, :], bank(3)[0:E + 1, 0:TOK]).then_inc(*tick("gT_sb"))
            keep_w_hi("f2b")
            hidden(0, ACT.Gelu_apprx_tanh)
            for e in range(E):
                keep_w_hi(f"f2e{e}")

            act.activation(z1[:, 0, 0:1], c_("neghalf"), ACT.Exp)
            keep_xT(bank(4))
            act.wait_ge(*made("k1_ps"))
            act.copy(K1, bank(7)[:, 0:DIM].rearrange("p (i t) -> p i t", i=KT)).then_inc(*tick("k1_sb"))
            act.wait_ge(*made("v1_ps"))
            act.copy(vsb[:, :], bank(6)[:, 0:DIM]).then_inc(ev("v_sb"), 1)
            act.wait_ge(ev("pads_zero"), 4)
            for r in range(ROWT + 2):
                if r >= 2:
                    q = r - 2
                    for n, (t, bk) in enumerate(((0, 4), (6, 7))):
                        act.wait_ge(ev("pt1_ps"), 3 * q + (1, 3)[n])
                        if q >= 2:
                            act.wait_ge(ev("pv1_ps"), q - 1)
                        act.copy(PT1[q % 2][:, t:t + 3, :], bank(bk)[:, 0:3 * P].rearrange("p (t m) -> p t m", t=3))\
                            .then_inc(ev("pt1_sbA"), 1)
                if r < ROWT:
                    b, j = r % 2, r // 2
                    m = b * PAIRS + j
                    act.wait_ge(ev("negm1_ready"), r + 1)
                    if r >= 4:
                        act.wait_ge(ev("pt1_ps"), 3 * (r - 3))
                    act.activation(probs1[:, r % 4, 0:NCTX], W[r % 2][:, :], ACT.Exp, bias=negm[:, m:m + 1],
                                   accum_out=z1[:, m, 0:1])
                    act.activation(probs1[:, r % 4, NCTX + NQ * b:NCTX + NQ * (b + 1)], SELF[:, b, j, :], ACT.Exp,
                                   bias=negm[:, m:m + 1], accum_out=z1[:, m, 1:2]).then_inc(ev("exp1_done"), 1)
            act.wait_ge(*made("rb_ps"))
            act.copy(RB, bank(1)[:, 0:DIM].rearrange("p (i t) -> p i t", i=KT)).then_inc(*tick("rb_sb"))

            act.activation(expA, v_("A_log"), ACT.Exp).then_inc(*tick("expA"))
            keep_xT(bank(0))
            act.wait_ge(*made("xbc_ps"))
            act.copy(XP[:, 4:6, :, TAPS - 1:], bank(3)[:, 0:2 * TOK].rearrange("p (t b q) -> p t b q", t=2, b=B))\
                .then_inc(*tick("xbc_sbA"))
            act.wait_ge(*made("xbc_sbA"))
            act.wait_ge(*made("xbc_sbV"))
            act.wait_ge(*made("dtn_ready"))
            act.activation(dte, dtn, ACT.Exp).then_inc(*tick("dte"))
            for t in range(CHT):
                act.activation(C1[:, t, :].rearrange("p (b q) -> p b q", b=B), XP[:, t, :, TAPS - 1:], ACT.Identity,
                               bias=p_("conv_b")[:, t:t + 1], scale=cw[:, t, TAPS - 1:TAPS]).then_inc(ev("tap3"), 1)
            act.wait_ge(*made("dte"))
            act.activation(dte, dte, ACT.Ln, bias=1.0).then_inc(*tick("dtl"))
            act.wait_ge(*made("z_ps"))
            act.activation(ZT, bank(4), ACT.Tanh, scale=0.5).then_inc(*tick("z_tanh"))
            act.wait_ge(*made("conv_done"))
            act.activation(TH, C1.rearrange("p t m -> p (t m)"), ACT.Tanh, scale=0.5).then_inc(*tick("conv_tanh"))
            act.wait_ge(*made("decay_ps"))
            act.copy(cums, bank(5)[:, 0:NH]).then_inc(*tick("cums"))
            act.wait_ge(*made("cums"))
            for h in range(NH):
                ex = act.activation(EX[:, h, :], W[1][:, h * TOK:(h + 1) * TOK], ACT.Exp, bias=cums[:, h:h + 1])
            ex.then_inc(*tick("ex_ready"))
            act.wait_ge(*made("G_ps"))
            act.mul(GM, bank(6)[:, 0:TOK], 0.25).then_inc(*tick("gm_ready"))
            act.wait_ge(*made("ya_ready"))
            act.activation(YSQ, YA, ACT.Square).then_inc(*tick("ysq_ready"))
            keep_xT(bank(0))

            act.wait_ge(*made("pq_ps"))
            act.copy(PQ[0:SD], bank(2)[0:SD, 0:2 * TOK].rearrange("p (n t) -> p n t", n=2)).then_inc(*tick("pq_sb"))
            act.wait_ge(*made("scz"))
            act.activation(sct, scz, ACT.Tanh, scale=0.5).then_inc(*tick("sct"))
            act.wait_ge(*made("km_ps"))
            act.copy(KM[0:SD, :], bank(3)[0:SD, 0:TOK]).then_inc(*tick("km_sb"))
            act.wait_ge(*made("vm_ps"))
            act.copy(VM, bank(4)[:, 0:DIM]).then_inc(*tick("vm_sb"))
            act.wait_ge(*made("lmax"))
            act.activation(PM, LG, ACT.Exp, bias=lmax, accum_out=zsum).then_inc(*tick("pm_exp"))
            act.wait_ge(*made("pmT_ps"))
            act.copy(PMT, bank(0)[:, 0:P]).then_inc(*tick("pmT_sb"))
            act.wait_ge(*made("retT_ps"))
            act.copy(RETT, bank(3)[:, 0:DIM].rearrange("p (k t) -> p k t", k=KT)).then_inc(*tick("retT_sb"))
            act.wait_ge(*made("gate_ps"))
            act.activation(GTH, bank(6)[:, 0:DIM], ACT.Tanh, scale=0.5).then_inc(*tick("gate_tanh"))

            keep_xT(bank(0))
            act.wait_ge(ev("xn_ready"), GIVEN_MOE)
            act.copy(HNS[0], hn[:, :]).then_inc(*tick("hn_hi"))
            act.wait_ge(*made("rneg"))
            act.activation(rl, rl, ACT.Exp, bias=rneg, accum_out=rz).then_inc(*tick("rz"))
            act.wait_ge(*made("maskT_ps"))
            act.copy(MASKT[0:E, :], bank(0)[0:E, 0:TOK]).then_inc(*tick("maskT_sb"))
            for n, (hf, k) in enumerate(QUARTERS):
                act.wait_ge(ev("xm_ps"), XM_AT[0][n] + 1)
                act.copy(XS[0][:, 4 * hf:4 * hf + 4, k, :], bank(XM_BANK[XM_AT[0][n]]).rearrange("p (e t) -> p e t", e=4))\
                    .then_inc(ev("xh_sb"), 1)
            for e in range(2, E):
                keep_w_hi(f"m1e{e}")
            keep_w_hi("m2e0")
            hidden(1, ACT.Gelu)
            for e in range(1, E):
                keep_w_hi(f"m2e{e}")

        @block.vector
        def _(dve):
            steps, asked, given = [0], [0], [0]

            def step(ins):
                steps[0] += 1
                ins.then_inc(ev("vector_step"), 1)
                dve.wait_ge(ev("vector_step"), steps[0])

            def rsqrt(ins, meanwhile=None):
                asked[0] += 1
                ins.then_inc(ev("var_ready"), 1)
                if meanwhile:
                    step(meanwhile())
                dve.wait_ge(ev("rstd_ready"), asked[0])

            def twice_normed(v, eps):
                return dve.tensor_scalar(v, mv[:, 1:2], 1.0 + eps, eps * eps, ALU.mult, ALU.add)

            def moments(src):
                step(dve.bn_stats(st6, src))
                step(dve.bn_aggr(mv, st6))

            def norm(src, dst, eps):
                moments(src)
                rsqrt(dve.tensor_scalar(ve, mv[:, 1:2], eps, None, ALU.add))
                return dve.tensor_scalar(dst, src, mv[:, 0:1], rstd, ALU.subtract, ALU.mult)

            def give(ins):
                given[0] += 1
                ins.then_inc(ev("xn_ready"), 1)

            def keep_w_lo(u, halves=(0, 1)):
                for p in [half_of(u, n) for n in halves]:
                    if lo_maker(p) == "vector":
                        dve.wait_ge(ev(hi_done(p)[0]), hi_done(p)[1])
                        dve.tensor_tensor(w_slot(1, p), half_in(p), f32(w_slot(0, p)), ALU.subtract)\
                            .then_inc(ev(lo_done(p)[0]), 1)

            def use_hidden(n):
                for hf in range(2):
                    dve.wait_ge(ev("uh_sb"), 2 * n + hf + 1)
                    dve.tensor_tensor(UTS[1][:, 4 * hf:4 * hf + 4, :], bank(6 + hf).rearrange("p (t m) -> p t m", t=4),
                                      f32(UTS[0][:, 4 * hf:4 * hf + 4, :]), ALU.subtract).then_inc(ev("ul_sb"), 1)

            for b in range(B):
                dve.memset(QB[b], 0.0).then_inc(ev("qb_zero"), 1)
            dve.wait_ge(ev("x_in"), 16)
            give(norm(x[:, :], xn[:, :], 1e-5))
            dve.wait_ge(ev("qT_ps"), 1)
            dve.wait_ge(ev("qb_zero"), B)
            for b in range(B):
                dve.tensor_scalar(QB[b][DH0:P, :, NQ:P],
                                  W[3][DH0:P].rearrange("p (j t) -> p j t", j=PAIRS)[:, :, b * NQ:(b + 1) * NQ],
                                  DH0 ** -0.5, None, ALU.mult).then_inc(ev("q_sbV"), 1)

            def keep_lo(n):
                dve.wait_ge(ev("ctx_hi"), n + 1)
                dve.tensor_tensor(chunk_of(n, 1), stage_of(n), f32(chunk_of(n, 0)), ALU.subtract)\
                    .then_inc(ev("ctx_lo"), 1)

            def keep_q_lo(b):
                for j in range(PAIRS):
                    dve.wait_ge(ev("qh_sb"), b * PAIRS + j + 1)
                    dve.tensor_tensor(QP[1][:, :, j, :], qp_bank(j), f32(QP[0][:, :, j, :]), ALU.subtract)\
                        .then_inc(ev("ql_sb"), 1)
                    if (b, j) in SPLIT_AT_Q:
                        keep_lo(SPLIT_AT_Q[b, j])

            def keep_probs_lo(r):
                for c in range(2):
                    dve.wait_ge(ev("ph_sb"), 2 * r + c + 1)
                    at = (slice(None), slice(4 * c, 4 * c + 4), slice((r % 2) * P, (r % 2 + 1) * P))
                    dve.tensor_tensor(PT[1][at], bank(4 + c).rearrange("p (t m) -> p t m", t=4), f32(PT[0][at]),
                                      ALU.subtract).then_inc(ev("pl_sb"), 1)

            def keep_heads(g):
                dve.wait_ge(ev("oT_ps"), g + 1)
                b, j = g // (GROUPS // B), 2 * (g % (GROUPS // B))
                dve.tensor_copy(oT0[:, j:j + 2, b * NQ:(b + 1) * NQ],
                                bank67("oT_sb", g)[:, 0:P].rearrange("p (j q) -> p j q", j=2)).then_inc(ev("oT_sb"), 1)

            def softmax0(r):
                dve.wait_ge(ev("sim_done"), r + 1)
                step(dve.tensor_reduce(mx[:, r % 2:r % 2 + 1], W[r % 2][:, :], AX_X, ALU.max))
                dve.tensor_scalar(negm[:, r:r + 1], mx[:, r % 2:r % 2 + 1], null_s[:, r:r + 1], -1.0, ALU.max, ALU.mult)\
                    .then_inc(ev("negm_ready"), 1)
                for n in SPLIT_AT.get(r, ()):
                    keep_lo(n)
                dve.wait_ge(ev("p0_done"), r + 1)
                z = zs[:, r % 2:r % 2 + 1]
                step(dve.tensor_tensor(z, stat[:, r, 0:1], stat[:, r, 1:2], ALU.add))
                dve.reciprocal(rinv0[:, r:r + 1], z).then_inc(ev("rinv_ready"), 1)

            def null_probs(g):
                dve.wait_ge(ev("rinv_ready"), 2 * g + 2)
                step(dve.tensor_tensor(w_null[:, 2 * g:2 * g + 2], stat[:, 2 * g:2 * g + 2, 0], rinv0[:, 2 * g:2 * g + 2],
                                       ALU.mult))
                if g >= 2:
                    dve.wait_ge(ev("oT_ps"), g - 1)
                dve.tensor_tensor(DW[g % 2], bc(c_("fold"), 1, 2), bc(w_null[:, 2 * g:2 * g + 2], 2, NQ), ALU.mult)\
                    .then_inc(ev("dw_ready"), 1)

            keep_q_lo(0)
            dve.wait_ge(*made("null_ps"))
            dve.tensor_copy(null_s, bank(5)[:, 0:ROWT]).then_inc(*tick("null_sb"))
            dve.wait_ge(*made("null_sb"))
            for r in range(ROWT + 1):
                if r == TURN:
                    keep_heads(r // 2 - 2)
                    keep_probs_lo(r - 1)
                    keep_q_lo(1)
                if r < ROWT:
                    softmax0(r)
                if r == TURN:
                    continue
                if r == 0:
                    dve.wait_ge(ev("const2_in"), 16)
                if r == 2:
                    dve.wait_ge(ev("vecs_in"), 16)
                    dve.tensor_tensor(NVL, bc(v_("nv"), 1, 2), bc(c_("headof"), 2, DH0), ALU.mult).then_inc(*tick("nv_ready"))
                    step(dve.tensor_tensor(x[:, :], x[:, :], v_("ln_bias"), ALU.add))
                if r % 2 == 1:
                    null_probs(r // 2)
                if r % 2 == 0 and r >= 4:
                    keep_heads(r // 2 - 2)
                if r >= 1:
                    keep_probs_lo(r - 1)
            keep_heads(GROUPS - 1)
            dve.wait_ge(*made("out0_ps"))
            moments(bank(0)[:, 0:DIM])
            rsqrt(dve.tensor_scalar(ve, mv[:, 1:2], 1e-6, None, ALU.add),
                  lambda: dve.scalar_tensor_tensor(out=xn[:, :], in0=bank(0)[:, 0:DIM], scalar=mv[:, 0:1], in1=v_("ln_scale"),
                                                   op0=ALU.subtract, op1=ALU.mult))
            step(dve.scalar_tensor_tensor(out=x[:, :], in0=xn[:, :], scalar=rstd, in1=x[:, :], op0=ALU.mult, op1=ALU.add))

            moments(x[:, :])
            rsqrt(twice_normed(ve, 1e-5),
                  lambda: dve.scalar_tensor_tensor(out=xn[:, :], in0=x[:, :], scalar=mv[:, 0:1], in1=v_("ln_g"),
                                                   op0=ALU.subtract, op1=ALU.mult))
            give(dve.scalar_tensor_tensor(out=xn[:, :], in0=xn[:, :], scalar=rstd, in1=v_("ln_b"), op0=ALU.mult, op1=ALU.add))
            step(dve.tensor_tensor(x[:, :], x[:, :], v_("bo"), ALU.add))
            dve.wait_ge(*made("sq_ready"))
            step(dve.tensor_reduce(ssq, SQ.rearrange("p (h d) -> p h d", h=8), AX_X, ALU.add))
            qk4 = QK.rearrange("p (n h d) -> p n h d", n=2, h=HA)
            rsqrt(dve.tensor_scalar(ssq, ssq, 1.0 / DH0, 1e-16, ALU.mult, ALU.max),
                  lambda: dve.tensor_tensor(qk4, bank(2).rearrange("p (n h d) -> p n h d", n=2, h=HA),
                                            bc(v_("qk_gamma").rearrange("p (n d) -> p n d", n=2), 2, HA), ALU.mult))
            qk8 = QK.rearrange("p (h d) -> p h d", h=8)
            dve.tensor_tensor(qk8, qk8, bc(rqk, 2, DH0), ALU.mult).then_inc(*tick("qk_ready"))
            dve.wait_ge(*made("simA_ps"))
            sa4 = SA.rearrange("p (i m) q -> p i m q", m=2)
            for b in range(B):
                for m in range(2):
                    ins = dve.tensor_copy(sa4[b * NQ:(b + 1) * NQ, :, m, :],
                                          bank(5 + m)[b * NQ:(b + 1) * NQ, 0:2 * TOK]
                                          .rearrange("p (i t) -> p i t", i=2)[:, :, b * NQ:(b + 1) * NQ])
            step(ins)
            step(dve.tensor_reduce(smax, SA, AX_X, ALU.max))
            dve.tensor_tensor(SA, SA, bc(smax, 2, NQ), ALU.subtract).then_inc(*tick("simA_max"))
            dve.wait_ge(*made("simA_exp"))
            step(dve.tensor_reduce(ssum, SA, AX_X, ALU.add))
            step(dve.reciprocal(srec, ssum))
            dve.wait_ge(ev("pa_zero"), 1)
            for b in range(B):
                lo, hi = b * NQ, (b + 1) * NQ
                ins = dve.tensor_tensor(PA[lo:hi, :, lo:hi], SA[lo:hi], bc(srec[lo:hi], 2, NQ), ALU.mult)
            ins.then_inc(*tick("probsA"))
            dve.wait_ge(*made("outA_ps"))
            step(dve.tensor_tensor(x[:, :], bank(2)[:, 0:DIM], x[:, :], ALU.add))

            give(norm(x[:, :], hn[:, :], 1e-5))
            keep_w_lo("f1e1", [0])
            dve.wait_ge(ev("hg_ready"), 2)
            step(dve.tensor_reduce(hmean, HG.rearrange("p k (b s) -> p k b s", b=B), AX_X, ALU.add))
            dve.wait_ge(ev("cols_in"), 16)
            dve.tensor_tensor(HM.rearrange("p k (b e) -> p k b e", b=B),
                              bc(p_("gw2").rearrange("p (k e) -> p k e", k=KT), 2, B), bc(hmean, 3, E), ALU.mult)\
                .then_inc(*tick("hm_ready"))
            keep_w_lo("f1e1", [1])
            dve.wait_ge(*made("g_ps"))
            dve.scalar_tensor_tensor(out=gmix, in0=bank(2)[:, 0:B * E].rearrange("p (b e) -> p b e", b=B),
                                     scalar=1.0 / NQ, in1=bc(v_("gate_b2"), 1, B), op0=ALU.mult, op1=ALU.add)\
                .then_inc(ev("gmix_ready"), 1)
            dve.wait_ge(ev("gmix_ready"), 1)
            dve.tensor_copy(gtok[0:NQ, 0:E], gmix[0:NQ, 0, :]).then_inc(ev("gtok_ready"), 1)
            dve.tensor_copy(gtok[NQ:P, 0:E], gmix[NQ:P, 1, :]).then_inc(ev("gtok_ready"), 1)
            dve.tensor_copy(gtok[:, E:E + 1], c_("ones")[:, 0:1]).then_inc(ev("gtok_ready"), 1)
            for e in range(E):
                for b in range(B):
                    dve.wait_ge(ev("xh_ready"), B * e + b + 1)
                    dve.scalar_tensor_tensor(out=XS[1][:, e, :, b * NQ:(b + 1) * NQ], in0=xT[:, :, b * NQ:(b + 1) * NQ],
                                             scalar=gmix[:, b, e:e + 1], in1=f32(XS[0][:, e, :, b * NQ:(b + 1) * NQ]),
                                             op0=ALU.mult, op1=ALU.subtract).then_inc(ev("xl_ready"), 1)
                if e >= 2:
                    keep_w_lo(f"f1e{e}")
            keep_w_lo("f2b")
            use_hidden(0)
            for n in range(E + 1):
                if n < E:
                    keep_w_lo(f"f2e{n}")
                dve.wait_ge(ev("y_ps"), n + 1)
                if n == 0:
                    dve.tensor_tensor(x[:, :], bank(0)[:, 0:DIM], x[:, :], ALU.add).then_inc(ev("y_used"), 1)
                else:
                    dve.scalar_tensor_tensor(out=x[:, :], in0=bank(n % 4)[:, 0:DIM], scalar=gtok[:, n - 1:n],
                                             in1=x[:, :], op0=ALU.mult, op1=ALU.add).then_inc(ev("y_used"), 1)
                dve.wait_ge(ev("y_used"), n + 1)

            give(norm(x[:, :], hn[:, :], 1e-5))
            step(dve.tensor_tensor(x[:, :], x[:, :], v_("b_proj"), ALU.add))
            dve.wait_ge(*made("q1_ps"))
            for i in range(2):
                for b in range(B):
                    dve.tensor_tensor(QZ[:, i, b], bc(bank(5)[:, i * TOK + b * NQ:i * TOK + (b + 1) * NQ], 1, 8),
                                      bc(c_("hmask"), 2, NQ), ALU.mult).then_inc(ev("qz_ready"), 1)
            for r in range(ROWT + 4):
                if r >= 7 and r % 4 == 3:
                    dve.wait_ge(ev("pv1_ps"), r - 3)
                    dve.tensor_copy(PV[:, r - 7:r - 3, :], bank(6).rearrange("p (r m) -> p r m", r=4))\
                        .then_inc(ev("pv1_sb"), 1)
                if r < ROWT:
                    m = (r % 2) * PAIRS + r // 2
                    dve.wait_ge(ev("sim1_done"), r + 1)
                    step(dve.tensor_reduce(mx[:, r % 2:r % 2 + 1], W[r % 2][:, :], AX_X, ALU.max))
                    if r < B:
                        dve.wait_ge(ev("self_ps"), r + 1)
                        dve.tensor_copy(SELF[:, r], bank((4, 7)[r]).rearrange("p (j q) -> p j q", j=PAIRS))\
                            .then_inc(ev("self_sb"), 1)
                        dve.wait_ge(ev("self_sb"), r + 1)
                        step(dve.tensor_reduce(selfmax[:, r * PAIRS:(r + 1) * PAIRS], SELF[:, r], AX_X, ALU.max))
                    dve.tensor_scalar(negm[:, m:m + 1], mx[:, r % 2:r % 2 + 1], selfmax[:, m:m + 1], -1.0, ALU.max, ALU.mult)\
                        .then_inc(ev("negm1_ready"), 1)
                if 2 <= r < ROWT + 2:
                    q = r - 2
                    dve.wait_ge(ev("pt1_ps"), 3 * q + 2)
                    if q >= 2:
                        dve.wait_ge(ev("pv1_ps"), q - 1)
                    dve.tensor_copy(PT1[q % 2][:, 3:6, :], bank(5)[:, 0:3 * P].rearrange("p (t m) -> p t m", t=3))\
                        .then_inc(ev("pt1_sbV"), 1)
                if r == ROWT:
                    dve.wait_ge(ev("exp1_done"), ROWT)
                    step(dve.tensor_tensor(z1s, z1[:, :, 0], z1[:, :, 1], ALU.add))
                    step(dve.reciprocal(rinv1, z1s))
                    dve.tensor_tensor(RSEL, bc(rinv1, 2, 32), bc(c_("ownhead"), 1, ROWT), ALU.mult)\
                        .then_inc(*tick("rsel_ready"))
            dve.wait_ge(*made("rb_sb"))
            dve.wait_ge(*made("o1T_ps"))
            dve.tensor_tensor(OT1, bank(0)[:, 0:DIM].rearrange("p (i t) -> p i t", i=KT), RB, ALU.mult)\
                .then_inc(*tick("o1_ready"))
            dve.wait_ge(*made("out1_ps"))
            step(dve.tensor_tensor(x[:, :], bank(2)[:, 0:DIM], x[:, :], ALU.add))

            moments(x[:, :])
            step(dve.tensor_scalar(ve2[:, 0:1], mv[:, 1:2], 1e-5, None, ALU.add))
            rsqrt(twice_normed(ve2[:, 1:2], 1e-5),
                  lambda: dve.scalar_tensor_tensor(out=xn[:, :], in0=x[:, :], scalar=mv[:, 0:1], in1=v_("norm_w"),
                                                   op0=ALU.subtract, op1=ALU.mult))
            give(dve.tensor_scalar(xn[:, :], xn[:, :], rstd2[:, 1:2], None, ALU.mult))
            step(dve.tensor_scalar(hn[:, :], x[:, :], mv[:, 0:1], rstd2[:, 0:1], ALU.subtract, ALU.mult))
            step(dve.tensor_tensor(x[:, :], x[:, :], hn[:, :], ALU.add))
            dve.wait_ge(*made("xbc_ps"))
            dve.wait_ge(ev("xp_zero"), 1)
            dve.tensor_copy(XP[:, 0:4, :, TAPS - 1:], bank(2).rearrange("p (t b q) -> p t b q", t=4, b=B))\
                .then_inc(*tick("xbc_sbV"))
            dve.wait_ge(*made("dt_ps"))
            step(dve.tensor_tensor(dta, bank(5)[:, 0:NH], v_("dt_bias"), ALU.add))
            step(dve.tensor_scalar(dneg, dta, -1.0, None, ALU.mult))
            dve.tensor_tensor(dtn, dta, dneg, ALU.min).then_inc(*tick("dtn_ready"))
            step(dve.tensor_scalar(dtm, dta, 0.0, None, ALU.max))
            dve.wait_ge(*made("xbc_sbA"))
            for k in range(TAPS - 1):
                for t in range(CHT):
                    if k == 0:
                        dve.wait_ge(ev("tap3"), t + 1)
                    c1 = C1[:, t, :].rearrange("p (b q) -> p b q", b=B)
                    ins = dve.scalar_tensor_tensor(out=c1, in0=XP[:, t, :, k:k + NQ], scalar=cw[:, t, k:k + 1], in1=c1,
                                                   op0=ALU.mult, op1=ALU.add)
                    if k < TAPS - 2 and t == CHT - 1:
                        step(ins)
                if k == TAPS - 3:
                    dve.wait_ge(*made("dtl"))
                    step(dve.tensor_tensor(dt, dtm, dte, ALU.add))
                    step(dve.tensor_tensor(dtAn, dt, expA, ALU.mult))
                    dve.tensor_scalar(dtA, dtAn, -1.0, None, ALU.mult).then_inc(*tick("dtA_ready"))
            ins.then_inc(*tick("conv_done"))
            dve.wait_ge(*made("conv_tanh"))
            dve.scalar_tensor_tensor(out=XC.rearrange("p t m -> p (t m)"), in0=TH, scalar=1.0,
                                     in1=C1.rearrange("p t m -> p (t m)"), op0=ALU.add, op1=ALU.mult)\
                .then_inc(*tick("xs_act"))
            step(dve.scalar_tensor_tensor(out=ZS, in0=ZT, scalar=1.0, in1=bank(4), op0=ALU.add, op1=ALU.mult))
            dve.wait_ge(*made("xs_ps"))
            step(dve.scalar_tensor_tensor(out=DTX.rearrange("p (h d) -> p h d", h=NH),
                                          in0=bank(1).rearrange("p (h d) -> p h d", h=NH), scalar=0.5,
                                          in1=bc(dt, 2, HD), op0=ALU.mult, op1=ALU.mult))
            dve.wait_ge(*made("ex_ready"))
            dve.wait_ge(*made("gm_ready"))
            dve.tensor_tensor(MT, EX, bc(GM, 1, NH), ALU.mult).then_inc(*tick("M_ready"))
            t4 = "p (t m) -> p t m"
            step(dve.scalar_tensor_tensor(out=DX.rearrange(t4, t=4), in0=XC[:, 0:4, :], scalar=0.5, in1=bc(p_("D"), 2, TOK),
                                          op0=ALU.mult, op1=ALU.mult))
            step(dve.scalar_tensor_tensor(out=ZW.rearrange(t4, t=4), in0=ZS.rearrange(t4, t=4), scalar=0.5,
                                          in1=bc(p_("gnorm_w"), 2, TOK), op0=ALU.mult, op1=ALU.mult))
            dve.wait_ge(*made("ym_ps"))
            step(dve.tensor_tensor(Y2, bank(7), DX, ALU.add))
            dve.tensor_tensor(YGT.rearrange("p t m -> p (t m)"), Y2, ZW, ALU.mult).then_inc(*tick("yg_ready"))
            dve.scalar_tensor_tensor(out=YA, in0=Y2, scalar=0.5, in1=ZS, op0=ALU.mult, op1=ALU.mult)\
                .then_inc(*tick("ya_ready"))
            dve.wait_ge(*made("ssq_ps"))
            rsqrt(dve.tensor_scalar(ve, bank(1)[:, 0:1], 1.0 / DIN, 1e-5, ALU.mult, ALU.add))
            dve.wait_ge(*made("y_tok_ps"))
            give(dve.tensor_scalar(xn[:, :], bank(2)[:, 0:DIM], rstd, None, ALU.mult))
            dve.wait_ge(ev("xn_ready"), given[0])
            step(dve.tensor_tensor(x[:, :], x[:, :], xn[:, :], ALU.add))

            dve.wait_ge(*made("sc_ps"))
            dve.scalar_tensor_tensor(out=SCB[:, 0:SD], in0=bank(1)[:, 0:SD], scalar=0.0, in1=v_("sw2"), op0=ALU.max,
                                     op1=ALU.mult, accum_out=scz).then_inc(*tick("scz"))
            dve.wait_ge(*made("sct"))
            step(dve.tensor_scalar(score, sct, 0.5, 0.5, ALU.mult, ALU.add))
            dve.tensor_scalar(SCB, c_("ones"), score, None, ALU.mult).then_inc(*tick("scb_ready"))
            dve.wait_ge(*made("scT_ps"))
            step(dve.tensor_copy(SCT, bank(7)[:, 0:P]))
            dve.scalar_tensor_tensor(out=CMP, in0=SCT, scalar=score, in1=c_("same"), op0=ALU.is_lt, op1=ALU.mult)
            step(dve.scalar_tensor_tensor(out=CMP2, in0=SCT, scalar=score, in1=c_("tie"), op0=ALU.is_equal,
                                          op1=ALU.mult))
            dve.tensor_tensor(CMP, CMP, CMP2, ALU.add).then_inc(*tick("cmp_ready"))
            step(dve.tensor_tensor_reduce(out=KEEP, in0=SCT, in1=c_("same"), scale=1.0, scalar=0.0, op0=ALU.mult,
                                          op1=ALU.add, accum_out=msum))
            step(dve.tensor_scalar(mtrue, msum, 1.0 / NQ, 0.3, ALU.mult, ALU.is_gt))
            dve.wait_ge(*made("rank_ps"))
            step(dve.scalar_tensor_tensor(out=KEEP, in0=bank(1)[:, 0:P], scalar=float(POOL), in1=c_("same"),
                                          op0=ALU.is_lt, op1=ALU.mult))
            step(dve.scalar_tensor_tensor(out=KEEPS, in0=SCT, scalar=0.5, in1=KEEP, op0=ALU.is_gt, op1=ALU.mult,
                                          accum_out=cnt))
            dve.tensor_scalar(PEN, KEEPS, -1.0, 1e9, ALU.add, ALU.mult)
            dve.wait_ge(*made("lg_ps"))
            step(dve.scalar_tensor_tensor(out=LG, in0=bank(5)[:, 0:P], scalar=RETDIM ** -0.5, in1=KEEPS, op0=ALU.mult,
                                          op1=ALU.mult))
            step(dve.tensor_tensor(LG, LG, PEN, ALU.add))
            dve.tensor_reduce(lmax, LG, AX_X, ALU.max, negate=True).then_inc(*tick("lmax"))
            step(dve.scalar_tensor_tensor(out=rm, in0=cnt, scalar=0.0, in1=mtrue, op0=ALU.is_gt, op1=ALU.mult))
            step(dve.tensor_scalar(rm, rm, 0.5, None, ALU.mult))
            dve.wait_ge(*made("pm_exp"))
            step(dve.reciprocal(zrec, zsum))
            dve.tensor_scalar(PM, PM, zrec, None, ALU.mult).then_inc(*tick("pm_ready"))
            dve.wait_ge(*made("ret_ps"))
            step(dve.tensor_copy(RET, bank(2)[:, 0:DIM]))
            dve.wait_ge(*made("gate_tanh"))
            step(dve.scalar_tensor_tensor(out=G1, in0=GTH, scalar=1.0, in1=RET, op0=ALU.add, op1=ALU.mult))
            step(dve.scalar_tensor_tensor(out=x[:, :], in0=G1, scalar=rm, in1=x[:, :], op0=ALU.mult, op1=ALU.add))

            give(norm(x[:, :], hn[:, :], 1e-5))
            assert given[0] == GIVEN_MOE
            dve.wait_ge(*made("hn_hi"))
            dve.tensor_tensor(HNS[1], hn[:, :], f32(HNS[0]), ALU.subtract).then_inc(*tick("hn_lo"))
            dve.wait_ge(*made("route_ps"))
            step(dve.tensor_tensor(rl, bank(1)[:, 0:E], v_("br"), ALU.add))
            step(dve.tensor_reduce(rmax, rl, AX_X, ALU.max))
            step(dve.scalar_tensor_tensor(out=req, in0=rl, scalar=rmax, in1=c_("dec"), op0=ALU.is_equal, op1=ALU.mult))
            step(dve.tensor_reduce(rsel, req, AX_X, ALU.max))
            dve.tensor_scalar(mask, req, rsel, None, ALU.is_equal).then_inc(*tick("mask_ready"))
            dve.wait_ge(*made("mask_ready"))
            for hf in range(2):
                dve.tensor_tensor(DM.rearrange("p (e t) -> p e t", e=E)[:, 4 * hf:4 * hf + 4], bc(ident, 1, 4),
                                  bc(mask[:, 4 * hf:4 * hf + 4], 2, TOK), ALU.mult).then_inc(ev("dm_ready"), 1)
            dve.tensor_scalar(rneg, rmax, -1.0, None, ALU.mult).then_inc(*tick("rneg"))
            for n, (hf, k) in enumerate(QUARTERS):
                dve.wait_ge(ev("xm_ps"), XM_AT[1][n] + 1)
                dve.tensor_copy(XS[1][:, 4 * hf:4 * hf + 4, k, :],
                                bank(XM_BANK[XM_AT[1][n]]).rearrange("p (e t) -> p e t", e=4)).then_inc(ev("xl_sb"), 1)
            dve.wait_ge(*made("rz"))
            step(dve.reciprocal(gate, rz))
            step(dve.tensor_scalar(mask, mask, gate, None, ALU.mult))
            for e in range(2, E):
                keep_w_lo(f"m1e{e}")
            keep_w_lo("m2e0")
            use_hidden(1)
            for n in range(E + 1):
                m = E + 1 + n
                if 1 <= n < E:
                    keep_w_lo(f"m2e{n}")
                dve.wait_ge(ev("y_ps"), m + 1)
                if n == 0:
                    ins = dve.scalar_tensor_tensor(out=x[:, :], in0=bank(0)[:, 0:DIM], scalar=gate, in1=x[:, :],
                                                   op0=ALU.mult, op1=ALU.add)
                else:
                    ins = dve.scalar_tensor_tensor(out=x[:, :], in0=bank(n % 4)[:, 0:DIM], scalar=mask[:, n - 1:n],
                                                   in1=x[:, :], op0=ALU.mult, op1=ALU.add)
                ins.then_inc(ev("y_used"), 1)
                dve.wait_ge(ev("y_used"), m + 1)

        @block.tensor
        def _(pe):
            turned, taken = [0], [0]

            def need(u):
                pe.wait_ge(ev(f"place{PLACE[u]}"), LANDED[u])

            def stay_warm(n, times):
                for _ in range(times):
                    pe.matmul(bank(n)[:, 0:P], ident, ident, start=True, stop=True)

            def kept_turned(mm):
                turned[0] += 1
                mm.then_inc(ev("xT_ps"), 1)
                pe.wait_ge(ev("xT_sb"), turned[0])

            def turn_x(dst, src, let_go=False):
                taken[0] += 1
                pe.wait_ge(ev("xn_ready"), taken[0])
                mm = pe.transpose(dst[:, 0:P], src[:, 0:P], ident)
                if let_go:
                    mm.then_inc(ev("units_used"), 1)
                kept_turned(pe.transpose(dst[:, P:2 * P], src[:, P:2 * P], ident))

            pe.wait_ge(ev("const_in"), 16)
            stay_warm(0, 5)
            turn_x(bank(4), xn)
            stay_warm(0, 9)
            wq = unit("wq").rearrange("p (k n) -> p k n", k=KT)
            need("wq")
            for j in range(PAIRS):
                for k in range(KT):
                    mm = pe.matmul(W[3][:, j * P:(j + 1) * P], wq[:, k, j * P:(j + 1) * P], xT[:, k, :],
                                   start=(k == 0), stop=(k == KT - 1))
            mm.then_inc(ev("qT_ps"), 1)

            def query_keys(b):
                pe.wait_ge(ev("q_sbA"), b + 1)
                pe.wait_ge(ev("q_sbV"), b + 1)
                for j in range(PAIRS):
                    u = "wk0" if j < 4 else "wk1"
                    wk = unit(u).rearrange("p (j c) -> p j c", j=4)
                    if b == 0 and j % 4 == 0:
                        need(u)
                    if j >= 4:
                        pe.wait_ge(ev("ql_sb"), b * PAIRS + j - 3)
                    for c in range(CT):
                        mm = pe.matmul(qp_bank(j)[:, c, :], wk[:, j % 4, c * P:(c + 1) * P], QB[b][:, j, :],
                                       start=True, stop=True)
                    mm.then_inc(ev("qp_ps"), 1)

            def sim(r):
                b, j = r // PAIRS, r % PAIRS
                if j == 0:
                    pe.wait_ge(ev("ql_sb"), (b + 1) * PAIRS)
                if r >= 2:
                    pe.wait_ge(ev("exp_done"), r - 1)
                for kh in range(2):
                    for c in range(CT):
                        if j == 0 and kh == 0:
                            pe.wait_ge(ev("ctx_lo"), 8 * b + c + 1)
                        for n, (a, z) in enumerate(TERMS):
                            mm = pe.matmul(W[r % 2][:, kh * 512:(kh + 1) * 512], QP[a][:, c, j, :],
                                           CXT[z][:, c, kh * 512:(kh + 1) * 512], start=(c == 0 and n == 0),
                                           stop=(c == CT - 1 and n == 2))
                mm.then_inc(ev("sim_done"), 1)

            def turn_probs(r):
                pe.wait_ge(ev("probs_ready"), r + 1)
                for c in range(2):
                    if r == 0:
                        pe.wait_ge(*made("null_sb"))
                    else:
                        pe.wait_ge(ev("pl_sb"), 2 * r - 1 + c)
                    for t in range(4):
                        mm = pe.transpose(bank(4 + c)[:, t * P:(t + 1) * P],
                                          probs0[:, r % 2, (4 * c + t) * P:(4 * c + t + 1) * P], ident)
                    mm.then_inc(ev("pt_ps"), 1)

            def free67(kind, n):
                at = uses67.index((kind, n))
                if at >= 2:
                    before, m = uses67[at - 2]
                    pe.wait_ge(ev(before), m + 1)
                return bank67(kind, n)

            def attend(g):
                pe.wait_ge(ev("pl_sb"), 4 * (g + 1))
                if g % (GROUPS // B) == 0:
                    pe.wait_ge(ev("ctx_lo"), 8 if g == 0 else CHUNKS)
                for c in range(CT):
                    ps = free67("op_sb", CT * g + c)[:, 0:2 * P]
                    for t in range(KEYT):
                        for n, (a, z) in enumerate(TERMS):
                            mm = pe.matmul(ps, CXN[a][:, t, c * P:(c + 1) * P], PT[z][:, t, :],
                                           start=(t == 0 and n == 0), stop=(t == KEYT - 1 and n == 2))
                            if 2 * g + 2 == TURN and c == 0 and t == 0 and n < 2:
                                mm.then_inc(ev("units_used"), 1)
                    mm.then_inc(ev("op_ps"), 1)

            def project_heads(g):
                if g == 0:
                    need("wv0")
                    need("wv1")
                    pe.wait_ge(*made("nv_ready"))
                ps = free67("oT_sb", g)
                pe.wait_ge(ev("dw_ready"), g + 1)
                pe.matmul(ps[:, 0:P], NVL.rearrange("p h d -> p (h d)"), DW[g % 2].rearrange("p j q -> p (j q)"),
                          start=True, stop=False, skip_group_check=True)
                pe.wait_ge(ev("op_sb"), CT * (g + 1))
                for jj in range(2):
                    for c in range(CT):
                        wv = unit("wv0" if c < 2 else "wv1").rearrange("p (c n) -> p c n", c=2)
                        for hh in range(2):
                            h = 4 * (g % (GROUPS // B)) + 2 * jj + hh
                            mm = pe.matmul(ps[hh * DH0:(hh + 1) * DH0, jj * NQ:(jj + 1) * NQ],
                                           wv[:, c % 2, h * DH0:(h + 1) * DH0], op[g % 2][:, c, 2 * jj + hh, :],
                                           start=False, stop=(c == CT - 1), skip_group_check=True)
                        if g == GROUPS - 1 and jj == 1 and c == 1:
                            mm.then_inc(ev("units_used"), 1)
                mm.then_inc(ev("oT_ps"), 1)

            query_keys(0)
            pe.wait_ge(ev("cols_in"), 16)
            pe.wait_ge(ev("q_sbA"), B)
            pe.wait_ge(ev("q_sbV"), B)
            for r in range(ROWT):
                mm = pe.matmul(bank(5)[:, r:r + 1], QB[r // PAIRS][:, r % PAIRS, :], p_("nk"), start=True, stop=True)
                if r == 0:
                    mm.then_inc(ev("units_used"), 1)
            mm.then_inc(*tick("null_ps"))
            for r in range(ROWT + 1):
                if r == TURN:
                    project_heads(r // 2 - 2)
                    turn_probs(r - 1)
                    query_keys(1)
                    attend(r // 2 - 1)
                if r < ROWT:
                    sim(r)
                if r == TURN:
                    continue
                if r % 2 == 1 and r >= 3 and r != TURN + 1:
                    attend((r - 3) // 2)
                if r % 2 == 0 and r >= 4:
                    project_heads(r // 2 - 2)
                if r >= 1:
                    turn_probs(r - 1)

            need("wout")
            wo = unit("wout").rearrange("p (j n) -> p j n", j=PAIRS)

            def project_out(pairs):
                for j in pairs:
                    mm = pe.matmul(bank(0)[:, 0:DIM], oT0[:, j, :], wo[:, j, :], start=(j == 0), stop=(j == PAIRS - 1))
                    if j == PAIRS - 2:
                        mm.then_inc(ev("units_used"), 1)
                return mm

            pe.wait_ge(ev("oT_sb"), GROUPS - 1)
            pe.wait_ge(ev("exp_done"), ROWT)
            project_out(range(PAIRS - 2))
            attend(GROUPS - 1)
            project_heads(GROUPS - 1)
            pe.wait_ge(ev("oT_sb"), GROUPS)
            project_out(range(PAIRS - 2, PAIRS)).then_inc(*tick("out0_ps"))

            stay_warm(3, 17)
            turn_x(bank(1), xn, let_go=True)
            need("att")
            wa = unit("att")[:, 0:KT * 768].rearrange("p (k n) -> p k n", k=KT)
            wo = unit("att")[:, KT * 768:].rearrange("p (k n) -> p k n", k=KT)
            for lo, hi in ((0, 512), (512, 768)):
                for k in range(KT):
                    mm = pe.matmul(W[1][:, lo:hi], xT[:, k, :], wa[:, k, lo:hi], start=(k == 0), stop=(k == KT - 1))
                mm.then_inc(ev("qkv_ps"), 1)
            stay_warm(6, 14)
            pe.wait_ge(*made("qk_ready"))
            for t in range(4):
                mm = pe.transpose(bank(4)[:, t * P:(t + 1) * P], QK[:, t * P:(t + 1) * P], ident)
            mm.then_inc(*tick("qkT_ps"))
            pe.wait_ge(*made("qkT_sb"))
            for h in range(HA):
                o = DH0 * (h % 2)
                mm = pe.matmul(bank(5 + h % 2)[:, (h // 2) * P:(h // 2 + 1) * P], QKT[o:o + DH0, h // 2, :],
                               QKT[o:o + DH0, 2 + h // 2, :], start=True, stop=True)
            mm.then_inc(*tick("simA_ps"))
            stay_warm(4, 17)
            pe.wait_ge(*made("probsA"))
            for h in range(HA):
                mm = pe.transpose(bank(7)[:, h * P:(h + 1) * P], PA[:, h, :], ident)
            mm.then_inc(*tick("ptA_ps"))
            pe.wait_ge(*made("ptA_sb"))
            pe.wait_ge(ev("v_sb"), 1)
            for h in range(HA):
                o = DH0 * (h % 2)
                mm = pe.matmul(bank(0)[o:o + DH0, (h // 2) * P:(h // 2 + 1) * P], vsb[:, h * DH0:(h + 1) * DH0],
                               PTA[:, h, :], start=True, stop=True)
            kept_turned(mm)
            for k in range(KT):
                mm = pe.matmul(bank(2)[:, 0:DIM], xT[:, k, :], wo[:, k, :], start=(k == 0), stop=(k == KT - 1))
            mm.then_inc(*tick("outA_ps"))

            stay_warm(3, 9)
            turn_x(bank(0), hn, let_go=True)
            pe.wait_ge(ev("gatew_in"), 16)
            for o in range(KT):
                for k in range(KT):
                    mm = pe.matmul(bank(1)[:, o * P:(o + 1) * P], gatew[:, k, o * P:(o + 1) * P], xT[:, k, :],
                                   start=(k == 0), stop=(k == KT - 1))
            mm.then_inc(*tick("gh_ps"))

            def split_products(u, products):
                for p in (half_of(u, 0), half_of(u, 1)):
                    pe.wait_ge(ev(lo_done(p)[0]), lo_done(p)[1])
                    mm = products(p)
                    if half_used(p)[0] == "w_used":
                        mm.then_inc(ev("w_used"), 1)
                return mm

            def layer1(u, e, biases=None):
                if e == E - 1:
                    for hf in range(2):
                        pe.matmul(bank(4 + hf), biases, bias_rows[0:biases.shape[0], 512 * hf:512 * (hf + 1)],
                                  start=False, stop=False)

                def products(p):
                    k = p % 2
                    for hf in range(2):
                        for n, (a, z) in enumerate(TERMS):
                            last = k == 1 and n == 2 and e == E - 1
                            mm = pe.matmul(bank(4 + hf), XS[a][:, e, k, :], w_slot(z, p)[:, hf * 512:(hf + 1) * 512],
                                           start=u == "m1e0" and k == 0 and n == 0, stop=last)
                            if last and hf == 0:
                                mm.then_inc(ev("pre_ps"), 1)
                    return mm
                split_products(u, products)

            w = unit("f1b").rearrange("p (k n) -> p k n", k=KT)
            need("f1b")
            for hf in range(2):
                for k in range(KT):
                    mm = pe.matmul(bank(4 + hf), xT[:, k, :], w[:, k, hf * 512:(hf + 1) * 512], start=(k == 0), stop=False)
            mm.then_inc(ev("units_used"), 1)
            pe.wait_ge(*made("hm_ready"))
            for k in range(KT):
                mm = pe.matmul(bank(2)[:, 0:B * E], c_("ones"), HM[:, k, :], start=(k == 0), stop=(k == KT - 1))
            mm.then_inc(*tick("g_ps"))
            for e in range(E):
                pe.wait_ge(ev("xl_ready"), B * (e + 1))
                if e == E - 1:
                    pe.wait_ge(*made("gT_sb"))
                    pe.wait_ge(ev("rows_in"), 16)
                layer1(f"f1e{e}", e, GT[0:E + 1, :])
                if e == 0:
                    pe.wait_ge(ev("gtok_ready"), 3)
                    pe.transpose(bank(3)[0:E + 1, 0:P], gtok, ident).then_inc(ev("gT_ps"), 1)

            def turn_hidden(n):
                for hf in range(2):
                    pe.wait_ge(ev("u_ready"), 2 * n + hf + 1)
                    for t in range(4):
                        mm = pe.transpose(bank(6 + hf)[:, t * P:(t + 1) * P],
                                          U[:, (4 * hf + t) * P:(4 * hf + t + 1) * P], ident)
                    mm.then_inc(ev("uT_ps"), 1)

            def layer2(u, n):
                if n % (E + 1) >= 4:
                    pe.wait_ge(ev("y_used"), n - 3)

                def products(p):
                    if u in ("f2b", "m2e0"):
                        pe.wait_ge(ev("ul_sb"), 2 * (n // (E + 1)) + p % 2 + 1)
                    for t in range(4 * (p % 2), 4 * (p % 2) + 4):
                        for i, (a, z) in enumerate(TERMS):
                            mm = pe.matmul(bank(n % (E + 1) % 4)[:, 0:DIM], UTS[a][:, t, :],
                                           w_slot(z, p)[:, (t % 4) * DIM:(t % 4 + 1) * DIM], start=(t == 0 and i == 0),
                                           stop=(t == FT - 1 and i == 2 and u != "f2b"))
                    return mm
                return split_products(u, products)

            turn_hidden(0)
            layer2("f2b", 0)
            pe.matmul(bank(0)[:, 0:DIM], GT[0:E + 1, :], bias_rows[0:E + 1, F:], start=False, stop=True)\
                .then_inc(ev("y_ps"), 1)
            for e in range(E):
                layer2(f"f2e{e}", e + 1).then_inc(ev("y_ps"), 1)

            stay_warm(5, 11)
            turn_x(bank(4), hn)
            need("xat")
            wx = unit("xat")[:, 0:KT * 768].rearrange("p (k n) -> p k n", k=KT)
            wp = unit("xat")[:, KT * 768:].rearrange("p (k n) -> p k n", k=KT)
            for i in range(4):
                for k in range(KT):
                    mm = pe.matmul(bank(5 + i // 2 * 2)[:, (i % 2) * P:(i % 2 + 1) * P], wx[:, k, i * P:(i + 1) * P],
                                   xT[:, k, :], start=(k == 0), stop=(k == KT - 1))
                if i % 2:
                    mm.then_inc(*tick(("q1_ps", "k1_ps")[i // 2]))
            for k in range(KT):
                mm = pe.matmul(bank(6)[:, 0:DIM], xT[:, k, :], wx[:, k, 512:768], start=(k == 0), stop=(k == KT - 1))
            mm.then_inc(*tick("v1_ps"))

            def sim1(r):
                b, j = r % 2, r // 2
                i, jj = j // 4, j % 4
                if r < 2:
                    pe.wait_ge(ev("qz_ready"), r + 1)
                if r >= 2:
                    pe.wait_ge(ev("exp1_done"), r - 1)
                for kh in range(2):
                    mm = pe.matmul(W[r % 2][:, kh * 512:(kh + 1) * 512],
                                   QZ[:, i, b, 2 * jj:2 * jj + 2, :].rearrange("p h q -> p (h q)"),
                                   ctxT[:, b, i, kh * 512:(kh + 1) * 512], start=True, stop=True)
                mm.then_inc(ev("sim1_done"), 1)

            pe.wait_ge(ev("ctxT_in"), 16 * B)
            pe.wait_ge(ev("ctxN_in"), 16 * B)
            pe.wait_ge(*made("k1_sb"))
            for b in range(B):
                sim1(b)
                if b == 0:
                    pe.wait_ge(ev("v_sb"), 2)
                pe.wait_ge(ev("qz_ready"), 3 + b)
                for j in range(PAIRS):
                    i, jj = j // 4, j % 4
                    mm = pe.matmul(bank((4, 7)[b])[:, j * NQ:(j + 1) * NQ],
                                   QZ[:, i, b, 2 * jj:2 * jj + 2, :].rearrange("p h q -> p (h q)"),
                                   K1[:, i, b * NQ:(b + 1) * NQ], start=True, stop=True)
                mm.then_inc(ev("self_ps"), 1)

            def turn1(r):
                pe.wait_ge(ev("exp1_done"), r + 1)
                for c in range(3):
                    if r >= 1:
                        pe.wait_ge(ev(("pt1_sbA", "pt1_sbV")[c % 2]), (2 * r if c != 1 else r))
                    elif c == 0:
                        pe.wait_ge(ev("self_sb"), 2)
                    for t in range(3):
                        mm = pe.transpose(bank((4, 5, 7)[c])[:, t * P:(t + 1) * P],
                                          probs1[:, r % 4, (3 * c + t) * P:(3 * c + t + 1) * P], ident)
                    mm.then_inc(ev("pt1_ps"), 1)

            def attend1(r):
                b, j = r % 2, r // 2
                pe.wait_ge(ev("pt1_sbA"), 2 * (r + 1))
                pe.wait_ge(ev("pt1_sbV"), r + 1)
                if r >= 4 and r % 4 == 0:
                    pe.wait_ge(ev("pv1_sb"), r // 4)
                for t in range(9):
                    v = ctxN[:, b, t, 32 * j:32 * j + 32] if t < 8 else vsb[:, 32 * j:32 * j + 32]
                    at = 32 * (t % 4)
                    mm = pe.matmul(bank(6)[at:at + 32, (r % 4) * P:(r % 4 + 1) * P], v, PT1[r % 2][:, t, :],
                                   start=(t < 4), stop=(t > 4))
                mm.then_inc(ev("pv1_ps"), 1)

            for r in range(2, ROWT + 3):
                if r < ROWT:
                    sim1(r)
                if 2 <= r < ROWT + 2:
                    turn1(r - 2)
                if r >= 3:
                    attend1(r - 3)
            pe.wait_ge(*made("rsel_ready"))
            blocks = [(i, b) for i in range(KT) for b in range(B)]
            for n, (i, b) in enumerate(blocks):
                for jj in range(4):
                    mm = pe.matmul(bank(1)[32 * jj:32 * jj + 32, n * NQ:(n + 1) * NQ], RSEL[:, b * PAIRS + 4 * i + jj, :],
                                   c_("fold"), start=True, stop=True)
            mm.then_inc(*tick("rb_ps"))
            pe.wait_ge(ev("pv1_sb"), ROWT // 4)
            sum4 = c_("sum4").rearrange("p (h m) -> p h m", h=2)
            for n, (i, b) in enumerate(blocks):
                for hh in range(2):
                    for jj in range(4):
                        mm = pe.matmul(bank(0)[32 * jj:32 * jj + 32, n * NQ:(n + 1) * NQ], sum4[:, hh, :],
                                       PV[:, 2 * (4 * i + jj) + b, hh * NQ:(hh + 1) * NQ],
                                       start=(hh == 0), stop=(hh == 1))
            mm.then_inc(*tick("o1T_ps"))
            pe.wait_ge(*made("o1_ready"))
            for k in range(KT):
                mm = pe.matmul(bank(2)[:, 0:DIM], OT1[:, k, :], wp[:, k, :], start=(k == 0), stop=(k == KT - 1))
            mm.then_inc(*tick("out1_ps"))

            stay_warm(3, 12)
            turn_x(bank(0), xn, let_go=True)
            need("mb1")
            wx = unit("mb1")[:, 0:KT * CONV].rearrange("p (k n) -> p k n", k=KT)
            wd = unit("mb1")[:, KT * CONV:KT * (CONV + NH)].rearrange("p (k n) -> p k n", k=KT)
            need("mb2")
            wz = unit("mb2")[:, 0:KT * DIN].rearrange("p (k n) -> p k n", k=KT)
            wo2 = unit("mb2")[:, KT * DIN:].rearrange("p (k n) -> p k n", k=DIN // P)
            need("mb3")
            w3 = unit("mb3")
            for t in range(CHT):
                for k in range(KT):
                    mm = pe.matmul(W[1][:, t * P:(t + 1) * P], wx[:, k, t * P:(t + 1) * P], xT[:, k, :],
                                   start=(k == 0), stop=(k == KT - 1))
            mm.then_inc(*tick("xbc_ps"))
            for k in range(KT):
                mm = pe.matmul(bank(5)[:, 0:NH], xT[:, k, :], wd[:, k, :], start=(k == 0), stop=(k == KT - 1))
            mm.then_inc(*tick("dt_ps"))
            for t in range(4):
                for k in range(KT):
                    mm = pe.matmul(bank(4)[:, t * P:(t + 1) * P], wz[:, k, t * P:(t + 1) * P], xT[:, k, :],
                                   start=(k == 0), stop=(k == KT - 1))
                if t == 0:
                    mm.then_inc(ev("units_used"), 1)
            mm.then_inc(*tick("z_ps"))
            pe.wait_ge(*made("xbc_sbA"))
            pe.wait_ge(*made("xbc_sbV"))
            for n in range(2):
                pe.matmul(bank(2 + n), ident, bc(c_("neg"), 1, 4), start=True, stop=False, skip_group_check=True)
            stay_warm(6, 12)
            pe.wait_ge(*made("dtA_ready"))
            for h in range(NH):
                pe.matmul(W[1][:, h * TOK:(h + 1) * TOK], dtA[:, h:h + 1].to_broadcast([P, P]), c_("causal"), start=False,
                          stop=(h % 4 == 3), skip_group_check=True)
            pe.matmul(bank(5)[:, 0:NH], c_("causal"), dtAn, start=True, stop=True).then_inc(*tick("decay_ps"))
            stay_warm(6, 6)
            pe.wait_ge(*made("xs_act"))
            pe.matmul(bank(6)[:, 0:P], XC[:, 4, :], XC[:, 5, :], start=True, stop=True).then_inc(*tick("G_ps"))
            for t in range(4):
                mm = pe.transpose(bank(1)[:, t * P:(t + 1) * P], XC[:, t, :], ident)
            mm.then_inc(*tick("xs_ps"))
            stay_warm(0, 9)
            pe.wait_ge(*made("M_ready"))
            for h in range(NH):
                o = HD * (h % 2)
                mm = pe.matmul(bank(7)[o:o + HD, (h // 2) * P:(h // 2 + 1) * P], DTX[:, h * HD:(h + 1) * HD], MT[:, h, :],
                               start=True, stop=True)
            mm.then_inc(*tick("ym_ps"))
            stay_warm(0, 6)
            pe.wait_ge(*made("yg_ready"))
            for t in range(4):
                mm = pe.matmul(bank(2)[:, 0:DIM], YGT[:, t, :], wo2[:, t, :], start=(t == 0), stop=(t == 3))
            mm.then_inc(*tick("y_tok_ps"))
            pe.wait_ge(*made("ysq_ready"))
            for t in range(4):
                mm = pe.matmul(bank(1)[:, 0:1], YSQ[:, t * P:(t + 1) * P], c_("ones")[:, 0:1], start=(t == 0), stop=(t == 3))
            mm.then_inc(*tick("ssq_ps"))
            stay_warm(3, 7)
            turn_x(bank(0), xn, let_go=True)

            sw1 = w3[:, 0:128].rearrange("p (k n) -> p k n", k=KT)
            summ = w3[:, 128:256].rearrange("p (k n) -> p k n", k=KT)
            qw = w3[:, 256:384].rearrange("p (k n) -> p k n", k=KT)
            kw = w3[0:SD, 384:448]
            vw = w3[0:SD, 448:704]
            gw2 = w3[:, 704:1728].rearrange("p (k n) -> p k n", k=4)
            for k in range(KT):
                mm = pe.matmul(bank(1)[:, 0:SD], xT[:, k, :], sw1[:, k, :], start=(k == 0), stop=(k == KT - 1))
            mm.then_inc(*tick("sc_ps"))
            for n, w in enumerate((summ, qw)):
                for k in range(KT):
                    mm = pe.matmul(bank(2)[0:SD, n * P:(n + 1) * P], w[:, k, :], xT[:, k, :],
                                   start=(k == 0), stop=(k == KT - 1))
            mm.then_inc(*tick("pq_ps"))
            for k in range(KT):
                pe.matmul(bank(6)[:, 0:DIM], xT[:, k, :], gw2[:, k, :], start=(k == 0), stop=False)
            pe.wait_ge(*made("pq_sb"))
            pe.matmul(bank(3)[0:SD, 0:P], kw, PQ[0:SD, 0, :], start=True, stop=True).then_inc(*tick("km_ps"))
            pe.matmul(bank(4)[:, 0:DIM], PQ[0:SD, 0, :], vw, start=True, stop=True).then_inc(*tick("vm_ps"))
            pe.wait_ge(*made("km_sb"))
            pe.matmul(bank(5)[:, 0:P], PQ[0:SD, 1, :], KM[0:SD, :], start=True, stop=True).then_inc(*tick("lg_ps"))
            stay_warm(7, 2)
            pe.wait_ge(*made("scb_ready"))
            pe.transpose(bank(7)[:, 0:P], SCB, ident).then_inc(*tick("scT_ps"))
            stay_warm(0, 5)
            pe.wait_ge(*made("cmp_ready"))
            pe.matmul(bank(1)[:, 0:P], c_("ones"), CMP, start=True, stop=True).then_inc(*tick("rank_ps"))
            stay_warm(3, 10)
            pe.wait_ge(*made("pm_ready"))
            pe.transpose(bank(0)[:, 0:P], PM, ident).then_inc(*tick("pmT_ps"))
            pe.wait_ge(*made("pmT_sb"))
            pe.wait_ge(*made("vm_sb"))
            for k in range(KT):
                mm = pe.matmul(bank(3)[:, k * P:(k + 1) * P], VM[:, k * P:(k + 1) * P], PMT, start=True, stop=True)
            mm.then_inc(*tick("retT_ps"))
            pe.matmul(bank(2)[:, 0:DIM], PMT, VM, start=True, stop=True).then_inc(*tick("ret_ps"))
            pe.wait_ge(*made("retT_sb"))
            for k in range(KT):
                mm = pe.matmul(bank(6)[:, 0:DIM], RETT[:, k, :], gw2[:, 2 + k, :], start=False, stop=(k == 1))
            mm.then_inc(*tick("gate_ps"))

            stay_warm(5, 14)
            turn_x(bank(0), hn, let_go=True)
            wr = p_("wr").rearrange("p (k e) -> p k e", k=KT)
            for k in range(KT):
                mm = pe.matmul(bank(1)[:, 0:E], xT[:, k, :], wr[:, k, :], start=(k == 0), stop=(k == KT - 1))
            mm.then_inc(*tick("route_ps"))
            stay_warm(4, 5)
            pe.wait_ge(*made("mask_ready"))
            pe.transpose(bank(0)[0:E, 0:P], mask, ident).then_inc(*tick("maskT_ps"))
            pe.wait_ge(*made("hn_lo"))
            for n, (part, hf, k) in enumerate(XM):
                pe.wait_ge(ev("dm_ready"), hf + 1)
                if XM_BANK[n] == 0:
                    pe.wait_ge(*made("maskT_sb"))
                if n >= 6:
                    pe.wait_ge(ev("xh_sb"), n - 5)
                pe.matmul(bank(XM_BANK[n]), HNS[part][:, k * P:(k + 1) * P], DM[:, hf * 512:(hf + 1) * 512],
                          start=True, stop=True).then_inc(ev("xm_ps"), 1)
            for e in range(E):
                if e % 4 == 0:
                    pe.wait_ge(ev("xh_sb"), 2 * (e // 4 + 1))
                    pe.wait_ge(ev("xl_sb"), 2 * (e // 4 + 1))
                if e == E - 1:
                    pe.wait_ge(ev("rows2_in"), 16)
                layer1(f"m1e{e}", e, MASKT[0:E, :])
            turn_hidden(1)
            pe.matmul(bank(0)[:, 0:DIM], MASKT[0:E, :], bias_rows[0:E, F:], start=True, stop=True)\
                .then_inc(ev("y_ps"), 1)
            for e in range(E):
                layer2(f"m2e{e}", E + 2 + e).then_inc(ev("y_ps"), 1)


def _unit(*parts):
    flat = []
    for a, rows in parts:
        tiles = a.shape[0] // rows
        a = a.reshape(tiles, rows, a.shape[1]).transpose(1, 0, 2).reshape(rows, -1)
        flat.append(a if rows == P else np.concatenate([a, np.zeros((P - rows, a.shape[1]), a.dtype)]))
    a = np.concatenate(flat, axis=1)
    return np.concatenate([a, np.zeros((P, UNIT - a.shape[1]), a.dtype)], axis=1)


def _columns(a):
    return a.reshape(a.shape[0] // P, P, -1).transpose(1, 0, 2).reshape(P, -1)


def _lay_units(i):
    wk, wv = i["L0_xattn_Wkv"][:, :INNER].T, i["L0_xattn_Wkv"][:, INNER:]
    att = np.concatenate([i["L0_attn_Wq"], i["L0_attn_Wk"], i["L0_attn_Wv"]]).T
    inw = i["L1_attn_in_w"].T
    u = {"wq": [(i["L0_xattn_Wq"], P)], "wk0": [(wk[:512], P)], "wk1": [(wk[512:], P)],
         "wv0": [(wv[:256], P)], "wv1": [(wv[256:], P)], "wout": [(i["L0_xattn_Wout"], P)],
         "att": [(att, P), (i["L0_attn_Wo"].T, P)],
         "f1b": [(i["L0_ffn_W1"].T, P)], "f2b": [(i["L0_ffn_W2"].T, P)],
         "xat": [(i["L1_xattn_w_qkv"].T, P), (i["L1_xattn_w_proj"].T, P)],
         "mb1": [(inw[:, DIN:DIN + CONV], P), (inw[:, DIN + CONV:], P)],
         "mb2": [(inw[:, :DIN], P), (i["L1_attn_out_w"].T, P)],
         "mb3": [(i["L1_attn_scorer_w1"].T, P), (i["L1_attn_summ_w"].T, P), (i["L1_attn_q_w"].T, P),
                 (i["L1_attn_k_w"].T, SD), (i["L1_attn_v_w"].T, SD), (i["L1_attn_gate_w"].T, P)]}
    for e in range(E):
        u[f"f1e{e}"] = [(i["L0_ffn_TW1"][e].T, P)]
        u[f"f2e{e}"] = [(i["L0_ffn_TW2"][e].T, P)]
        u[f"m1e{e}"] = [(i["L1_ffn_W1"][e], P)]
        u[f"m2e{e}"] = [(i["L1_ffn_W2"][e], P)]
    return np.stack([_unit(*u[name]) for name in UNITS])


def _lay_constants():
    t = np.arange(P)
    same = (t[:, None] // NQ == t[None, :] // NQ)
    causal = same & (t[:, None] <= t[None, :])
    c = {"ident": np.eye(P), "ones": np.ones((P, P)), "same": same, "causal": causal,
         "tie": same & (t[:, None] < t[None, :]), "neg": np.where(causal, 0.0, -1e30),
         "hmask": np.where(t[:, None] // DH1 == np.arange(8)[None, :], DH1 ** -0.5, 0.0),
         "neghalf": np.full((P, 1), -0.5), "dec": np.tile(np.arange(E, 0, -1), (P, 1)),
         "fold": t[:, None] % NQ == np.arange(NQ)[None, :], "headof": t[:, None] // DH0 == np.arange(2)[None, :],
         "sum4": np.concatenate([(t[:, None] % 32 == np.arange(32)) & (np.arange(32) // DH1 == hh) for hh in range(2)], 1),
         "ownhead": t[:, None] // NQ == np.arange(32)[None, :] // DH1}
    return np.concatenate([np.asarray(c[name], np.float32) for name in CONST], axis=1)


def kernel(**inputs):
    import concourse.bacc as bacc
    from concourse.bass_utils import run_bass_kernel_spmd as run

    i = {name: np.asarray(a) for name, a in inputs.items()}
    nk = i["L0_xattn_null_kv"][0][:, None]
    c = {"gate_b1": _columns(i["L0_ffn_gate_b1"]), "conv_w": _columns(i["L1_attn_conv_w"]),
         "conv_b": _columns(i["L1_attn_conv_b"]), "nk": np.concatenate([nk, nk]),
         "gw2": _columns(i["L0_ffn_gate_w2"].T), "wr": _columns(i["L1_ffn_Wr"]),
         "D": _columns(np.repeat(i["L1_attn_D_param"], HD)), "gnorm_w": _columns(i["L1_attn_gnorm_w"])}
    v = {"ln_scale": i["L0_xattn_ln_scale"], "ln_bias": i["L0_xattn_ln_bias"], "ln_g": i["L0_attn_ln_g"],
         "ln_b": i["L0_attn_ln_b"], "bo": i["L0_attn_bo"],
         "qk_gamma": np.concatenate([i["L0_attn_q_gamma"], i["L0_attn_k_gamma"]]), "gate_b2": i["L0_ffn_gate_b2"],
         "nv": i["L0_xattn_null_kv"][1], "b_proj": i["L1_xattn_b_proj"], "norm_w": i["L1_attn_norm_w"],
         "dt_bias": i["L1_attn_dt_bias"], "A_log": i["L1_attn_A_log"],
         "sw2": i["L1_attn_scorer_w2"][0], "br": i["L1_ffn_br"]}
    biases = np.concatenate([
        np.concatenate([i["L0_ffn_Tb1"], i["L0_ffn_b1"][None]]), i["L1_ffn_b1"]])
    biases2 = np.concatenate([np.concatenate([i["L0_ffn_Tb2"], i["L0_ffn_b2"][None]]), i["L1_ffn_b2"]])
    arrays = {
        "x": i["x"].reshape(TOK, DIM),
        "ctx": i["ctx_2048"],
        "ctxT": i["ctx_2048"].transpose(0, 2, 1),
        "units": _lay_units(i),
        "constants": _lay_constants(),
        "columns": np.concatenate([c[name] for name in COLS], axis=1),
        "vectors": np.concatenate([v[name] for name in VECS]),
        "bias_rows_in": np.concatenate([biases, biases2], axis=1),
        "gate_w1": _columns(i["L0_ffn_gate_w1"].T).reshape(P, KT, DIM),
    }
    arrays = {name + "_dram": np.ascontiguousarray(a) for name, a in arrays.items()}
    nc = bacc.Bacc("TRN2", target_bir_lowering=False, num_devices=1)
    args = [nc.dram_tensor(name, a.shape, mybir.dt.from_np(a.dtype), kind="ExternalInput").ap()
            for name, a in arrays.items()]
    result = nc.dram_tensor("result_dram", (TOK, DIM), F32, kind="ExternalOutput").ap()
    perceiver_kernel(nc, *args, result)
    r = run(nc, [arrays], core_ids=[0])
    return r.results[0]["result_dram"].reshape(B, NQ, DIM)
```
